# Optimizing a Trainium2 kernel written in Bass

```python
import numpy as np
import jax
import jax.numpy as jnp

def _softmax(x, axis=-1):
    return jax.nn.softmax(x, axis=axis)

def _gelu(x):
    return jax.nn.gelu(x, approximate=True)

def _silu(x):
    return jax.nn.silu(x)

def _sigmoid(x):
    return jax.nn.sigmoid(x)

def _layernorm(x, axis=-1, eps=1e-05):
    m = jnp.mean(x, axis=axis, keepdims=True)
    v = jnp.var(x, axis=axis, keepdims=True)
    return (x - m) / jnp.sqrt(v + eps)

def _scatter_add(tgt, idx, src, axis=0):
    return tgt.at[idx].add(src)

def _segment_sum(src, seg, n):
    return jax.ops.segment_sum(src, seg, n)
kernel_name = 'mk_adaln_d1_jaxref_r4_f2e7a4'

def setup_inputs(seed: int=0):
    np.random.seed(seed)
    _w = jnp.asarray

    def _L0_attn_setup():
        import jax, jax.numpy as jnp
        import numpy as np
        B, T, C = (2, 512, 256)
        H = 16
        D = C // H
        HID = C // 4
        FF = 4 * C

        def _rms_norm(x):
            eps = jnp.finfo(x.dtype).eps
            return x * jax.lax.rsqrt(jnp.mean(jnp.square(x), axis=-1, keepdims=True) + eps)
        key = jax.random.key(seed)
        ks = jax.random.split(key, 11)
        s = lambda fan_in: 1.0 / np.sqrt(fan_in)
        inp = {'x': jax.random.normal(ks[0], (B, T, C), jnp.float32), 'Wq': jax.random.uniform(ks[1], (C, C), jnp.float32, -s(C), s(C)), 'Wk': jax.random.uniform(ks[2], (C, C), jnp.float32, -s(C), s(C)), 'Wv': jax.random.uniform(ks[3], (C, C), jnp.float32, -s(C), s(C)), 'Wm1': jax.random.uniform(ks[4], (HID, C), jnp.float32, -s(C), s(C)), 'bm1': jax.random.uniform(ks[5], (HID,), jnp.float32, -s(C), s(C)), 'Wm2': jax.random.uniform(ks[6], (H, HID), jnp.float32, -s(HID), s(HID)), 'bm2': jax.random.uniform(ks[7], (H,), jnp.float32, -s(HID), s(HID)), 'Wproj': jax.random.uniform(ks[8], (C, C), jnp.float32, -s(C), s(C)), 'Wfc': jax.random.uniform(ks[9], (FF, C), jnp.float32, -s(C), s(C)), 'Wcp': jax.random.uniform(ks[10], (C, FF), jnp.float32, -s(FF), s(FF))}
        return inp
    _L0_attn_in = _L0_attn_setup()

    def _L0_ffn_setup():
        import jax, jax.numpy as jnp
        import numpy as np
        D_MODEL = 256
        HIDDEN = 512
        MOE_DIM = 64
        N_EXPERTS = 8
        TOP_K = 2
        EXP_HIDDEN = HIDDEN // 2
        B, S = (4, 512)
        key = jax.random.key(seed)
        ks = jax.random.split(key, 20)

        def w(k, shape, fan_in):
            return (jax.random.normal(k, shape, dtype=jnp.float32) / np.sqrt(fan_in)).astype(jnp.float32)
        return {'inputs_embeds': jax.random.normal(ks[0], (B, S, D_MODEL), dtype=jnp.float32), 'enc_w': w(ks[1], (D_MODEL, HIDDEN), D_MODEL), 'enc_b': jnp.zeros((HIDDEN,), jnp.float32), 's2c_w': w(ks[2], (HIDDEN, MOE_DIM), HIDDEN), 's2c_b': jnp.zeros((MOE_DIM,), jnp.float32), 'r_w1': w(ks[3], (MOE_DIM, 64), MOE_DIM), 'r_b1': jnp.zeros((64,), jnp.float32), 'r_w2': w(ks[4], (64, N_EXPERTS), 64), 'r_b2': jnp.zeros((N_EXPERTS,), jnp.float32), 'e_w1': w(ks[5], (N_EXPERTS, MOE_DIM, EXP_HIDDEN), MOE_DIM), 'e_b1': jnp.zeros((N_EXPERTS, EXP_HIDDEN), jnp.float32), 'e_w2': w(ks[6], (N_EXPERTS, EXP_HIDDEN, MOE_DIM), EXP_HIDDEN), 'e_b2': jnp.zeros((N_EXPERTS, MOE_DIM), jnp.float32), 'c2s_w': w(ks[7], (MOE_DIM, HIDDEN), MOE_DIM), 'c2s_b': jnp.zeros((HIDDEN,), jnp.float32), 'dec_w': w(ks[8], (HIDDEN, D_MODEL), HIDDEN), 'dec_b': jnp.zeros((D_MODEL,), jnp.float32), 'ln_g': jnp.ones((D_MODEL,), jnp.float32), 'ln_b': jnp.zeros((D_MODEL,), jnp.float32)}
    _L0_ffn_in = _L0_ffn_setup()
    _L0_c = _w((lambda *s: np.random.randn(*s).astype(np.float32) * 0.05)(2, 256))
    _L0_wmod = _w((lambda *s: np.random.randn(*s).astype(np.float32) * 0.05)(256, 6 * 256) * 256 ** (-0.5))
    _d = {'L0_attn_x': _L0_attn_in['x'], 'L0_attn_Wq': _L0_attn_in['Wq'], 'L0_attn_Wk': _L0_attn_in['Wk'], 'L0_attn_Wv': _L0_attn_in['Wv'], 'L0_attn_Wm1': _L0_attn_in['Wm1'], 'L0_attn_bm1': _L0_attn_in['bm1'], 'L0_attn_Wm2': _L0_attn_in['Wm2'], 'L0_attn_bm2': _L0_attn_in['bm2'], 'L0_attn_Wproj': _L0_attn_in['Wproj'], 'L0_attn_Wfc': _L0_attn_in['Wfc'], 'L0_attn_Wcp': _L0_attn_in['Wcp'], 'L0_ffn_enc_w': _L0_ffn_in['enc_w'], 'L0_ffn_enc_b': _L0_ffn_in['enc_b'], 'L0_ffn_s2c_w': _L0_ffn_in['s2c_w'], 'L0_ffn_s2c_b': _L0_ffn_in['s2c_b'], 'L0_ffn_r_w1': _L0_ffn_in['r_w1'], 'L0_ffn_r_b1': _L0_ffn_in['r_b1'], 'L0_ffn_r_w2': _L0_ffn_in['r_w2'], 'L0_ffn_r_b2': _L0_ffn_in['r_b2'], 'L0_ffn_e_w1': _L0_ffn_in['e_w1'], 'L0_ffn_e_b1': _L0_ffn_in['e_b1'], 'L0_ffn_e_w2': _L0_ffn_in['e_w2'], 'L0_ffn_e_b2': _L0_ffn_in['e_b2'], 'L0_ffn_c2s_w': _L0_ffn_in['c2s_w'], 'L0_ffn_c2s_b': _L0_ffn_in['c2s_b'], 'L0_ffn_dec_w': _L0_ffn_in['dec_w'], 'L0_ffn_dec_b': _L0_ffn_in['dec_b'], 'L0_ffn_ln_g': _L0_ffn_in['ln_g'], 'L0_ffn_ln_b': _L0_ffn_in['ln_b'], 'L0_c': _L0_c, 'L0_wmod': _L0_wmod}
    _x0 = _d['L0_attn_x']
    _d['L0_attn_x'] = jax.random.normal(jax.random.fold_in(jax.random.key(seed), 1), (2, 2048, 256), dtype=_x0.dtype)
    del _x0
    return _d

def reference(L0_attn_x, L0_attn_Wq, L0_attn_Wk, L0_attn_Wv, L0_attn_Wm1, L0_attn_bm1, L0_attn_Wm2, L0_attn_bm2, L0_attn_Wproj, L0_attn_Wfc, L0_attn_Wcp, L0_ffn_enc_w, L0_ffn_enc_b, L0_ffn_s2c_w, L0_ffn_s2c_b, L0_ffn_r_w1, L0_ffn_r_b1, L0_ffn_r_w2, L0_ffn_r_b2, L0_ffn_e_w1, L0_ffn_e_b1, L0_ffn_e_w2, L0_ffn_e_b2, L0_ffn_c2s_w, L0_ffn_c2s_b, L0_ffn_dec_w, L0_ffn_dec_b, L0_ffn_ln_g, L0_ffn_ln_b, L0_c, L0_wmod):

    def _L0_attn_ref(x, Wq, Wk, Wv, Wm1, bm1, Wm2, bm2, Wproj, Wfc, Wcp):
        import jax, jax.numpy as jnp
        import numpy as np
        B, T, C = (2, 512, 256)
        H = 16
        D = C // H
        HID = C // 4
        FF = 4 * C

        def _rms_norm(x):
            eps = jnp.finfo(x.dtype).eps
            return x * jax.lax.rsqrt(jnp.mean(jnp.square(x), axis=-1, keepdims=True) + eps)
        b, t, c = x.shape
        h = Wm2.shape[0]
        d = c // h
        q = (x @ Wq.T).reshape(b, t, h, d)
        k = (x @ Wk.T).reshape(b, t, h, d)
        v = (x @ Wv.T).reshape(b, t, h, d)
        surprise = jax.nn.sigmoid(jnp.maximum(x @ Wm1.T + bm1, 0.0) @ Wm2.T + bm2)
        decay = 1.0 - surprise
        qT = jnp.transpose(q, (1, 0, 2, 3))
        kT = jnp.transpose(k, (1, 0, 2, 3))
        vT = jnp.transpose(v, (1, 0, 2, 3))
        dT = jnp.transpose(decay, (1, 0, 2))
        gT = jnp.transpose(surprise, (1, 0, 2))

        def step(state, inp):
            qt, kt, vt, dt, gt = inp
            state = state * dt[..., None, None] + gt[..., None, None] * (kt[..., :, None] * vt[..., None, :])
            yt = jnp.einsum('bhd,bhde->bhe', qt, state)
            return (state, yt)
        state0 = jnp.zeros((b, h, d, d), x.dtype)
        _, ys = jax.lax.scan(step, state0, (qT, kT, vT, dT, gT))
        y = jnp.transpose(ys, (1, 0, 2, 3)).reshape(b, t, c)
        y = y @ Wproj.T
        yn = _rms_norm(y)
        mlp = jnp.square(jnp.maximum(yn @ Wfc.T, 0.0)) @ Wcp.T
        return y + mlp

    def _L0_ffn_ref(inputs_embeds, enc_w, enc_b, s2c_w, s2c_b, r_w1, r_b1, r_w2, r_b2, e_w1, e_b1, e_w2, e_b2, c2s_w, c2s_b, dec_w, dec_b, ln_g, ln_b):
        import jax, jax.numpy as jnp
        import numpy as np
        D_MODEL = 256
        HIDDEN = 512
        MOE_DIM = 64
        N_EXPERTS = 8
        TOP_K = 2
        EXP_HIDDEN = HIDDEN // 2
        B, S = (4, 512)
        b, s, _ = inputs_embeds.shape
        spikes = jax.nn.sigmoid(inputs_embeds @ enc_w + enc_b)
        cont = spikes.reshape(b * s, -1) @ s2c_w + s2c_b
        rh = jax.nn.relu(cont @ r_w1 + r_b1)
        probs = jax.nn.softmax(rh @ r_w2 + r_b2, axis=-1)
        topw, topi = jax.lax.top_k(probs, TOP_K)
        topw = topw / jnp.sum(topw, axis=-1, keepdims=True)
        comb = jnp.sum(jax.nn.one_hot(topi, N_EXPERTS, dtype=cont.dtype) * topw[..., None], axis=1)
        eh = jax.nn.relu(jnp.einsum('nd,edh->neh', cont, e_w1) + e_b1)
        eo = jnp.einsum('neh,ehd->ned', eh, e_w2) + e_b2
        moe_out = jnp.einsum('ned,ne->nd', eo, comb)
        rates = jax.nn.sigmoid(moe_out @ c2s_w + c2s_b)
        x = rates.reshape(b, s, -1)
        dec = jax.nn.sigmoid(x @ dec_w + dec_b)
        mu = jnp.mean(dec, axis=-1, keepdims=True)
        var = jnp.var(dec, axis=-1, keepdims=True)
        return (dec - mu) * jax.lax.rsqrt(var + 1e-05) * ln_g + ln_b
    x = L0_attn_x
    mod = (_silu(L0_c) @ L0_wmod).reshape(L0_c.shape[0], 6, 1, -1)
    sa, ca, ga, sb, cb, gb = (mod[:, 0], mod[:, 1], mod[:, 2], mod[:, 3], mod[:, 4], mod[:, 5])
    ga = (2 * (ga >= 0) - 1) * jnp.maximum(jnp.abs(ga), 0.25)
    gb = (2 * (gb >= 0) - 1) * jnp.maximum(jnp.abs(gb), 0.25)
    h = _layernorm(x, axis=-1) * (1 + ca) + sa
    x = x + ga * _L0_attn_ref(h, L0_attn_Wq, L0_attn_Wk, L0_attn_Wv, L0_attn_Wm1, L0_attn_bm1, L0_attn_Wm2, L0_attn_bm2, L0_attn_Wproj, L0_attn_Wfc, L0_attn_Wcp)
    h = _layernorm(x, axis=-1) * (1 + cb) + sb
    x = x + gb * _L0_ffn_ref(h, L0_ffn_enc_w, L0_ffn_enc_b, L0_ffn_s2c_w, L0_ffn_s2c_b, L0_ffn_r_w1, L0_ffn_r_b1, L0_ffn_r_w2, L0_ffn_r_b2, L0_ffn_e_w1, L0_ffn_e_b1, L0_ffn_e_w2, L0_ffn_e_b2, L0_ffn_c2s_w, L0_ffn_c2s_b, L0_ffn_dec_w, L0_ffn_dec_b, L0_ffn_ln_g, L0_ffn_ln_b)
    return x

_drawn_inputs = setup_inputs


def setup_inputs(seed=0):
    import zlib

    import numpy as np

    out = dict(_drawn_inputs(seed))
    spreads = {'L0_ffn_enc_b': (0.0, 2.0),
     'L0_ffn_s2c_b': (0.0, 0.8),
     'L0_ffn_r_b1': (0.0, 0.8),
     'L0_ffn_r_b2': (0.0, 0.477),
     'L0_ffn_e_b1': (0.0, 0.8),
     'L0_ffn_e_b2': (0.0, 0.8),
     'L0_ffn_c2s_b': (0.0, 0.596),
     'L0_ffn_dec_b': (0.0, 0.1),
     'L0_ffn_ln_g': (1.0, 0.2),
     'L0_ffn_ln_b': (0.0, 0.348)}
    factors = {'L0_attn_Wm1': 5.522,
     'L0_attn_bm1': 33.545,
     'L0_attn_Wm2': 4.699,
     'L0_attn_bm2': 31.8,
     'L0_ffn_enc_w': 4.534,
     'L0_ffn_r_w1': 3.443}
    for name, (base, spread) in spreads.items():
        noise = np.random.default_rng([zlib.crc32(name.encode()), seed]).standard_normal(out[name].shape)
        drawn = base * np.exp(spread * noise) if base else spread * noise
        out[name] = jnp.asarray(drawn.astype(out[name].dtype))
    for name, factor in factors.items():
        out[name] = (out[name] * factor).astype(out[name].dtype)
    return out
```

```python
import numpy as np
import concourse.bass as bass
from concourse import mybir
from contextlib import ExitStack

BATCH, SEQ, C = 2, 2048, 256
HEADS, HD = 16, 16
HID = 64
FF = 1024
ENC = 512
MOE = 64
NE = 8
EH = 256
P = 128
BLK = 512
NBLK = BATCH * SEQ // BLK
NT = BLK // P
CH = 32
NC = BLK // CH
CT = P // CH
LN_EPS = 1e-5
RMS_EPS = float(np.finfo(np.float32).eps)

WEIGHTS = [
    ("wq", 128, 2 * C), ("wkv", 128, 2 * 2 * C), ("wm1", 128, 2 * HID), ("wm2", 65, HEADS),
    ("wproj", 128, 2 * C), ("wfc", 128, 2 * FF), ("wcp", 128, 8 * C), ("enc", 128, 2 * ENC),
    ("s2c", 128, 4 * MOE), ("rw1", 64, 64), ("rw2", 65, NE), ("ew1", 65, NE * EH),
    ("ew2", 128, 2 * NE * MOE), ("eb2", 8, MOE), ("c2s", 64, ENC), ("dec", 128, 4 * C), ("decb", 1, C),
    ("bm1", 64, 1), ("bm2", 16, 1), ("encb", 128, 4), ("s2cb", 64, 1), ("rb1", 64, 1), ("c2sb", 128, 4),
]
CONSTS = [
    ("ident", 128, 128), ("headblk", 128, 128), ("later", 128, 128), ("eye32", 128, CH), ("pair", 128, 2),
    ("selP", 16, 2 * 128), ("tie", 128, NE * NE), ("inchunk", 16, BLK),
    ("neghalf", 128, NT), ("chunk", 128, CT), ("ones", 1, 128),
]
SETUP = [("wmod", 128, 2 * 6 * C), ("lng", 128, C), ("lnb", 128, C), ("cT", 128, 2 * BATCH)]


def offsets(table):
    out, at = {}, 0
    for name, parts, cols in table:
        out[name] = (at, parts, cols)
        at += cols
    return out, at


WOFF, WCOLS = offsets(WEIGHTS)
COFF, CCOLS = offsets(CONSTS)
SOFF, SCOLS = offsets(SETUP)

G_PE = ["xT0", "xT1", "m1", "q0", "q1", "kv0", "kv1", "kv2", "kv3", "zf", "zt", "kT0", "kT1", "P0", "P1",
        "dk0", "dk1", "dk2", "dk3", "scores", "U0", "U1", "Y0", "Y1", "Y2", "Y3",
        "proj0", "proj1", "y2a", "y2b"]
G_ACT = ["hT0", "hT1", "m1s", "q0", "q1", "gf", "gt", "kT0", "kT1", "Ae0", "Ae1", "Ae2", "Ae3", "yT0", "yT1",
         "y2T0", "y2T1", "sq"]
G_DVE = ["stats", "mv", "xn", "kv0", "kv1", "kv2", "kv3", "df", "dt", "d0", "d1", "P", "pend", "qP",
         "D0", "D1", "D2", "D3", "A0", "A1", "A2", "A3"] \
    + [f"S{c}" for c in range(2 * NC)] + ["y2a", "y2b"]
G_POOL = ["var", "rstd", "Qx", "B0", "B1", "B2", "B3", "G0", "G1", "G2", "G3", "Ks0", "Ks1", "Ks2", "Ks3",
          "Vx0", "Sm0", "Sm1", "Sm2", "Vx1", "Sm3", "Vx2", "Vx3"]
F_PE = [f"fc{m}" for m in range(8)] + [f"cp{i}" for i in range(4)] + ["hT0", "hT1"] \
    + [f"enc{m}" for m in range(4)] + ["s2c", "r1", "contK", "r2", "cT"] \
    + ["sp0"] + [s for e in range(NE) for s in ([f"sp{e + 1}"] if e < NE - 1 else []) + [f"e1_{2 * e}", f"e1_{2 * e + 1}"]
                 + ([f"e2_{e - 1}"] if e else [])] \
    + [f"e2_{NE - 1}"] + [f"c2s{m}" for m in range(4)] + [f"dec{i}" for i in range(4)]
F_ACT = [f"relu{m}" for m in range(8)] + ["hT0", "hT1"] + [f"enc{m}" for m in range(4)] \
    + ["cont", "rh", "contK", "w1", "cT"] + [f"eh{m}" for m in range(16)] + ["mT"] + [f"ra{m}" for m in range(4)] \
    + [f"dec{i}" for i in range(4)]
F_DVE = ["ms", "r2"] + [f"sq{m}" for m in range(8)] + [f"t{i}" for i in range(4)] \
    + ["tg", "x1", "stats", "mv", "xn", "L", "gt", "eq", "eqm", "rank4", "rank", "top1", "top2", "l1", "l2m", "l2", "diff",
       "w2", "c1", "c2", "comb"] + [f"ce{e}" for e in range(NE)] + ["stats3", "mv3", "dn", "g3", "out"]
F_POOL = ["var", "rstd", "x1b"] + [f"cs{e}" for e in range(NE)] + ["var3", "rstd3"]


def done(steps, n, name):
    return n * len(steps) + steps.index(name) + 1


def build(nc, x, w_d, c_d, s_d, out):
    f32 = mybir.dt.float32
    ALU, ACT, AX = mybir.AluOpType, mybir.ActivationFunctionType, mybir.AxisListType
    ctx = ExitStack()
    with ctx:
        def sb(name, shape):
            return ctx.enter_context(nc.sbuf_tensor(name, shape, f32))

        def sem(name):
            return ctx.enter_context(nc.semaphore(name))

        W = sb("W", [P, WCOLS])
        K = sb("K", [P, CCOLS])

        def w(name):
            at, parts, cols = WOFF[name]
            return W[0:parts, at:at + cols]

        def k(name):
            at, parts, cols = COFF[name]
            return K[0:parts, at:at + cols]

        wq = w("wq").rearrange("p (k m) -> p k m", k=2)
        wkv = w("wkv").rearrange("p (k m) -> p k m", k=2)
        wm1 = w("wm1").rearrange("p (k m) -> p k m", k=2)
        wproj = w("wproj").rearrange("p (k m) -> p k m", k=2)
        wfc = w("wfc").rearrange("p (k m) -> p k m", k=2)
        wcp = w("wcp").rearrange("p (k m) -> p k m", k=8)
        wenc = w("enc").rearrange("p (k m) -> p k m", k=2)
        ws2c = w("s2c").rearrange("p (k m) -> p k m", k=4)
        we1 = w("ew1").rearrange("p (e m) -> p e m", e=NE)
        we2 = w("ew2").rearrange("p (k e m) -> p k e m", k=2, e=NE)
        wdec = w("dec").rearrange("p (k m) -> p k m", k=4)
        ident = k("ident")
        selP = k("selP").rearrange("p (a m) -> p a m", a=2)

        modT = sb("modT", [P, 12, BATCH])
        ga = [sb(f"ga{b}", [P, C]) for b in range(BATCH)]
        gscale = [sb(f"gscale{b}", [P, C]) for b in range(BATCH)]
        gshift = [sb(f"gshift{b}", [P, C]) for b in range(BATCH)]

        xin = [sb(f"xin{i}", [P, NT, C]) for i in range(2)]
        stat = sb("stat", [P, NT, 6])
        mv = sb("mv", [P, NT, 2])
        rstd = sb("rstd", [P, NT])
        m1s = sb("m1s", [65, BLK])
        qs = sb("qs", [P, 2, BLK])
        Qx = sb("Qx", [P, 2, 2, BLK])
        kv = sb("kv", [P, NT, 2 * C])
        kT = sb("kT", [P, 2, BLK])
        xn = Qx[:, 0, :, :].rearrange("p a (b c) -> p (a b) c", c=C)
        hT = kT
        gf = sb("gf", [16, BLK])
        df = gf
        pm = sb("pm", [16, 2, BLK])
        Pf = pm[:, 1, :]
        gt = sb("gt", [P, NT, HEADS])
        dt = sb("dt", [P, NT, HEADS])
        pend = sb("pend", [P, 2, NC])
        BA = sb("BA", [P, NT, HEADS, CH])
        D = sb("D", [P, NT, HEADS, CH])
        S = sb("S", [P, NC, 2, P])
        carry = [sb(f"carry{b}", [P, 2, P]) for b in range(BATCH)]
        Vx = sb("Vx", [P, 2, 8 * (P + HD)])
        vx_diag = Vx[:, :, :].rearrange("p a (h m) -> p a h m", h=8)[:, :, :, 0:HD]
        Aexp = [sb(f"Aexp{i}", [P, HEADS, P]) for i in range(2)]
        y2T = sb("y2T", [P, 2, BLK])
        y2 = sb("y2", [P, NT, C])
        Ks = y2
        sumsq = sb("sumsq", [P, NT])

        ms = sb("ms", [P, NT])
        r2 = sb("r2", [P, NT])
        R = sb("R", [P, 8, BLK])
        x1 = sb("x1", [P, NT, C])
        stat2 = sb("stat2", [P, NT, 6])
        mv2 = sb("mv2", [P, NT, 2])
        rstd2 = sb("rstd2", [P, NT])
        xn2 = sb("xn2", [P, NT, C])
        h2T = sb("h2T", [P, 2, BLK])
        cont = sb("cont", [65, BLK])
        rh = sb("rh", [65, BLK])
        L = sb("L", [P, NT, NE])
        cmp = sb("cmp", [P, 2, NT, NE, NE])
        idle = sb("idle", [P, 16])
        rank = sb("rank", [P, NT, NE])
        top = sb("top", [P, 2, NT, NE])
        sc = sb("sc", [P, 6, NT])
        lm = sb("lm", [P, NT, NE])
        comb = sb("comb", [P, NT, NE])
        cT = R[0:NE, 3, :]
        ce = h2T
        contK = R[:, 0, 0:NT * (MOE + 1)].rearrange("p (i m) -> p i m", i=NT)
        cs = [R[:, 1 + a, 0:NT * (MOE + 1)].rearrange("p (i m) -> p i m", i=NT) for a in range(2)]
        mT = rh[0:MOE, :]
        dec = xn2
        res = x1

        pg_all = ctx.enter_context(nc.psum_tensor("pg", [P, 4, BLK], f32))
        pg = [pg_all[:, i, :] for i in range(4)]
        pf = [ctx.enter_context(nc.psum_tensor(f"pf{i}", [P, BLK], f32)) for i in range(4)]

        loaded = sem("loaded")
        mod_loaded = sem("mod_loaded")
        x_loaded = [sem(f"x_loaded{i}") for i in range(2)]
        stored = sem("stored")
        zeroed = sem("zeroed")
        setup_act, setup_dve, setup_pe = sem("setup_act"), sem("setup_dve"), sem("setup_pe")
        g_pe, g_act, g_dve, g_pool = sem("g_pe"), sem("g_act"), sem("g_dve"), sem("g_pool")
        f_pe, f_act, f_dve, f_pool = sem("f_pe"), sem("f_act"), sem("f_dve"), sem("f_pool")
        SETUP_DVE = 30

        s_all = sb("s_all", [P, 8])
        wm_v = S[:, 0:12, :, :].rearrange("p a b c -> p (a b c)")
        wmod = wm_v.rearrange("p (k m) -> p k m", k=2)
        lng = S[:, 12, :, :].rearrange("p a b -> p (a b)")
        lnb = S[:, 13, :, :].rearrange("p a b -> p (a b)")
        cTs = s_all[:, 0:4]
        silu = s_all[:, 4:8]
        silu_bc = BA[:, 0, :, :].rearrange("p a b -> p (a b)").rearrange("p (k b m) -> p k b m", k=2, b=2)

        ORDER = ["G0", "F1", "G1", "F2", "F3", "G2", "F4", "G3", "F5", "G5", "F6", "G6", "F7", "G7", "F8", "G8", "G9",
                 "F9", "X0", "G10", "X1", "G10b", "X2", "G11", "X3", "X4", "G13", "X5", "X6", "G14", "X7", "X8",
                 "F20", "F21"]

        def steps(eng, emit):
            def step(ng, nf, pg_, pf_):
                for part in ORDER:
                    if part[0] == "G" and ng is not None:
                        emit(part, ng, pg_)
                    if part[0] != "G" and nf is not None:
                        emit(part, nf, pf_)
            step(0, None, 0, None)
            step(1, 0, 1, 0)
            with eng.Fori(0, NBLK // 2 - 1) as j:
                step(j * 2 + 2, j * 2 + 1, 0, 1)
                step(j * 2 + 3, j * 2 + 2, 1, 0)
            step(None, NBLK - 1, None, 1)

        carried = [0]

        def carry_wait(eng):
            if eng is nc.tensor:
                nc.tensor.ldweights(K[:, 0:64].bitcast(mybir.dt.bfloat16), tile_position=(0, 0))
            elif eng is nc.vector:
                nc.vector.memset(idle[:, 0:1], 0.0)
            else:
                carried[0] = carried[0] % 15 + 1
                nc.gpsimd.tensor_tensor(idle[:, carried[0]:carried[0] + 1], K[:, 0:1], K[:, 0:1], ALU.add)

        def first(n):
            return isinstance(n, int) and n == 0

        def x_count(n, b):
            return (n // 2 + 1) * 16 if isinstance(n, int) else (n - b) * 8 + 16

        block = ctx.enter_context(nc.Block())

        @block.sync
        def _(sp):
            xv = x.rearrange("b (t i p) c -> b t p i c", p=P, i=NT)
            ov = out.rearrange("b (t i p) c -> b t p i c", p=P, i=NT)

            def load_x(t, b):
                sp.dma_start(xin[b][:, :, :], xv[b, t, :, :, :]).then_inc(x_loaded[b], 16)

            def store(n, t, b):
                sp.wait_ge(f_dve, done(F_DVE, n, "out"))
                sp.dma_start(ov[b, t, :, :, :], res[:, :, :]).then_inc(stored, 16)

            sp.dma_start(s_all[:, 0:4], s_d[:, SOFF["cT"][0]:SOFF["cT"][0] + 4]).then_inc(mod_loaded, 16)
            sp.dma_start(wm_v, s_d[:, 0:12 * C]).then_inc(mod_loaded, 16)
            sp.dma_start(S[:, 12:14, :, :].rearrange("p a b c -> p (a b c)"), s_d[:, 12 * C:14 * C]).then_inc(mod_loaded, 16)
            load_x(0, 0)
            sp.dma_start(K[:, :], c_d).then_inc(loaded, 16)
            cut = WOFF["wfc"][0]
            sp.dma_start(W[:, 0:cut], w_d[:, 0:cut]).then_inc(loaded, 16)
            sp.dma_start(W[:, cut:WCOLS], w_d[:, cut:WCOLS]).then_inc(loaded, 16)
            load_x(0, 1)
            with sp.Fori(0, SEQ // BLK - 1) as t:
                for b in range(BATCH):
                    sp.wait_ge(f_dve, done(F_DVE, t * 2 + b, "x1"))
                    load_x(t + 1, b)
                    store(t * 2 + b, t, b)
            for b in range(BATCH):
                store(NBLK - 2 + b, SEQ // BLK - 1, b)
            sp.wait_ge(stored, 16 * NBLK)

        @block.tensor
        def _(pe):
            mm = nc.tensor.matmul

            def tr(out_, in_):
                return nc.tensor.transpose(out_, in_, ident[0:in_.shape[0], 0:in_.shape[0]])

            pe.wait_ge(mod_loaded, 48)
            pe.wait_ge(setup_dve, 2)
            for m in range(12):
                for kk in range(2):
                    last = mm(pg[0][:, 2 * m:2 * m + 2], wmod[:, kk, m * P:(m + 1) * P], silu[:, 2 * kk:2 * kk + 2],
                              start=(kk == 0), stop=(kk == 1))
            last.then_inc(setup_pe, 1)
            for b in range(BATCH):
                for a, which in enumerate((2, 5)):
                    for kk in range(2):
                        last = mm(pg[1 + b][:, a * C:(a + 1) * C], silu_bc[:, kk, b, :],
                                  wmod[:, kk, which * C:(which + 1) * C], start=(kk == 0), stop=(kk == 1))
            last.then_inc(setup_pe, 1)
            pe.wait_ge(loaded, 48)
            pe.wait_ge(setup_dve, SETUP_DVE)

            def before(n, sem_, table, name):
                if not first(n):
                    pe.wait_ge(sem_, done(table, n - 1, name))

            def emit(part, n, b):
                if part == "G1":
                    pe.wait_ge(g_dve, done(G_DVE, n, "xn"))
                    before(n, g_dve, G_DVE, "y2b")
                    for h in range(2):
                        for i in range(NT):
                            last = tr(pg[h][:, i * P:(i + 1) * P], xn[:, i, h * P:(h + 1) * P])
                        last.then_inc(g_pe, 1)
                if part == "G2":
                    pe.wait_ge(g_act, done(G_ACT, n, "hT1"))
                    for kk in range(2):
                        last = mm(pg[2][0:HID, :], wm1[:, kk, :], hT[:, kk, :], start=(kk == 0), stop=(kk == 1))
                    last.then_inc(g_pe, 1)
                    for h, bank in ((0, 3), (1, 0)):
                        for kk in range(2):
                            last = mm(pg[bank][:, :], wq[:, kk, h * P:(h + 1) * P], hT[:, kk, :],
                                      start=(kk == 0), stop=(kk == 1))
                        last.then_inc(g_pe, 1)
                    for i, bank, freed in ((0, 1, None), (1, 2, "m1s"), (2, 3, "q0"), (3, 0, "q1")):
                        if freed:
                            pe.wait_ge(g_act, done(G_ACT, n, freed))
                        for kk in range(2):
                            last = mm(pg[bank][:, :], hT[:, kk, i * P:(i + 1) * P], wkv[:, kk, :],
                                      start=(kk == 0), stop=(kk == 1))
                        last.then_inc(g_pe, 1)
                if part == "G3":
                    pe.wait_ge(g_dve, done(G_DVE, n, "kv1"))
                    carry_wait(nc.tensor)
                    mm(pg[1][0:HEADS, :], w("wm2")[0:HID, :], m1s[0:HID, :], start=True, stop=True).then_inc(g_pe, 1)
                    for i in range(NT):
                        last = mm(pg[2][:, i * HEADS:(i + 1) * HEADS], m1s[:, i * P:(i + 1) * P], w("wm2"),
                                  start=True, stop=True)
                    last.then_inc(g_pe, 1)
                    pe.wait_ge(g_dve, done(G_DVE, n, "kv3"))
                    for h, bank in ((0, 3), (1, 0)):
                        for i in range(NT):
                            last = tr(pg[bank][:, i * P:(i + 1) * P], kv[:, i, h * P:(h + 1) * P])
                        last.then_inc(g_pe, 1)
                if part == "G5":
                    pe.wait_ge(g_dve, done(G_DVE, n, "P"))
                    pe.wait_ge(g_act, done(G_ACT, n, "gt"))
                    for h in range(2):
                        mm(pg[1 + h][:, :], selP[:, h, :], Pf[:, :], start=True, stop=True).then_inc(g_pe, 1)
                if part == "G6":
                    pe.wait_ge(g_act, done(G_ACT, n, "kT1"))
                    for i, bank in enumerate((3, 0, 1, 2)):
                        pe.wait_ge(g_pool, done(G_POOL, n, f"B{i}"))
                        if i == 2:
                            pe.wait_ge(g_dve, done(G_DVE, n, "qP"))
                        mm(pg[bank][:, :], k("later"), BA[:, i, :, :].rearrange("p h t -> p (h t)"),
                           start=True, stop=True).then_inc(g_pe, 1)
                if part == "G7":
                    pe.wait_ge(g_pool, done(G_POOL, n, "Qx"))
                    pe.wait_ge(g_dve, done(G_DVE, n, "D3"))
                    carry_wait(nc.tensor)
                    for i in range(NT):
                        for h in range(2):
                            for c in range(CT):
                                t0 = i * P + c * CH
                                for r in range(4):
                                    last = mm(pg[r][c * CH:(c + 1) * CH, i * P + h * 64:i * P + h * 64 + 64],
                                              kT[32 * r:32 * r + 32, h, t0:t0 + CH],
                                              Qx[32 * r:32 * r + 32, h, :, t0:t0 + CH], start=True, stop=True)
                    last.then_inc(g_pe, 1)
                if part in ("G8", "G9"):
                    u = int(part == "G9")
                    pe.wait_ge(g_pool, done(G_POOL, n, f"Ks{2 * u + 1}"))
                    pe.wait_ge(g_dve, done(G_DVE, n, f"S{NC - 1}" if u else "A3"))
                    for ii in range(2):
                        i = 2 * u + ii
                        for h in range(2):
                            for c in range(CT):
                                rows = slice(c * CH, (c + 1) * CH)
                                last = mm(pg[c][:, ii * C + h * P:ii * C + (h + 1) * P], Ks[rows, i, h * P:(h + 1) * P],
                                          kv[rows, i, C + h * P:C + (h + 1) * P], start=True, stop=True)
                    last.then_inc(g_pe, 1)
                if part in ("G10", "G11"):
                    u = int(part == "G11")
                    if u == 0:
                        pe.wait_ge(g_dve, done(G_DVE, n, f"S{2 * NC - 1}"))
                    for i in (2 * u, 2 * u + 1):
                        pe.wait_ge(g_pool, done(G_POOL, n, f"Vx{i}" if i else "Sm0"))
                        pe.wait_ge(g_act, done(G_ACT, n, f"Ae{i}"))
                        for h in range(2):
                            for c in range(CT):
                                t0 = i * P + c * CH
                                mm(pg[h][:, t0:t0 + CH], S[:, i * CT + c, h, :], qs[:, h, t0:t0 + CH],
                                   start=(c == 0), stop=False, skip_group_check=True)
                            for a in range(8 * h, 8 * h + 8):
                                last = mm(pg[h][:, i * P:(i + 1) * P], Vx[:, h, (a % 8) * P:(a % 8 + 1) * P], Aexp[i % 2][:, a, :],
                                          start=False, stop=(a == 8 * h + 7), skip_group_check=True)
                        last.then_inc(g_pe, 1)
                if part == "G13":
                    pe.wait_ge(g_act, done(G_ACT, n, "yT1"))
                    for h in range(2):
                        for kk in range(2):
                            last = mm(pg[2 + h][:, :], wproj[:, kk, h * P:(h + 1) * P], hT[:, kk, :],
                                      start=(kk == 0), stop=(kk == 1))
                        last.then_inc(g_pe, 1)
                if part == "G14":
                    pe.wait_ge(g_act, done(G_ACT, n, "y2T1"))
                    for i in range(NT):
                        for h in range(2):
                            last = tr(pg[i // 2][:, (i % 2) * C + h * P:(i % 2) * C + (h + 1) * P],
                                      y2T[:, h, i * P:(i + 1) * P])
                        if i % 2:
                            last.then_inc(g_pe, 1)
                if part in ("F1", "F2"):
                    if part == "F1":
                        pe.wait_ge(g_act, done(G_ACT, n, "y2T1"))
                        before(n, f_act, F_ACT, "dec3")
                    for m in (range(4) if part == "F1" else range(4, 8)):
                        if m >= 4:
                            pe.wait_ge(f_act, done(F_ACT, n, f"relu{m - 4}"))
                        for kk in range(2):
                            last = mm(pf[m % 4][:, :], wfc[:, kk, m * P:(m + 1) * P], y2T[:, kk, :],
                                      start=(kk == 0), stop=(kk == 1))
                        last.then_inc(f_pe, 1)
                if part == "F3":
                    for i in range(NT):
                        pe.wait_ge(f_act, done(F_ACT, n, f"relu{4 + i}"))
                        for kk in range(8):
                            if i == 0:
                                pe.wait_ge(f_dve, done(F_DVE, n, f"sq{kk}"))
                            last = mm(pf[i][:, 0:C], R[:, kk, i * P:(i + 1) * P], wcp[:, kk, :],
                                      start=(kk == 0), stop=(kk == 7))
                        last.then_inc(f_pe, 1)
                if part == "F4":
                    pe.wait_ge(f_dve, done(F_DVE, n, "xn"))
                    for h in range(2):
                        for i in range(NT):
                            last = tr(pf[h][:, i * P:(i + 1) * P], xn2[:, i, h * P:(h + 1) * P])
                        last.then_inc(f_pe, 1)
                if part == "F5":
                    pe.wait_ge(f_act, done(F_ACT, n, "hT1"))
                    for m in range(4):
                        for kk in range(2):
                            last = mm(pf[(2 + m) % 4][:, :], wenc[:, kk, m * P:(m + 1) * P], h2T[:, kk, :],
                                      start=(kk == 0), stop=(kk == 1))
                        last.then_inc(f_pe, 1)
                if part == "F6":
                    for kk in range(4):
                        pe.wait_ge(f_act, done(F_ACT, n, f"enc{kk}"))
                        last = mm(pf[2][0:MOE, :], ws2c[:, kk, :], R[:, kk, :], start=(kk == 0), stop=(kk == 3))
                    last.then_inc(f_pe, 1)
                if part == "F7":
                    pe.wait_ge(f_act, done(F_ACT, n, "cont"))
                    carry_wait(nc.tensor)
                    mm(pf[3][0:64, :], w("rw1"), cont[0:64, :], start=True, stop=True).then_inc(f_pe, 1)
                if part == "F8":
                    pe.wait_ge(f_act, done(F_ACT, n, "rh"))
                    for i in range(NT):
                        last = mm(pf[2][:, i * 65:(i + 1) * 65], cont[:, i * P:(i + 1) * P], ident[0:65, 0:65],
                                  is_transpose=True)
                    last.then_inc(f_pe, 1)
                    for i in range(NT):
                        last = mm(pf[0][:, i * NE:(i + 1) * NE], rh[:, i * P:(i + 1) * P], w("rw2"),
                                  start=True, stop=True)
                    last.then_inc(f_pe, 1)
                if part == "F9":
                    pe.wait_ge(f_dve, done(F_DVE, n, "comb"))
                    for i in range(NT):
                        last = tr(pf[1][0:NE, i * P:(i + 1) * P], comb[:, i, :])
                    last.then_inc(f_pe, 1)
                    pe.wait_ge(f_act, done(F_ACT, n, "cT"))

                def scaled(e):
                    if e:
                        pe.wait_ge(f_dve, done(F_DVE, n, f"ce{e - 1}"))
                    pe.wait_ge(f_pool, done(F_POOL, n, f"cs{e}"))
                    for i in range(NT):
                        last = tr(pf[0][0:MOE + 1, i * P:(i + 1) * P], cs[e % 2][:, i, :])
                    last.then_inc(f_pe, 1)

                def second(e):
                    for m in range(2):
                        pe.wait_ge(f_act, done(F_ACT, n, f"eh{2 * e + m}"))
                        last = mm(pf[3][0:MOE, :], we2[:, m, e, :], R[:, 4 + (2 * e + m) % 4, :],
                                  start=(e == 0 and m == 0), stop=False)
                    return last

                if part[0] == "X":
                    e = int(part[1:])
                    if e == 0:
                        scaled(0)
                    if e < NE - 1:
                        scaled(e + 1)
                    if e < NE:
                        pe.wait_ge(f_dve, done(F_DVE, n, f"ce{e}"))
                        for m in range(2):
                            if e:
                                pe.wait_ge(f_act, done(F_ACT, n, f"eh{2 * e - 2 + m}"))
                            mm(pf[1 + m][:, :], we1[:, e, m * P:(m + 1) * P], ce[0:65, e % 2, :],
                               start=True, stop=True).then_inc(f_pe, 1)
                    if e:
                        last = second(e - 1)
                        if e < NE:
                            last.then_inc(f_pe, 1)
                    if e == NE:
                        mm(pf[3][0:MOE, :], w("eb2"), cT, start=False, stop=True).then_inc(f_pe, 1)
                if part == "F20":
                    pe.wait_ge(f_act, done(F_ACT, n, "mT"))
                    for m in range(4):
                        mm(pf[(1 + m) % 4][:, :], w("c2s")[:, m * P:(m + 1) * P], mT,
                           start=True, stop=True).then_inc(f_pe, 1)
                if part == "F21":
                    for i in range(NT):
                        for kk in range(4):
                            if i == 0:
                                pe.wait_ge(f_act, done(F_ACT, n, f"ra{kk}"))
                            mm(pf[(1 + i) % 4][:, 0:C], R[:, kk, i * P:(i + 1) * P], wdec[:, kk, :],
                               start=(kk == 0), stop=False)
                        mm(pf[(1 + i) % 4][:, 0:C], k("ones"), w("decb"), start=False, stop=True).then_inc(f_pe, 1)

            steps(pe, emit)

        @block.scalar
        def _(act):
            A = nc.scalar.activation
            act.wait_ge(mod_loaded, 48)
            A(silu, cTs, ACT.Sigmoid).then_inc(setup_act, 1)
            act.wait_ge(loaded, 48)
            act.wait_ge(setup_dve, SETUP_DVE)

            def before(n, sem_, table, name):
                if not first(n):
                    act.wait_ge(sem_, done(table, n - 1, name))

            def emit(part, n, b):
                if part == "G1":
                    before(n, g_pe, G_PE, "proj1")
                    before(n, g_act, G_ACT, "sq")
                    for h in range(2):
                        act.wait_ge(g_pe, done(G_PE, n, f"xT{h}"))
                        A(hT[:, h, :], pg[h][:, :], ACT.Identity, scale=modT[:, 2 + h, b:b + 1],
                          bias=modT[:, h, b:b + 1]).then_inc(g_act, 1)
                if part == "G2":
                    act.wait_ge(g_pe, done(G_PE, n, "m1"))
                    A(m1s[0:HID, :], pg[2][0:HID, :], ACT.Relu, bias=w("bm1")).then_inc(g_act, 1)
                    for h, bank in ((0, 3), (1, 0)):
                        act.wait_ge(g_pe, done(G_PE, n, f"q{h}"))
                        A(qs[:, h, :], pg[bank][:, :], ACT.Copy).then_inc(g_act, 1)
                if part == "G3":
                    act.wait_ge(g_pe, done(G_PE, n, "zf"))
                    A(gf[:, :], pg[1][0:HEADS, :], ACT.Sigmoid, bias=w("bm2")).then_inc(g_act, 1)
                    act.wait_ge(g_pe, done(G_PE, n, "zt"))
                    A(gt[:, :, :].rearrange("p i h -> p (i h)"), pg[2][:, 0:NT * HEADS], ACT.Sigmoid).then_inc(g_act, 1)
                    for h, bank in ((0, 3), (1, 0)):
                        act.wait_ge(g_pe, done(G_PE, n, f"kT{h}"))
                        A(kT[:, h, :], pg[bank][:, :], ACT.Copy).then_inc(g_act, 1)
                if part in ("G7", "G8", "G10b"):
                    for i in {"G7": [0], "G8": [1], "G10b": [2, 3]}[part]:
                        act.wait_ge(g_dve, done(G_DVE, n, f"A{i}"))
                        if i >= 2:
                            act.wait_ge(g_pe, done(G_PE, n, f"Y{i - 2}"))
                        else:
                            before(n, g_pe, G_PE, f"Y{i + 2}")
                        for c in range(CT):
                            last = A(Aexp[i % 2][:, :, c * CH:(c + 1) * CH], BA[:, i, :, :], ACT.Copy,
                                     scale=k("chunk")[:, c:c + 1])
                        last.then_inc(g_act, 1)
                if part == "G11":
                    act.wait_ge(g_pe, done(G_PE, n, "Y3"))
                    for h in range(2):
                        A(hT[:, h, :], pg[h][:, :], ACT.Copy).then_inc(g_act, 1)
                if part == "G13":
                    before(n, f_pe, F_PE, "fc7")
                    for h in range(2):
                        act.wait_ge(g_pe, done(G_PE, n, f"proj{h}"))
                        A(y2T[:, h, :], pg[2 + h][:, :], ACT.Copy).then_inc(g_act, 1)
                if part == "G14":
                    act.wait_ge(g_dve, done(G_DVE, n, "y2b"))
                    before(n, f_dve, F_DVE, "ms")
                    act.wait_ge(g_pe, done(G_PE, n, "proj1"))
                    for i in range(NT):
                        last = A(hT[:, i // 2, (i % 2) * C:(i % 2 + 1) * C], y2[:, i, :], ACT.Square,
                                 accum_out=sumsq[:, i:i + 1])
                    last.then_inc(g_act, 1)
                if part in ("F1", "F2"):
                    if part == "F1":
                        before(n, f_pe, F_PE, "dec3")
                    for m in (range(4) if part == "F1" else range(4, 8)):
                        act.wait_ge(f_pe, done(F_PE, n, f"fc{m}"))
                        A(R[:, m, :], pf[m % 4][:, :], ACT.Relu).then_inc(f_act, 1)
                if part == "F4":
                    for h in range(2):
                        act.wait_ge(f_pe, done(F_PE, n, f"hT{h}"))
                        A(h2T[:, h, :], pf[h][:, :], ACT.Identity, scale=modT[:, 8 + h, b:b + 1],
                          bias=modT[:, 6 + h, b:b + 1]).then_inc(f_act, 1)
                if part == "F5":
                    for m in range(4):
                        act.wait_ge(f_pe, done(F_PE, n, f"enc{m}"))
                        A(R[:, m, :], pf[(2 + m) % 4][:, :], ACT.Sigmoid, bias=w("encb")[:, m:m + 1]).then_inc(f_act, 1)
                if part == "F6":
                    act.wait_ge(f_pe, done(F_PE, n, "s2c"))
                    A(cont[0:MOE, :], pf[2][0:MOE, :], ACT.Identity, bias=w("s2cb")).then_inc(f_act, 1)
                if part == "F7":
                    act.wait_ge(f_pe, done(F_PE, n, "r1"))
                    A(rh[0:64, :], pf[3][0:64, :], ACT.Relu, bias=w("rb1")).then_inc(f_act, 1)
                if part == "F8":
                    act.wait_ge(f_pe, done(F_PE, n, "contK"))
                    A(contK[:, :, :].rearrange("p i m -> p (i m)"), pf[2][:, 0:NT * 65], ACT.Copy).then_inc(f_act, 1)
                    act.wait_ge(f_dve, done(F_DVE, n, "diff"))
                    A(sc[:, 3, :], sc[:, 2, :], ACT.Sigmoid).then_inc(f_act, 1)
                if part == "F9":
                    act.wait_ge(f_pe, done(F_PE, n, "cT"))
                    A(cT, pf[1][0:NE, :], ACT.Copy).then_inc(f_act, 1)
                if part[0] == "X" and int(part[1:]) < NE:
                    e = int(part[1:])
                    for m in (2 * e, 2 * e + 1):
                        act.wait_ge(f_pe, done(F_PE, n, f"e1_{m}"))
                        if e >= 2:
                            act.wait_ge(f_pe, done(F_PE, n, f"e2_{e - 2}"))
                        A(R[:, 4 + m % 4, :], pf[1 + m % 2][:, :], ACT.Relu).then_inc(f_act, 1)
                if part == "X8":
                    act.wait_ge(f_pe, done(F_PE, n, f"e2_{NE - 1}"))
                    A(mT, pf[3][0:MOE, :], ACT.Copy).then_inc(f_act, 1)
                if part == "F20":
                    for m in range(4):
                        act.wait_ge(f_pe, done(F_PE, n, f"c2s{m}"))
                        A(R[:, m, :], pf[(1 + m) % 4][:, :], ACT.Sigmoid, bias=w("c2sb")[:, m:m + 1]).then_inc(f_act, 1)
                if part == "F21":
                    for i in range(NT):
                        act.wait_ge(f_pe, done(F_PE, n, f"dec{i}"))
                        A(dec[:, i, :], pf[(1 + i) % 4][:, 0:C], ACT.Sigmoid).then_inc(f_act, 1)

            steps(act, emit)

        @block.vector
        def _(dve):
            V = nc.vector
            made = [0]

            def setup(ins):
                made[0] += 1
                ins.then_inc(setup_dve, 1)
                dve.wait_ge(setup_dve, made[0])

            dve.wait_ge(setup_act, 1)
            setup(V.tensor_tensor(silu, cTs, silu, ALU.mult))
            setup(V.tensor_copy(silu_bc, silu.rearrange("p (k b) -> p k b", k=2).unsqueeze(3).to_broadcast([P, 2, 2, P])))
            dve.wait_ge(setup_pe, 1)
            setup(V.tensor_copy(modT[:, :, :].rearrange("p m b -> p (m b)"), pg[0][:, 0:24]))
            for m in (2, 8):
                setup(V.tensor_scalar(modT[:, m:m + 2, :], modT[:, m:m + 2, :], 1.0, None, ALU.add))
            dve.wait_ge(setup_pe, 2)
            for b in range(BATCH):
                raw, sgn, mag = (xn[:, a, :] for a in range(3))
                for a in range(2):
                    setup(V.tensor_copy(raw, pg[1 + b][:, a * C:(a + 1) * C]))
                    setup(V.tensor_scalar(sgn, raw, 0.0, 2.0, ALU.is_ge, ALU.mult))
                    setup(V.scalar_tensor_tensor(mag, sgn, -1.0, raw, ALU.add, ALU.mult))
                    setup(V.tensor_scalar(mag, mag, 0.25, None, ALU.max))
                    dst = ga[b] if a == 0 else gshift[b]
                    setup(V.scalar_tensor_tensor(dst[:, :], sgn, -1.0, mag, ALU.add, ALU.mult))
                setup(V.tensor_tensor(gscale[b][:, :], gshift[b][:, :], lng, ALU.mult))
                setup(V.tensor_tensor(gshift[b][:, :], gshift[b][:, :], lnb, ALU.mult))
            for t_ in (m1s, cont, rh):
                V.memset(t_[64:65, :], 1.0)
            V.memset(carry[0][:, :, :].rearrange("p a b -> p (a b)"), 0.0)
            setup(V.memset(carry[1][:, :, :].rearrange("p a b -> p (a b)"), 0.0))
            assert made[0] == SETUP_DVE
            dve.wait_ge(loaded, 48)

            def before(n, sem_, table, name):
                if not first(n):
                    dve.wait_ge(sem_, done(table, n - 1, name))

            def mine(table, n, name):
                dve.wait_ge(g_dve if table is G_DVE else f_dve, done(table, n, name))

            def emit(part, n, b):
                if part == "G0":
                    dve.wait_ge(x_loaded[b], x_count(n, b))
                    for i in range(NT):
                        last = V.bn_stats(stat[:, i, :], xin[b][:, i, :])
                    last.then_inc(g_dve, 1)
                    dve.wait_ge(g_dve, done(G_DVE, n, "stats"))
                    carry_wait(nc.vector)
                    for i in range(NT):
                        last = V.bn_aggr(mv[:, i, :], stat[:, i, :])
                    last.then_inc(g_dve, 1)
                    mine(G_DVE, n, "mv")
                    dve.wait_ge(g_pool, done(G_POOL, n, "rstd"))
                    before(n, g_pe, G_PE, "scores")
                    for i in range(NT):
                        last = V.tensor_scalar(xn[:, i, :], xin[b][:, i, :], mv[:, i, 0:1], rstd[:, i:i + 1],
                                               ALU.subtract, ALU.mult)
                    last.then_inc(g_dve, 1)
                if part == "G2":
                    for i, bank in enumerate((1, 2, 3, 0)):
                        dve.wait_ge(g_pe, done(G_PE, n, f"kv{i}"))
                        V.tensor_copy(kv[:, i, :], pg[bank][:, :]).then_inc(g_dve, 1)
                if part == "G3":
                    dve.wait_ge(g_act, done(G_ACT, n, "gf"))
                    V.tensor_scalar(df[:, :], gf[:, :], -1.0, 1.0, ALU.mult, ALU.add).then_inc(g_dve, 1)
                    dve.wait_ge(g_act, done(G_ACT, n, "gt"))
                    V.tensor_scalar(dt[:, :, :].rearrange("p i h -> p (i h)"), gt[:, :, :].rearrange("p i h -> p (i h)"),
                                    -1.0, 1.0, ALU.mult, ALU.add).then_inc(g_dve, 1)
                    mine(G_DVE, n, "df")
                    V.tensor_tensor(pm[:, 0, :], df[:, :], k("inchunk"), ALU.mult).then_inc(g_dve, 1)
                    mine(G_DVE, n, "d0")
                    V.tensor_tensor(pm[:, 1, :], df[:, :], pm[:, 0, :], ALU.subtract).then_inc(g_dve, 1)
                    mine(G_DVE, n, "d1")
                    V.tensor_tensor_scan(Pf[:, :], pm[:, 0, :], pm[:, 1, :], 0.0, ALU.mult, ALU.add).then_inc(g_dve, 1)
                if part == "G5":
                    dve.wait_ge(g_pe, done(G_PE, n, "P1"))
                    for h in range(2):
                        last = V.tensor_copy(pend[:, h, :], pg[1 + h][:, CH - 1:BLK:CH])
                    last.then_inc(g_dve, 1)
                    dve.wait_ge(g_pool, done(G_POOL, n, "Qx"))
                    for h in range(2):
                        last = V.tensor_tensor(qs[:, h, :], qs[:, h, :], pg[1 + h][:, :], ALU.mult)
                    last.then_inc(g_dve, 1)
                if part == "G6":
                    for i, bank in enumerate((3, 0, 1, 2)):
                        dve.wait_ge(g_pe, done(G_PE, n, f"dk{i}"))
                        dve.wait_ge(g_pool, done(G_POOL, n, f"G{i}"))
                        d = D[:, i, :, :].rearrange("p h t -> p (h t)")
                        V.tensor_tensor_scan(d, pg[bank][:, :], d, 0.0, ALU.mult, ALU.add).then_inc(g_dve, 1)
                if part == "G7":
                    dve.wait_ge(g_pe, done(G_PE, n, "scores"))
                    mine(G_DVE, n, "D3")
                    for i in range(NT):
                        V.tensor_tensor(BA[:, i, :, :].rearrange("p (a r b) t -> p r a (b t)", a=2, r=4),
                                        pg_all[:, :, i * P:(i + 1) * P].rearrange("p r (a m) -> p r a m", a=2),
                                        D[:, i, :, :].rearrange("p (a r b) t -> p r a (b t)", a=2, r=4),
                                        ALU.mult).then_inc(g_dve, 1)
                if part in ("G8", "G9"):
                    u = int(part == "G9")
                    dve.wait_ge(g_pe, done(G_PE, n, f"U{u}"))
                    if u == 1:
                        dve.wait_ge(g_pool, done(G_POOL, n, "Sm0"))
                    for c in range(NC // 2 * u, NC // 2 * (u + 1)):
                        ii, cc = (c // CT) % 2, c % CT
                        for h in range(2):
                            if c:
                                mine(G_DVE, n, f"S{2 * (c - 1) + h}")
                            src = S[:, c, h, :] if c else carry[b][:, h, :]
                            dst = S[:, c + 1, h, :] if c < NC - 1 else carry[b][:, h, :]
                            V.scalar_tensor_tensor(dst, src, pend[:, h, c:c + 1], pg[cc][:, ii * C + h * P:ii * C + (h + 1) * P],
                                                   ALU.mult, ALU.add).then_inc(g_dve, 1)
                if part == "G14":
                    for a in range(2):
                        dve.wait_ge(g_pe, done(G_PE, n, f"y2{'ab'[a]}"))
                        V.tensor_copy(y2[:, 2 * a:2 * a + 2, :].rearrange("p i c -> p (i c)"), pg[a][:, :]).then_inc(g_dve, 1)
                if part == "F1":
                    dve.wait_ge(g_act, done(G_ACT, n, "sq"))
                    V.tensor_scalar(ms[:, :], sumsq[:, :], 1.0 / C, RMS_EPS, ALU.mult, ALU.add).then_inc(f_dve, 1)
                    mine(F_DVE, n, "ms")
                    V.reciprocal(r2[:, :], ms[:, :]).then_inc(f_dve, 1)
                if part in ("F1", "F2"):
                    for m in (range(4) if part == "F1" else range(4, 8)):
                        dve.wait_ge(f_act, done(F_ACT, n, f"relu{m}"))
                        V.tensor_tensor(R[:, m, :], R[:, m, :], R[:, m, :], ALU.mult).then_inc(f_dve, 1)
                if part == "F3":
                    if not first(n):
                        dve.wait_ge(stored, n * 16)
                    for i in range(NT):
                        dve.wait_ge(f_pe, done(F_PE, n, f"cp{i}"))
                        V.scalar_tensor_tensor(x1[:, i, :], pf[i][:, 0:C], r2[:, i:i + 1], y2[:, i, :],
                                               ALU.mult, ALU.add).then_inc(f_dve, 1)
                    mine(F_DVE, n, "t3")
                    V.tensor_tensor(x1[:, :, :], x1[:, :, :], ga[b][:, :].unsqueeze(1).to_broadcast([P, NT, C]), ALU.mult).then_inc(f_dve, 1)
                    mine(F_DVE, n, "tg")
                    V.tensor_tensor(x1[:, :, :], x1[:, :, :], xin[b][:, :, :], ALU.add).then_inc(f_dve, 1)
                    mine(F_DVE, n, "x1")
                    for i in range(NT):
                        last = V.bn_stats(stat2[:, i, :], x1[:, i, :])
                    last.then_inc(f_dve, 1)
                    dve.wait_ge(f_dve, done(F_DVE, n, "stats"))
                    carry_wait(nc.vector)
                    for i in range(NT):
                        last = V.bn_aggr(mv2[:, i, :], stat2[:, i, :])
                    last.then_inc(f_dve, 1)
                    mine(F_DVE, n, "mv")
                    dve.wait_ge(f_pool, done(F_POOL, n, "rstd"))
                    for i in range(NT):
                        last = V.tensor_scalar(xn2[:, i, :], x1[:, i, :], mv2[:, i, 0:1], rstd2[:, i:i + 1],
                                               ALU.subtract, ALU.mult)
                    last.then_inc(f_dve, 1)
                if part == "F8":
                    dve.wait_ge(f_pe, done(F_PE, n, "r2"))
                    V.tensor_copy(L[:, :, :].rearrange("p i e -> p (i e)"), pf[0][:, 0:NT * NE]).then_inc(f_dve, 1)
                    mine(F_DVE, n, "L")
                    full = [P, NT, NE, NE]
                    le, lf = L[:, :, :].unsqueeze(3).to_broadcast(full), L[:, :, :].unsqueeze(2).to_broadcast(full)
                    tie = k("tie").rearrange("p (e f) -> p e f", e=NE).unsqueeze(1).to_broadcast(full)
                    V.tensor_tensor(cmp[:, 0], le, lf, ALU.is_lt).then_inc(f_dve, 1)
                    V.tensor_tensor(cmp[:, 1], le, lf, ALU.is_equal).then_inc(f_dve, 1)
                    mine(F_DVE, n, "eq")
                    V.tensor_tensor(cmp[:, 1], cmp[:, 1], tie, ALU.mult).then_inc(f_dve, 1)
                    mine(F_DVE, n, "eqm")
                    V.tensor_tensor(cmp[:, 0], cmp[:, 0], cmp[:, 1], ALU.add).then_inc(f_dve, 1)
                    mine(F_DVE, n, "rank4")
                    V.tensor_reduce(rank[:, :, :], cmp[:, 0], AX.X, ALU.add).then_inc(f_dve, 1)
                    mine(F_DVE, n, "rank")
                    for a in range(2):
                        V.tensor_scalar(top[:, a, :, :], rank[:, :, :], float(a), None, ALU.is_equal).then_inc(f_dve, 1)
                    V.tensor_reduce(sc[:, 0, :], L[:, :, :], AX.X, ALU.max).then_inc(f_dve, 1)
                    mine(F_DVE, n, "top2")
                    V.tensor_tensor(lm[:, :, :], L[:, :, :], top[:, 1, :, :], ALU.mult).then_inc(f_dve, 1)
                    mine(F_DVE, n, "l2m")
                    V.tensor_reduce(sc[:, 1, :], lm[:, :, :], AX.X, ALU.add).then_inc(f_dve, 1)
                    mine(F_DVE, n, "l2")
                    V.tensor_tensor(sc[:, 2, :], sc[:, 0, :], sc[:, 1, :], ALU.subtract).then_inc(f_dve, 1)
                    dve.wait_ge(f_act, done(F_ACT, n, "w1"))
                    V.tensor_scalar(sc[:, 4, :], sc[:, 3, :], -1.0, 1.0, ALU.mult, ALU.add).then_inc(f_dve, 1)
                    mine(F_DVE, n, "w2")
                    V.tensor_tensor(lm[:, :, :], top[:, 0, :, :], sc[:, 3, :].unsqueeze(2).to_broadcast([P, NT, NE]), ALU.mult).then_inc(f_dve, 1)
                    V.tensor_tensor(comb[:, :, :], top[:, 1, :, :], sc[:, 4, :].unsqueeze(2).to_broadcast([P, NT, NE]), ALU.mult).then_inc(f_dve, 1)
                    mine(F_DVE, n, "c2")
                    V.tensor_tensor(comb[:, :, :], comb[:, :, :], lm[:, :, :], ALU.add).then_inc(f_dve, 1)
                if part[0] == "X":
                    e = int(part[1:])
                    for ee in ([0, 1] if e == 0 else [e + 1] if e < NE - 1 else []):
                        dve.wait_ge(f_pe, done(F_PE, n, f"sp{ee}"))
                        if ee >= 2:
                            dve.wait_ge(f_pe, done(F_PE, n, f"e1_{2 * (ee - 2) + 1}"))
                        V.tensor_copy(ce[0:65, ee % 2, :], pf[0][0:65, :]).then_inc(f_dve, 1)
                if part == "F21":
                    for i in range(NT):
                        dve.wait_ge(f_act, done(F_ACT, n, f"dec{i}"))
                        last = V.bn_stats(stat2[:, i, :], dec[:, i, :])
                    last.then_inc(f_dve, 1)
                    dve.wait_ge(f_dve, done(F_DVE, n, "stats3"))
                    carry_wait(nc.vector)
                    for i in range(NT):
                        last = V.bn_aggr(mv2[:, i, :], stat2[:, i, :])
                    last.then_inc(f_dve, 1)
                    mine(F_DVE, n, "mv3")
                    dve.wait_ge(f_pool, done(F_POOL, n, "rstd3"))
                    for i in range(NT):
                        last = V.tensor_scalar(dec[:, i, :], dec[:, i, :], mv2[:, i, 0:1], rstd2[:, i:i + 1],
                                               ALU.subtract, ALU.mult)
                    last.then_inc(f_dve, 1)
                    mine(F_DVE, n, "dn")
                    V.tensor_tensor(dec[:, :, :], dec[:, :, :], gscale[b][:, :].unsqueeze(1).to_broadcast([P, NT, C]), ALU.mult).then_inc(f_dve, 1)
                    mine(F_DVE, n, "g3")
                    V.tensor_tensor(res[:, :, :], dec[:, :, :], x1[:, :, :], ALU.add).then_inc(f_dve, 1)

            steps(dve, emit)

        @block.gpsimd
        def _(pool):
            G = nc.gpsimd
            G.memset(Vx[:, :, :].rearrange("p a b -> p (a b)"), 0.0).then_inc(zeroed, 1)
            pool.wait_ge(zeroed, 1)
            pool.wait_ge(loaded, 48)
            pool.wait_ge(setup_dve, SETUP_DVE)

            def before(n, sem_, table, name):
                if not first(n):
                    pool.wait_ge(sem_, done(table, n - 1, name))

            def rsqrt(mv_, out_, eps, table, sem_, n, a):
                G.tensor_scalar(out_[:, :], mv_[:, :, 1], eps, None, ALU.add).then_inc(sem_, 1)
                pool.wait_ge(sem_, done(table, n, a))
                G.tensor_tensor(out_[:, :], out_[:, :], k("neghalf"), ALU.pow).then_inc(sem_, 1)

            def spread_v(n, i):
                if i:
                    pool.wait_ge(g_pe, done(G_PE, n, f"Y{i - 1}"))
                else:
                    before(n, g_pe, G_PE, "Y3")
                carry_wait(nc.gpsimd)
                G.tensor_scalar(vx_diag, kv[:, i, C:2 * C].rearrange("p (a h d) -> p a h d", a=2, h=8), 1.0, 0.0,
                                ALU.mult, ALU.add).then_inc(g_pool, 1)

            def emit(part, n, b):
                if part == "G0":
                    pool.wait_ge(g_dve, done(G_DVE, n, "mv"))
                    carry_wait(nc.gpsimd)
                    rsqrt(mv, rstd, LN_EPS, G_POOL, g_pool, n, "var")
                if part == "G3":
                    pool.wait_ge(g_act, done(G_ACT, n, "q1"))
                    carry_wait(nc.gpsimd)
                    for h in range(2):
                        for a in range(2):
                            last = G.tensor_scalar(Qx[:, h, a, :], qs[:, h, :], k("pair")[:, a:a + 1], 0.0, ALU.mult, ALU.add)
                    last.then_inc(g_pool, 1)
                    full = [P, HEADS, CH]
                    eye = k("eye32").unsqueeze(1).to_broadcast(full)
                    pool.wait_ge(g_dve, done(G_DVE, n, "dt"))
                    before(n, g_act, G_ACT, "Ae3")
                    for i in range(NT):
                        G.tensor_tensor(BA[:, i, :, :], eye, dt[:, i, :].unsqueeze(2).to_broadcast(full), ALU.mult).then_inc(g_pool, 1)
                    for i in range(NT):
                        G.tensor_tensor(D[:, i, :, :], eye, gt[:, i, :].unsqueeze(2).to_broadcast(full), ALU.mult).then_inc(g_pool, 1)
                if part == "G6":
                    before(n, f_dve, F_DVE, "t3")
                    for i in range(NT):
                        pool.wait_ge(g_dve, done(G_DVE, n, f"D{i}"))
                        full = [P, HEADS, HD]
                        G.tensor_tensor(Ks[:, i, :].rearrange("p (h d) -> p h d", h=HEADS),
                                        kv[:, i, 0:C].rearrange("p (h d) -> p h d", h=HEADS),
                                        D[:, i, :, CH - 1:CH].to_broadcast(full), ALU.mult).then_inc(g_pool, 1)
                def keep_blocks(i):
                    blk = k("headblk").unsqueeze(1)
                    lo = i * CT
                    if i == 0:
                        lo = 1
                        G.tensor_tensor(S[:, 0, :, :], carry[b][:, :, :], blk.to_broadcast([P, 2, P]), ALU.mult)
                    pool.wait_ge(g_dve, done(G_DVE, n, f"S{2 * CT * i + 2 * CT - 1}"))
                    hi = (i + 1) * CT
                    v = S[:, lo:hi, :, :].rearrange("p c h m -> p (c h) m")
                    G.tensor_tensor(v, v, blk.to_broadcast([P, 2 * (hi - lo), P]), ALU.mult).then_inc(g_pool, 1)

                if part == "G7":
                    spread_v(n, 0)
                if part == "G9":
                    keep_blocks(0)
                    keep_blocks(1)
                if part == "G10":
                    keep_blocks(2)
                    spread_v(n, 1)
                    keep_blocks(3)
                if part == "G10b":
                    spread_v(n, 2)
                if part == "G11":
                    spread_v(n, 3)
                if part == "F3":
                    pool.wait_ge(f_dve, done(F_DVE, n, "mv"))
                    carry_wait(nc.gpsimd)
                    rsqrt(mv2, rstd2, LN_EPS, F_POOL, f_pool, n, "var")
                if part == "F5":
                    pool.wait_ge(f_dve, done(F_DVE, n, "xn"))
                    G.tensor_tensor(x1[:, :, :], x1[:, :, :], gshift[b][:, :].unsqueeze(1).to_broadcast([P, NT, C]),
                                    ALU.add).then_inc(f_pool, 1)
                if part[0] == "X":
                    e = int(part[1:])
                    for ee in ([0, 1] if e == 0 else [e + 1] if e < NE - 1 else []):
                        if ee == 0:
                            pool.wait_ge(f_act, done(F_ACT, n, "contK"))
                            pool.wait_ge(f_dve, done(F_DVE, n, "comb"))
                        if ee >= 2:
                            pool.wait_ge(f_pe, done(F_PE, n, f"sp{ee - 2}"))
                        G.tensor_tensor(cs[ee % 2][:, :, :], contK[:, :, :],
                                        comb[:, :, ee:ee + 1].to_broadcast([P, NT, MOE + 1]), ALU.mult).then_inc(f_pool, 1)
                if part == "F21":
                    pool.wait_ge(f_dve, done(F_DVE, n, "mv3"))
                    carry_wait(nc.gpsimd)
                    rsqrt(mv2, rstd2, LN_EPS, F_POOL, f_pool, n, "var3")

            steps(pool, emit)


def pack(table, offs, cols, arrays):
    out = np.zeros((P, cols), np.float32)
    for name, parts, n in table:
        out[0:parts, offs[name][0]:offs[name][0] + n] = arrays[name].reshape(parts, n)
    return out


def kernel(**inputs):
    import concourse.bacc as bacc
    from concourse.bass_utils import run_bass_kernel_spmd as run

    a = {n: np.asarray(v) for n, v in inputs.items()}
    at = {n[len("L0_attn_"):]: v for n, v in a.items() if n.startswith("L0_attn_")}
    ff = {n[len("L0_ffn_"):]: v for n, v in a.items() if n.startswith("L0_ffn_")}

    def rows(m, k=P):
        m = np.ascontiguousarray(m)
        return m.reshape(-1, k, m.shape[-1]).transpose(1, 0, 2)

    def under(m, bias):
        return np.concatenate([m, bias[..., None, :]], axis=-2)

    weights = {
        "wq": rows(at["Wq"].T), "wkv": rows(np.concatenate([at["Wk"].T, at["Wv"].T], axis=1)), "wm1": rows(at["Wm1"].T),
        "wm2": under(at["Wm2"].T, at["bm2"]), "wproj": rows(at["Wproj"].T), "wfc": rows(at["Wfc"].T),
        "wcp": rows(at["Wcp"].T), "enc": rows(ff["enc_w"]), "s2c": rows(ff["s2c_w"]), "rw1": ff["r_w1"],
        "rw2": under(ff["r_w2"], ff["r_b2"]), "ew1": under(ff["e_w1"], ff["e_b1"]).transpose(1, 0, 2),
        "ew2": ff["e_w2"].reshape(NE, 2, P, MOE).transpose(2, 1, 0, 3), "eb2": ff["e_b2"], "c2s": ff["c2s_w"],
        "dec": rows(ff["dec_w"]), "decb": ff["dec_b"], "bm1": at["bm1"], "bm2": at["bm2"],
        "encb": ff["enc_b"].reshape(4, P).T, "s2cb": ff["s2c_b"], "rb1": ff["r_b1"], "c2sb": ff["c2s_b"].reshape(4, P).T,
    }
    p, f = np.arange(P)[:, None], np.arange(P)[None, :]
    consts = {
        "ident": p == f, "headblk": p // HD == f // HD, "later": (p // CH == f // CH) & (p > f),
        "eye32": p % CH == np.arange(CH)[None, :], "pair": (p // HD) % 2 == np.arange(2)[None, :],
        "selP": np.arange(16)[:, None, None] == np.arange(2)[None, :, None] * 8 + (np.arange(P) // HD)[None, None, :],
        "tie": np.broadcast_to(np.arange(NE)[None, :] < np.arange(NE)[:, None], (P, NE, NE)),
        "inchunk": np.broadcast_to(np.arange(BLK) % CH != 0, (16, BLK)), "neghalf": np.full((P, NT), -0.5),
        "chunk": p // CH == np.arange(CT)[None, :], "ones": np.ones((1, P)),
    }
    consts = {n: np.asarray(v, np.float32) for n, v in consts.items()}
    setup = {
        "wmod": rows(a["L0_wmod"]), "lng": np.broadcast_to(ff["ln_g"], (P, C)), "lnb": np.broadcast_to(ff["ln_b"], (P, C)),
        "cT": a["L0_c"].T.reshape(2, P, BATCH).transpose(1, 0, 2),
    }
    arrays = {"x": np.ascontiguousarray(at["x"]), "w": pack(WEIGHTS, WOFF, WCOLS, weights),
              "c": pack(CONSTS, COFF, CCOLS, consts), "s": pack(SETUP, SOFF, SCOLS, setup)}
    nc = bacc.Bacc("TRN2", target_bir_lowering=False, num_devices=1)
    args = [nc.dram_tensor(n, v.shape, mybir.dt.float32, kind="ExternalInput").ap() for n, v in arrays.items()]
    out = nc.dram_tensor("out", (BATCH, SEQ, C), mybir.dt.float32, kind="ExternalOutput").ap()
    build(nc, *args, out)
    r = run(nc, [arrays], core_ids=[0])
    return r.results[0]["out"]
```

```python
import numpy as np
import concourse.bass as bass
from concourse import mybir
from contextlib import ExitStack

BATCH, SEQ, C = 2, 2048, 256
HEADS, HD = 16, 16
HID = 64
FF = 1024
ENC = 512
MOE = 64
NE = 8
EH = 256
P = 128
BLK = 512
NBLK = BATCH * SEQ // BLK
NT = BLK // P
CH = 32
NC = BLK // CH
CT = P // CH
LN_EPS = 1e-5
RMS_EPS = float(np.finfo(np.float32).eps)

WEIGHTS = [
    ("wq", 128, 2 * C), ("wkv", 128, 2 * 2 * C), ("wm1", 128, 2 * HID), ("wm2", 65, HEADS),
    ("wproj", 128, 2 * C), ("bm1", 64, 1), ("bm2", 16, 1), ("wfc", 128, 2 * FF), ("wcp", 128, 8 * C), ("enc", 128, 2 * ENC),
    ("s2c", 128, 4 * MOE), ("rw1", 64, 64), ("rw2", 65, NE), ("ew1", 65, NE * EH),
    ("ew2", 128, 2 * NE * MOE), ("eb2", 16, MOE), ("c2s", 64, ENC), ("dec", 128, 4 * C), ("decb", 1, C),
    ("encb", 128, 4), ("s2cb", 64, 1), ("rb1", 64, 1), ("c2sb", 128, 4),
]
CONSTS = [
    ("ident", 128, 128), ("headblk", 128, 128), ("later", 128, 128), ("eye32", 128, CH), ("pair", 128, 2),
    ("selP", 16, 2 * 128), ("tie", 128, NE * NE), ("inchunk", 16, BLK),
    ("neghalf", 128, NT), ("chunk", 128, CT), ("ones", 1, 128), ("expert", 16, NE),
]
SETUP = [("wmod", 128, 2 * 6 * C), ("lng", 128, C), ("lnb", 128, C), ("cT", 128, 2 * BATCH)]


def offsets(table):
    out, at = {}, 0
    for name, parts, cols in table:
        out[name] = (at, parts, cols)
        at += cols
    return out, at


WOFF, WCOLS = offsets(WEIGHTS)
COFF, CCOLS = offsets(CONSTS)
SOFF, SCOLS = offsets(SETUP)

G_PE = ["xT0", "xT1", "m1", "q0", "q1", "kv0", "kv1", "kv2", "kv3", "zf", "zt", "kT0", "kT1", "P0", "P1",
        "dk0", "dk1", "dk2", "dk3", "scores", "U0", "U1", "Y0", "Y1", "Y2", "Y3",
        "proj0", "proj1", "y2a", "y2b"]
G_ACT = ["hT0", "hT1", "m1s", "q0", "q1", "gf", "gt", "kT0", "kT1", "Vm0", "Vm1", "Ae0", "Vm2", "Vm3", "Ae1", "Ae2", "Ae3", "yT0", "yT1",
         "y2T0", "y2T1", "sq"]
G_DVE = ["stats", "mv", "xn", "kv0", "kv1", "kv2", "kv3", "df", "dt", "d0", "d1", "P", "pend", "qP",
         "D0", "D1", "D2", "D3", "A0", "A1", "A2", "A3"] \
    + [f"S{c}" for c in range(2 * NC)] + ["y2a", "y2b"]
G_POOL = ["var", "rstd", "Qx", "B0", "B1", "B2", "B3", "G0", "G1", "G2", "G3", "Ks0", "Ks1", "Ks2", "Ks3",
          "Vx0", "Sm0", "Vx1", "Sm1", "Vx2", "Sm2", "Sm3", "Vx3"]
F_PE = [f"fc{m}" for m in range(8)] + [f"cp{i}" for i in range(4)] + ["hT0", "hT1"] \
    + [f"enc{m}" for m in range(4)] + ["s2c", "r1", "r2", "cT"] \
    + ["sp0"] + [s for e in range(NE) for s in ([f"sp{e + 1}"] if e < NE - 1 else []) + [f"e1_{2 * e}", f"e1_{2 * e + 1}"]
                 + ([f"e2_{e - 1}"] if e else [])] \
    + [f"e2_{NE - 1}"] + [f"c2s{m}" for m in range(4)] + [f"dec{i}" for i in range(4)]
F_ACT = [f"relu{m}" for m in range(8)] + ["hT0", "hT1"] + [f"enc{m}" for m in range(4)] \
    + ["cont", "rh", "w1", "cT"] + [f"eh{m}" for m in range(16)] + ["mT"] + [f"ra{m}" for m in range(4)] \
    + [f"dec{i}" for i in range(4)]
F_DVE = ["ms", "r2"] + [f"sq{m}" for m in range(8)] + [f"t{i}" for i in range(4)] \
    + ["tg", "x1", "stats", "mv", "xn", "L", "gt", "eq", "eqm", "rank4", "rank", "top1", "top2", "l1", "l2m", "l2", "diff",
       "w2", "c1", "c2", "comb", "chi", "clo"] + [f"ce{e}" for e in range(NE)] + ["stats3", "mv3", "dn", "g3", "out"]
F_POOL = ["var", "rstd", "x1b", "var3", "rstd3"]


def done(steps, n, name):
    return n * len(steps) + steps.index(name) + 1


def build(nc, x, w_d, c_d, s_d, out):
    f32, f32r = mybir.dt.float32, mybir.dt.float32r
    ALU, ACT, AX = mybir.AluOpType, mybir.ActivationFunctionType, mybir.AxisListType
    ctx = ExitStack()
    with ctx:
        def sb(name, shape):
            return ctx.enter_context(nc.sbuf_tensor(name, shape, f32))

        def sem(name):
            return ctx.enter_context(nc.semaphore(name))

        W = sb("W", [P, WCOLS])
        K = sb("K", [P, CCOLS])

        def w(name):
            at, parts, cols = WOFF[name]
            return W[0:parts, at:at + cols]

        def k(name):
            at, parts, cols = COFF[name]
            return K[0:parts, at:at + cols]

        wq = w("wq").rearrange("p (k m) -> p k m", k=2)
        wkv = w("wkv").rearrange("p (k m) -> p k m", k=2)
        wm1 = w("wm1").rearrange("p (k m) -> p k m", k=2)
        wproj = w("wproj").rearrange("p (k m) -> p k m", k=2)
        wfc = w("wfc").rearrange("p (k m) -> p k m", k=2)
        wcp = w("wcp").rearrange("p (k m) -> p k m", k=8)
        wenc = w("enc").rearrange("p (k m) -> p k m", k=2)
        ws2c = w("s2c").rearrange("p (k m) -> p k m", k=4)
        we1 = w("ew1").rearrange("p (e m) -> p e m", e=NE)
        we2 = w("ew2").rearrange("p (k e m) -> p k e m", k=2, e=NE)
        wdec = w("dec").rearrange("p (k m) -> p k m", k=4)
        ident = k("ident")
        selP = k("selP").rearrange("p (a m) -> p a m", a=2)

        modT = sb("modT", [P, 12, BATCH])
        ga = [sb(f"ga{b}", [P, C]) for b in range(BATCH)]
        gscale = [sb(f"gscale{b}", [P, C]) for b in range(BATCH)]
        gshift = [sb(f"gshift{b}", [P, C]) for b in range(BATCH)]

        xin = [sb(f"xin{i}", [P, NT, C]) for i in range(2)]
        stat = sb("stat", [P, NT, 6])
        mv = sb("mv", [P, NT, 2])
        rstd = sb("rstd", [P, NT])
        m1s = sb("m1s", [65, BLK])
        qs = sb("qs", [P, 2, BLK])
        Qx = sb("Qx", [P, 2, 2, BLK])
        kv = sb("kv", [P, NT, 2 * C])
        kT = sb("kT", [P, 2, BLK])
        xn = Qx[:, 0, :, :].rearrange("p a (b c) -> p (a b) c", c=C)
        hT = kT
        gf = sb("gf", [16, BLK])
        df = gf
        pm = sb("pm", [16, 2, BLK])
        Pf = pm[:, 1, :]
        gt = sb("gt", [P, NT, HEADS])
        dt = sb("dt", [P, NT, HEADS])
        pend = sb("pend", [P, 2, NC])
        BA = sb("BA", [P, NT, HEADS, CH])
        D = sb("D", [P, NT, HEADS, CH])
        S = sb("S", [P, NC, 2, P])
        carry = [sb(f"carry{b}", [P, 2, P]) for b in range(BATCH)]
        Vx = sb("Vx", [P, 2, 8 * (P + HD)])
        vx_diag = Vx[:, :, :].rearrange("p a (h m) -> p a h m", h=8)[:, :, :, 0:HD]
        Aexp = sb("Aexp", [P, HEADS, P])
        Vm = [sb(f"Vm{i}", [P, CT, C]) for i in range(2)]
        y2T = sb("y2T", [P, 2, BLK])
        y2 = sb("y2", [P, NT, C])
        Ks = y2
        sumsq = sb("sumsq", [P, NT])

        ms = sb("ms", [P, NT])
        r2 = sb("r2", [P, NT])
        R = sb("R", [P, 8, BLK])
        x1 = sb("x1", [P, NT, C])
        stat2 = sb("stat2", [P, NT, 6])
        mv2 = sb("mv2", [P, NT, 2])
        rstd2 = sb("rstd2", [P, NT])
        xn2 = sb("xn2", [P, NT, C])
        h2T = sb("h2T", [P, 2, BLK])
        cont = sb("cont", [65, BLK])
        rh = sb("rh", [65, BLK])
        L = sb("L", [P, NT, NE])
        cmp = sb("cmp", [P, 2, NT, NE, NE])
        idle = sb("idle", [P, 16])
        rank = sb("rank", [P, NT, NE])
        top = sb("top", [P, 2, NT, NE])
        sc = sb("sc", [P, 6, NT])
        lm = sb("lm", [P, NT, NE])
        comb = sb("comb", [P, NT, NE])
        parts16 = sb("parts16", [P, NT, 2, NE])
        sel16 = sb("sel16", [16, NE])
        cTr = sb("cTr", [16, BLK])
        cT = cTr[:, :]
        ce = h2T
        mT = rh[0:MOE, :]
        dec = xn2
        res = x1

        pg_all = ctx.enter_context(nc.psum_tensor("pg", [P, 4, BLK], f32))
        pg = [pg_all[:, i, :] for i in range(4)]
        pf = [ctx.enter_context(nc.psum_tensor(f"pf{i}", [P, BLK], f32)) for i in range(4)]

        const_loaded, gla_loaded, ffn_loaded = sem("const_loaded"), sem("gla_loaded"), sem("ffn_loaded")
        mod_loaded = sem("mod_loaded")
        x_loaded = [sem(f"x_loaded{i}") for i in range(2)]
        stored = sem("stored")
        zeroed = sem("zeroed")
        setup_act, setup_dve, setup_pe = sem("setup_act"), sem("setup_dve"), sem("setup_pe")
        g_pe, g_act, g_dve, g_pool = sem("g_pe"), sem("g_act"), sem("g_dve"), sem("g_pool")
        f_pe, f_act, f_dve, f_pool = sem("f_pe"), sem("f_act"), sem("f_dve"), sem("f_pool")
        SETUP_DVE = 30

        s_all = sb("s_all", [P, 8])
        wm_v = S[:, 0:12, :, :].rearrange("p a b c -> p (a b c)")
        wmod = wm_v.rearrange("p (k m) -> p k m", k=2)
        lng = S[:, 12, :, :].rearrange("p a b -> p (a b)")
        lnb = S[:, 13, :, :].rearrange("p a b -> p (a b)")
        cTs = s_all[:, 0:4]
        silu = s_all[:, 4:8]
        silu_bc = BA[:, 0, :, :].rearrange("p a b -> p (a b)").rearrange("p (k b m) -> p k b m", k=2, b=2)

        ORDER = ["F1", "F2", "G0", "F3a", "G1", "F3b", "G2", "F4", "G3", "F5", "G5", "F6", "G6a", "F7", "G6b", "F8",
                 "G7a", "F9", "G7b", "F10", "G7c", "X0", "G8", "X1", "X2", "G9", "X3", "X4", "GY0", "X5", "GY1", "X6",
                 "GY2", "X7", "GY3", "X8", "G13", "F20", "G14", "F21"]

        def steps(eng, emit):
            def step(ng, nf, pg_, pf_):
                for part in ORDER:
                    if part[0] == "G" and ng is not None:
                        emit(part, ng, pg_)
                    if part[0] != "G" and nf is not None:
                        emit(part, nf, pf_)
            step(0, None, 0, None)
            step(1, 0, 1, 0)
            with eng.Fori(0, NBLK // 2 - 1) as j:
                step(j * 2 + 2, j * 2 + 1, 0, 1)
                step(j * 2 + 3, j * 2 + 2, 1, 0)
            step(None, NBLK - 1, None, 1)

        carried = [0]

        def carry_wait(eng):
            if eng is nc.tensor:
                nc.tensor.ldweights(K[:, 0:64].bitcast(mybir.dt.bfloat16), tile_position=(0, 0))
            elif eng is nc.vector:
                nc.vector.memset(idle[:, 0:1], 0.0)
            else:
                carried[0] = carried[0] % 15 + 1
                nc.gpsimd.tensor_tensor(idle[:, carried[0]:carried[0] + 1], K[:, 0:1], K[:, 0:1], ALU.add)

        def first(n):
            return isinstance(n, int) and n == 0

        def x_count(n, b):
            return (n // 2 + 1) * 16 if isinstance(n, int) else (n - b) * 8 + 16

        block = ctx.enter_context(nc.Block())

        @block.sync
        def _(sp):
            xv = x.rearrange("b (t i p) c -> b t p i c", p=P, i=NT)
            ov = out.rearrange("b (t i p) c -> b t p i c", p=P, i=NT)

            def load_x(t, b):
                sp.dma_start(xin[b][:, :, :], xv[b, t, :, :, :]).then_inc(x_loaded[b], 16)

            def store(n, t, b):
                sp.wait_ge(f_dve, done(F_DVE, n, "out"))
                sp.dma_start(ov[b, t, :, :, :], res[:, :, :]).then_inc(stored, 16)

            sp.dma_start(s_all[:, 0:4], s_d[:, SOFF["cT"][0]:SOFF["cT"][0] + 4]).then_inc(mod_loaded, 16)
            sp.dma_start(wm_v, s_d[:, 0:12 * C]).then_inc(mod_loaded, 16)
            sp.dma_start(S[:, 12:14, :, :].rearrange("p a b c -> p (a b c)"), s_d[:, 12 * C:14 * C]).then_inc(mod_loaded, 16)
            load_x(0, 0)
            sp.dma_start(K[:, :], c_d).then_inc(const_loaded, 16)
            cut = WOFF["wfc"][0]
            sp.dma_start(W[:, 0:cut], w_d[:, 0:cut]).then_inc(gla_loaded, 16)
            sp.dma_start(W[:, cut:WCOLS], w_d[:, cut:WCOLS]).then_inc(ffn_loaded, 16)
            load_x(0, 1)
            with sp.Fori(0, SEQ // BLK - 1) as t:
                for b in range(BATCH):
                    sp.wait_ge(f_dve, done(F_DVE, t * 2 + b, "x1"))
                    load_x(t + 1, b)
                    store(t * 2 + b, t, b)
            for b in range(BATCH):
                store(NBLK - 2 + b, SEQ // BLK - 1, b)
            sp.wait_ge(stored, 16 * NBLK)

        @block.tensor
        def _(pe):
            mm = nc.tensor.matmul

            def tr(out_, in_):
                return nc.tensor.transpose(out_, in_, ident[0:in_.shape[0], 0:in_.shape[0]])

            pe.wait_ge(mod_loaded, 48)
            pe.wait_ge(setup_dve, 2)
            for m in range(12):
                for kk in range(2):
                    last = mm(pg[0][:, 2 * m:2 * m + 2], wmod[:, kk, m * P:(m + 1) * P], silu[:, 2 * kk:2 * kk + 2],
                              start=(kk == 0), stop=(kk == 1))
            last.then_inc(setup_pe, 1)
            for b in range(BATCH):
                for a, which in enumerate((2, 5)):
                    for kk in range(2):
                        last = mm(pg[1 + b][:, a * C:(a + 1) * C], silu_bc[:, kk, b, :],
                                  wmod[:, kk, which * C:(which + 1) * C], start=(kk == 0), stop=(kk == 1))
            last.then_inc(setup_pe, 1)
            pe.wait_ge(const_loaded, 16)
            pe.wait_ge(gla_loaded, 16)
            pe.wait_ge(setup_dve, SETUP_DVE)

            def before(n, sem_, table, name):
                if not first(n):
                    pe.wait_ge(sem_, done(table, n - 1, name))

            def emit(part, n, b):
                if part == "G1":
                    pe.wait_ge(g_dve, done(G_DVE, n, "xn"))
                    before(n, g_dve, G_DVE, "y2b")
                    for h in range(2):
                        for i in range(NT):
                            last = tr(pg[h][:, i * P:(i + 1) * P], xn[:, i, h * P:(h + 1) * P])
                        last.then_inc(g_pe, 1)
                if part == "G2":
                    pe.wait_ge(g_act, done(G_ACT, n, "hT1"))
                    for kk in range(2):
                        last = mm(pg[2][0:HID, :], wm1[:, kk, :], hT[:, kk, :], start=(kk == 0), stop=(kk == 1))
                    last.then_inc(g_pe, 1)
                    for h, bank in ((0, 3), (1, 0)):
                        for kk in range(2):
                            last = mm(pg[bank][:, :], wq[:, kk, h * P:(h + 1) * P], hT[:, kk, :],
                                      start=(kk == 0), stop=(kk == 1))
                        last.then_inc(g_pe, 1)
                    for i, bank, freed in ((0, 1, None), (1, 2, "m1s"), (2, 3, "q0"), (3, 0, "q1")):
                        if freed:
                            pe.wait_ge(g_act, done(G_ACT, n, freed))
                        for kk in range(2):
                            last = mm(pg[bank][:, :], hT[:, kk, i * P:(i + 1) * P], wkv[:, kk, :],
                                      start=(kk == 0), stop=(kk == 1))
                        last.then_inc(g_pe, 1)
                if part == "G3":
                    pe.wait_ge(g_dve, done(G_DVE, n, "kv1"))
                    carry_wait(nc.tensor)
                    mm(pg[1][0:HEADS, :], w("wm2")[0:HID, :], m1s[0:HID, :], start=True, stop=True).then_inc(g_pe, 1)
                    for i in range(NT):
                        last = mm(pg[2][:, i * HEADS:(i + 1) * HEADS], m1s[:, i * P:(i + 1) * P], w("wm2"),
                                  start=True, stop=True)
                    last.then_inc(g_pe, 1)
                    pe.wait_ge(g_dve, done(G_DVE, n, "kv3"))
                    for h, bank in ((0, 3), (1, 0)):
                        for i in range(NT):
                            last = tr(pg[bank][:, i * P:(i + 1) * P], kv[:, i, h * P:(h + 1) * P])
                        last.then_inc(g_pe, 1)
                if part == "G5":
                    pe.wait_ge(g_dve, done(G_DVE, n, "P"))
                    pe.wait_ge(g_act, done(G_ACT, n, "gt"))
                    for h in range(2):
                        mm(pg[1 + h][:, :], selP[:, h, :], Pf[:, :], start=True, stop=True).then_inc(g_pe, 1)
                if part in ("G6a", "G6b"):
                    pe.wait_ge(g_act, done(G_ACT, n, "kT1"))
                    for i, bank in ((0, 3), (1, 0)) if part == "G6a" else ((2, 1), (3, 2)):
                        pe.wait_ge(g_pool, done(G_POOL, n, f"B{i}"))
                        if i == 2:
                            pe.wait_ge(g_dve, done(G_DVE, n, "qP"))
                        mm(pg[bank][:, :], k("later"), BA[:, i, :, :].rearrange("p h t -> p (h t)"),
                           start=True, stop=True).then_inc(g_pe, 1)
                if part in ("G7a", "G7b", "G7c"):
                    if part == "G7a":
                        pe.wait_ge(g_pool, done(G_POOL, n, "Qx"))
                        pe.wait_ge(g_dve, done(G_DVE, n, "D3"))
                        carry_wait(nc.tensor)
                    for ih in {"G7a": range(0, 5), "G7b": range(5, 7), "G7c": range(7, 8)}[part]:
                        i, h = ih // 2, ih % 2
                        for c in range(CT):
                            t0 = i * P + c * CH
                            for r in range(4):
                                last = mm(pg[r][c * CH:(c + 1) * CH, i * P + h * 64:i * P + h * 64 + 64],
                                          kT[32 * r:32 * r + 32, h, t0:t0 + CH],
                                          Qx[32 * r:32 * r + 32, h, :, t0:t0 + CH], start=True, stop=True)
                    if part == "G7c":
                        last.then_inc(g_pe, 1)
                if part in ("G8", "G9"):
                    u = int(part == "G9")
                    pe.wait_ge(g_pool, done(G_POOL, n, f"Ks{2 * u + 1}"))
                    pe.wait_ge(g_dve, done(G_DVE, n, f"S{NC - 1}" if u else "A3"))
                    for ii in range(2):
                        i = 2 * u + ii
                        pe.wait_ge(g_act, done(G_ACT, n, f"Vm{i}"))
                        for h in range(2):
                            last = mm(pg[2 * ii + h][:, :], Ks[:, i, h * P:(h + 1) * P], Vm[ii][:, :, h * P:(h + 1) * P],
                                      start=True, stop=True)
                    last.then_inc(g_pe, 1)
                if part[0:2] == "GY":
                    i = int(part[2])
                    if i == 0:
                        pe.wait_ge(g_dve, done(G_DVE, n, f"S{2 * NC - 1}"))
                    pe.wait_ge(g_pool, done(G_POOL, n, ("Sm0", "Sm1", "Sm2", "Vx3")[i]))
                    pe.wait_ge(g_act, done(G_ACT, n, f"Ae{i}"))
                    for h in range(2):
                        for c in range(CT):
                            t0 = i * P + c * CH
                            mm(pg[h][:, t0:t0 + CH], S[:, i * CT + c, h, :], qs[:, h, t0:t0 + CH],
                               start=(c == 0), stop=False, skip_group_check=True)
                        for a in range(8 * h, 8 * h + 8):
                            last = mm(pg[h][:, i * P:(i + 1) * P], Vx[:, h, (a % 8) * P:(a % 8 + 1) * P], Aexp[:, a, :],
                                      start=False, stop=(a == 8 * h + 7), skip_group_check=True)
                    last.then_inc(g_pe, 1)
                if part == "G13":
                    pe.wait_ge(g_act, done(G_ACT, n, "yT1"))
                    for h in range(2):
                        for kk in range(2):
                            last = mm(pg[2 + h][:, :], wproj[:, kk, h * P:(h + 1) * P], hT[:, kk, :],
                                      start=(kk == 0), stop=(kk == 1))
                        last.then_inc(g_pe, 1)
                if part == "G14":
                    pe.wait_ge(g_act, done(G_ACT, n, "y2T1"))
                    for i in range(NT):
                        for h in range(2):
                            last = tr(pg[i // 2][:, (i % 2) * C + h * P:(i % 2) * C + (h + 1) * P],
                                      y2T[:, h, i * P:(i + 1) * P])
                        if i % 2:
                            last.then_inc(g_pe, 1)
                if part in ("F1", "F2"):
                    if part == "F1":
                        if first(n):
                            pe.wait_ge(ffn_loaded, 16)
                        pe.wait_ge(g_act, done(G_ACT, n, "y2T1"))
                    for m in (range(4) if part == "F1" else range(4, 8)):
                        if m >= 4:
                            pe.wait_ge(f_act, done(F_ACT, n, f"relu{m - 4}"))
                        else:
                            before(n, f_act, F_ACT, f"dec{m}")
                        for kk in range(2):
                            last = mm(pf[(1 + m) % 4][:, :], wfc[:, kk, m * P:(m + 1) * P], y2T[:, kk, :],
                                      start=(kk == 0), stop=(kk == 1))
                        last.then_inc(f_pe, 1)
                if part in ("F3a", "F3b"):
                    for i in (0, 1) if part == "F3a" else (2, 3):
                        pe.wait_ge(f_act, done(F_ACT, n, f"relu{4 + i}"))
                        for kk in range(8):
                            if i == 0:
                                pe.wait_ge(f_dve, done(F_DVE, n, f"sq{kk}"))
                            last = mm(pf[(1 + i) % 4][:, 0:C], R[:, kk, i * P:(i + 1) * P], wcp[:, kk, :],
                                      start=(kk == 0), stop=(kk == 7))
                        last.then_inc(f_pe, 1)
                if part == "F4":
                    pe.wait_ge(f_dve, done(F_DVE, n, "xn"))
                    for h in range(2):
                        for i in range(NT):
                            last = tr(pf[h][:, i * P:(i + 1) * P], xn2[:, i, h * P:(h + 1) * P])
                        last.then_inc(f_pe, 1)
                if part == "F5":
                    pe.wait_ge(f_act, done(F_ACT, n, "hT1"))
                    for m in range(4):
                        for kk in range(2):
                            last = mm(pf[(2 + m) % 4][:, :], wenc[:, kk, m * P:(m + 1) * P], h2T[:, kk, :],
                                      start=(kk == 0), stop=(kk == 1))
                        last.then_inc(f_pe, 1)
                if part == "F6":
                    for kk in range(4):
                        pe.wait_ge(f_act, done(F_ACT, n, f"enc{kk}"))
                        last = mm(pf[2][0:MOE, :], ws2c[:, kk, :], R[:, kk, :], start=(kk == 0), stop=(kk == 3))
                    last.then_inc(f_pe, 1)
                if part == "F7":
                    pe.wait_ge(f_act, done(F_ACT, n, "cont"))
                    carry_wait(nc.tensor)
                    mm(pf[3][0:64, :], w("rw1"), cont[0:64, :], start=True, stop=True).then_inc(f_pe, 1)
                if part == "F8":
                    pe.wait_ge(f_act, done(F_ACT, n, "rh"))
                    for i in range(NT):
                        last = mm(pf[0][:, i * NE:(i + 1) * NE], rh[:, i * P:(i + 1) * P], w("rw2"),
                                  start=True, stop=True)
                    last.then_inc(f_pe, 1)
                if part == "F9":
                    pe.wait_ge(f_dve, done(F_DVE, n, "clo"))
                    for i in range(NT):
                        last = tr(pf[1][0:2 * NE, i * P:(i + 1) * P], parts16[:, i, :, :].rearrange("p a e -> p (a e)"))
                    last.then_inc(f_pe, 1)

                def spread(e):
                    if e:
                        pe.wait_ge(f_dve, done(F_DVE, n, f"ce{e - 1}"))
                    mm(pf[0][:, :], sel16[:, e:e + 1].to_broadcast([16, P]).bitcast(f32r), cT.bitcast(f32r),
                       start=True, stop=True).then_inc(f_pe, 1)

                def second(e):
                    for m in range(2):
                        pe.wait_ge(f_act, done(F_ACT, n, f"eh{2 * e + m}"))
                        last = mm(pf[3][0:MOE, :], we2[:, m, e, :], R[:, 4 + (2 * e + m) % 4, :],
                                  start=(e == 0 and m == 0), stop=False)
                    return last

                if part == "F10":
                    pe.wait_ge(f_act, done(F_ACT, n, "cT"))
                    spread(0)
                if part[0] == "X":
                    e = int(part[1:])
                    if e < NE - 1:
                        spread(e + 1)
                    if e < NE:
                        pe.wait_ge(f_dve, done(F_DVE, n, f"ce{e}"))
                        for m in range(2):
                            if e:
                                pe.wait_ge(f_act, done(F_ACT, n, f"eh{2 * e - 2 + m}"))
                            mm(pf[1 + m][:, :], we1[:, e, m * P:(m + 1) * P], ce[0:65, e % 2, :],
                               start=True, stop=True).then_inc(f_pe, 1)
                    if e:
                        last = second(e - 1)
                        if e < NE:
                            last.then_inc(f_pe, 1)
                    if e == NE:
                        mm(pf[3][0:MOE, :], w("eb2"), cT, start=False, stop=True).then_inc(f_pe, 1)
                if part == "F20":
                    pe.wait_ge(f_act, done(F_ACT, n, "mT"))
                    for m in range(4):
                        mm(pf[(1 + m) % 4][:, :], w("c2s")[:, m * P:(m + 1) * P], mT,
                           start=True, stop=True).then_inc(f_pe, 1)
                if part == "F21":
                    for i in range(NT):
                        for kk in range(4):
                            if i == 0:
                                pe.wait_ge(f_act, done(F_ACT, n, f"ra{kk}"))
                            mm(pf[(1 + i) % 4][:, 0:C], R[:, kk, i * P:(i + 1) * P], wdec[:, kk, :],
                               start=(kk == 0), stop=False)
                        mm(pf[(1 + i) % 4][:, 0:C], k("ones"), w("decb"), start=False, stop=True).then_inc(f_pe, 1)

            steps(pe, emit)

        @block.scalar
        def _(act):
            A = nc.scalar.activation
            act.wait_ge(mod_loaded, 48)
            A(silu, cTs, ACT.Sigmoid).then_inc(setup_act, 1)
            act.wait_ge(const_loaded, 16)
            act.wait_ge(gla_loaded, 16)
            act.wait_ge(setup_dve, SETUP_DVE)

            def before(n, sem_, table, name):
                if not first(n):
                    act.wait_ge(sem_, done(table, n - 1, name))

            def mask_v(n, i):
                for c in range(CT):
                    last = A(Vm[i % 2][:, c, :], kv[:, i, C:2 * C], ACT.Copy, scale=k("chunk")[:, c:c + 1])
                last.then_inc(g_act, 1)

            def expand(n, i):
                act.wait_ge(g_dve, done(G_DVE, n, f"A{i}"))
                for c in range(CT):
                    last = A(Aexp[:, :, c * CH:(c + 1) * CH], BA[:, i, :, :], ACT.Copy, scale=k("chunk")[:, c:c + 1])
                last.then_inc(g_act, 1)

            def emit(part, n, b):
                if part == "G1":
                    before(n, g_pe, G_PE, "proj1")
                    before(n, g_act, G_ACT, "sq")
                    for h in range(2):
                        act.wait_ge(g_pe, done(G_PE, n, f"xT{h}"))
                        A(hT[:, h, :], pg[h][:, :], ACT.Identity, scale=modT[:, 2 + h, b:b + 1],
                          bias=modT[:, h, b:b + 1]).then_inc(g_act, 1)
                if part == "G2":
                    act.wait_ge(g_pe, done(G_PE, n, "m1"))
                    A(m1s[0:HID, :], pg[2][0:HID, :], ACT.Relu, bias=w("bm1")).then_inc(g_act, 1)
                    for h, bank in ((0, 3), (1, 0)):
                        act.wait_ge(g_pe, done(G_PE, n, f"q{h}"))
                        A(qs[:, h, :], pg[bank][:, :], ACT.Copy).then_inc(g_act, 1)
                if part == "G3":
                    act.wait_ge(g_pe, done(G_PE, n, "zf"))
                    A(gf[:, :], pg[1][0:HEADS, :], ACT.Sigmoid, bias=w("bm2")).then_inc(g_act, 1)
                    act.wait_ge(g_pe, done(G_PE, n, "zt"))
                    A(gt[:, :, :].rearrange("p i h -> p (i h)"), pg[2][:, 0:NT * HEADS], ACT.Sigmoid).then_inc(g_act, 1)
                    for h, bank in ((0, 3), (1, 0)):
                        act.wait_ge(g_pe, done(G_PE, n, f"kT{h}"))
                        A(kT[:, h, :], pg[bank][:, :], ACT.Copy).then_inc(g_act, 1)
                    act.wait_ge(g_dve, done(G_DVE, n, "kv3"))
                    before(n, g_pe, G_PE, "U1")
                    mask_v(n, 0)
                    mask_v(n, 1)
                if part == "G8":
                    before(n, g_pe, G_PE, "Y3")
                    expand(n, 0)
                    act.wait_ge(g_pe, done(G_PE, n, "U0"))
                    mask_v(n, 2)
                    mask_v(n, 3)
                if part in ("GY0", "GY1", "GY2"):
                    act.wait_ge(g_pe, done(G_PE, n, f"Y{part[2]}"))
                    expand(n, int(part[2]) + 1)
                if part == "GY3":
                    act.wait_ge(g_pe, done(G_PE, n, "Y3"))
                    for h in range(2):
                        A(hT[:, h, :], pg[h][:, :], ACT.Copy).then_inc(g_act, 1)
                if part == "G13":
                    before(n, f_pe, F_PE, "fc7")
                    for h in range(2):
                        act.wait_ge(g_pe, done(G_PE, n, f"proj{h}"))
                        A(y2T[:, h, :], pg[2 + h][:, :], ACT.Copy).then_inc(g_act, 1)
                if part == "G14":
                    act.wait_ge(g_dve, done(G_DVE, n, "y2b"))
                    before(n, f_dve, F_DVE, "ms")
                    act.wait_ge(g_pe, done(G_PE, n, "proj1"))
                    for i in range(NT):
                        last = A(hT[:, i // 2, (i % 2) * C:(i % 2 + 1) * C], y2[:, i, :], ACT.Square,
                                 accum_out=sumsq[:, i:i + 1])
                    last.then_inc(g_act, 1)
                if part in ("F1", "F2"):
                    if part == "F1":
                        if first(n):
                            act.wait_ge(ffn_loaded, 16)
                        before(n, f_pe, F_PE, "dec3")
                    for m in (range(4) if part == "F1" else range(4, 8)):
                        act.wait_ge(f_pe, done(F_PE, n, f"fc{m}"))
                        A(R[:, m, :], pf[(1 + m) % 4][:, :], ACT.Relu).then_inc(f_act, 1)
                if part == "F4":
                    for h in range(2):
                        act.wait_ge(f_pe, done(F_PE, n, f"hT{h}"))
                        A(h2T[:, h, :], pf[h][:, :], ACT.Identity, scale=modT[:, 8 + h, b:b + 1],
                          bias=modT[:, 6 + h, b:b + 1]).then_inc(f_act, 1)
                if part == "F5":
                    for m in range(4):
                        act.wait_ge(f_pe, done(F_PE, n, f"enc{m}"))
                        A(R[:, m, :], pf[(2 + m) % 4][:, :], ACT.Sigmoid, bias=w("encb")[:, m:m + 1]).then_inc(f_act, 1)
                if part == "F6":
                    act.wait_ge(f_pe, done(F_PE, n, "s2c"))
                    A(cont[0:MOE, :], pf[2][0:MOE, :], ACT.Identity, bias=w("s2cb")).then_inc(f_act, 1)
                if part == "F7":
                    act.wait_ge(f_pe, done(F_PE, n, "r1"))
                    A(rh[0:64, :], pf[3][0:64, :], ACT.Relu, bias=w("rb1")).then_inc(f_act, 1)
                if part == "F8":
                    act.wait_ge(f_dve, done(F_DVE, n, "diff"))
                    A(sc[:, 3, :], sc[:, 2, :], ACT.Sigmoid).then_inc(f_act, 1)
                if part == "F9":
                    act.wait_ge(f_pe, done(F_PE, n, "cT"))
                    A(cT.bitcast(f32r), pf[1][0:2 * NE, :], ACT.Copy).then_inc(f_act, 1)
                if part[0] == "X" and int(part[1:]) < NE:
                    e = int(part[1:])
                    for m in (2 * e, 2 * e + 1):
                        act.wait_ge(f_pe, done(F_PE, n, f"e1_{m}"))
                        if e >= 2:
                            act.wait_ge(f_pe, done(F_PE, n, f"e2_{e - 2}"))
                        A(R[:, 4 + m % 4, :], pf[1 + m % 2][:, :], ACT.Relu).then_inc(f_act, 1)
                if part == "X8":
                    act.wait_ge(f_pe, done(F_PE, n, f"e2_{NE - 1}"))
                    A(mT, pf[3][0:MOE, :], ACT.Copy).then_inc(f_act, 1)
                if part == "F20":
                    for m in range(4):
                        act.wait_ge(f_pe, done(F_PE, n, f"c2s{m}"))
                        A(R[:, m, :], pf[(1 + m) % 4][:, :], ACT.Sigmoid, bias=w("c2sb")[:, m:m + 1]).then_inc(f_act, 1)
                if part == "F21":
                    for i in range(NT):
                        act.wait_ge(f_pe, done(F_PE, n, f"dec{i}"))
                        A(dec[:, i, :], pf[(1 + i) % 4][:, 0:C], ACT.Sigmoid).then_inc(f_act, 1)

            steps(act, emit)

        @block.vector
        def _(dve):
            V = nc.vector
            made = [0]

            def setup(ins):
                made[0] += 1
                ins.then_inc(setup_dve, 1)
                dve.wait_ge(setup_dve, made[0])

            dve.wait_ge(setup_act, 1)
            setup(V.tensor_tensor(silu, cTs, silu, ALU.mult))
            setup(V.tensor_copy(silu_bc, silu.rearrange("p (k b) -> p k b", k=2).unsqueeze(3).to_broadcast([P, 2, 2, P])))
            dve.wait_ge(setup_pe, 1)
            setup(V.tensor_copy(modT[:, :, :].rearrange("p m b -> p (m b)"), pg[0][:, 0:24]))
            for m in (2, 8):
                setup(V.tensor_scalar(modT[:, m:m + 2, :], modT[:, m:m + 2, :], 1.0, None, ALU.add))
            dve.wait_ge(setup_pe, 2)
            for b in range(BATCH):
                raw, sgn, mag = (xn[:, a, :] for a in range(3))
                for a in range(2):
                    setup(V.tensor_copy(raw, pg[1 + b][:, a * C:(a + 1) * C]))
                    setup(V.tensor_scalar(sgn, raw, 0.0, 2.0, ALU.is_ge, ALU.mult))
                    setup(V.scalar_tensor_tensor(mag, sgn, -1.0, raw, ALU.add, ALU.mult))
                    setup(V.tensor_scalar(mag, mag, 0.25, None, ALU.max))
                    dst = ga[b] if a == 0 else gshift[b]
                    setup(V.scalar_tensor_tensor(dst[:, :], sgn, -1.0, mag, ALU.add, ALU.mult))
                setup(V.tensor_tensor(gscale[b][:, :], gshift[b][:, :], lng, ALU.mult))
                setup(V.tensor_tensor(gshift[b][:, :], gshift[b][:, :], lnb, ALU.mult))
            dve.wait_ge(const_loaded, 16)
            V.tensor_copy(sel16[:, :].bitcast(f32r), k("expert"))
            for t_ in (m1s, cont, rh):
                V.memset(t_[64:65, :], 1.0)
            V.memset(carry[0][:, :, :].rearrange("p a b -> p (a b)"), 0.0)
            setup(V.memset(carry[1][:, :, :].rearrange("p a b -> p (a b)"), 0.0))
            assert made[0] == SETUP_DVE

            def before(n, sem_, table, name):
                if not first(n):
                    dve.wait_ge(sem_, done(table, n - 1, name))

            def mine(table, n, name):
                dve.wait_ge(g_dve if table is G_DVE else f_dve, done(table, n, name))

            def emit(part, n, b):
                if part == "G0":
                    dve.wait_ge(x_loaded[b], x_count(n, b))
                    for i in range(NT):
                        last = V.bn_stats(stat[:, i, :], xin[b][:, i, :])
                    last.then_inc(g_dve, 1)
                    dve.wait_ge(g_dve, done(G_DVE, n, "stats"))
                    carry_wait(nc.vector)
                    for i in range(NT):
                        last = V.bn_aggr(mv[:, i, :], stat[:, i, :])
                    last.then_inc(g_dve, 1)
                    mine(G_DVE, n, "mv")
                    dve.wait_ge(g_pool, done(G_POOL, n, "rstd"))
                    before(n, g_pe, G_PE, "scores")
                    for i in range(NT):
                        last = V.tensor_scalar(xn[:, i, :], xin[b][:, i, :], mv[:, i, 0:1], rstd[:, i:i + 1],
                                               ALU.subtract, ALU.mult)
                    last.then_inc(g_dve, 1)
                if part == "G2":
                    for i, bank in enumerate((1, 2, 3, 0)):
                        dve.wait_ge(g_pe, done(G_PE, n, f"kv{i}"))
                        V.tensor_copy(kv[:, i, :], pg[bank][:, :]).then_inc(g_dve, 1)
                if part == "G3":
                    dve.wait_ge(g_act, done(G_ACT, n, "gf"))
                    V.tensor_scalar(df[:, :], gf[:, :], -1.0, 1.0, ALU.mult, ALU.add).then_inc(g_dve, 1)
                    dve.wait_ge(g_act, done(G_ACT, n, "gt"))
                    V.tensor_scalar(dt[:, :, :].rearrange("p i h -> p (i h)"), gt[:, :, :].rearrange("p i h -> p (i h)"),
                                    -1.0, 1.0, ALU.mult, ALU.add).then_inc(g_dve, 1)
                    mine(G_DVE, n, "df")
                    V.tensor_tensor(pm[:, 0, :], df[:, :], k("inchunk"), ALU.mult).then_inc(g_dve, 1)
                    mine(G_DVE, n, "d0")
                    V.tensor_tensor(pm[:, 1, :], df[:, :], pm[:, 0, :], ALU.subtract).then_inc(g_dve, 1)
                    mine(G_DVE, n, "d1")
                    V.tensor_tensor_scan(Pf[:, :], pm[:, 0, :], pm[:, 1, :], 0.0, ALU.mult, ALU.add).then_inc(g_dve, 1)
                if part == "G5":
                    dve.wait_ge(g_pe, done(G_PE, n, "P1"))
                    for h in range(2):
                        last = V.tensor_copy(pend[:, h, :], pg[1 + h][:, CH - 1:BLK:CH])
                    last.then_inc(g_dve, 1)
                    dve.wait_ge(g_pool, done(G_POOL, n, "Qx"))
                    for h in range(2):
                        last = V.tensor_tensor(qs[:, h, :], qs[:, h, :], pg[1 + h][:, :], ALU.mult)
                    last.then_inc(g_dve, 1)
                if part in ("G6a", "G6b"):
                    for i, bank in ((0, 3), (1, 0)) if part == "G6a" else ((2, 1), (3, 2)):
                        dve.wait_ge(g_pe, done(G_PE, n, f"dk{i}"))
                        dve.wait_ge(g_pool, done(G_POOL, n, f"G{i}"))
                        d = D[:, i, :, :].rearrange("p h t -> p (h t)")
                        V.tensor_tensor_scan(d, pg[bank][:, :], d, 0.0, ALU.mult, ALU.add).then_inc(g_dve, 1)
                if part == "G7c":
                    dve.wait_ge(g_pe, done(G_PE, n, "scores"))
                    mine(G_DVE, n, "D3")
                    for i in range(NT):
                        V.tensor_tensor(BA[:, i, :, :].rearrange("p (a r b) t -> p r a (b t)", a=2, r=4),
                                        pg_all[:, :, i * P:(i + 1) * P].rearrange("p r (a m) -> p r a m", a=2),
                                        D[:, i, :, :].rearrange("p (a r b) t -> p r a (b t)", a=2, r=4),
                                        ALU.mult).then_inc(g_dve, 1)
                if part in ("G8", "G9"):
                    u = int(part == "G9")
                    dve.wait_ge(g_pe, done(G_PE, n, f"U{u}"))
                    if u == 1:
                        dve.wait_ge(g_pool, done(G_POOL, n, "Sm0"))
                    for c in range(NC // 2 * u, NC // 2 * (u + 1)):
                        ii, cc = (c // CT) % 2, c % CT
                        for h in range(2):
                            if c:
                                mine(G_DVE, n, f"S{2 * (c - 1) + h}")
                            src = S[:, c, h, :] if c else carry[b][:, h, :]
                            dst = S[:, c + 1, h, :] if c < NC - 1 else carry[b][:, h, :]
                            V.scalar_tensor_tensor(dst, src, pend[:, h, c:c + 1], pg[2 * ii + h][:, cc * P:(cc + 1) * P],
                                                   ALU.mult, ALU.add).then_inc(g_dve, 1)
                if part == "G14":
                    for a in range(2):
                        dve.wait_ge(g_pe, done(G_PE, n, f"y2{'ab'[a]}"))
                        V.tensor_copy(y2[:, 2 * a:2 * a + 2, :].rearrange("p i c -> p (i c)"), pg[a][:, :]).then_inc(g_dve, 1)
                if part == "F1":
                    dve.wait_ge(g_act, done(G_ACT, n, "sq"))
                    V.tensor_scalar(ms[:, :], sumsq[:, :], 1.0 / C, RMS_EPS, ALU.mult, ALU.add).then_inc(f_dve, 1)
                    mine(F_DVE, n, "ms")
                    V.reciprocal(r2[:, :], ms[:, :]).then_inc(f_dve, 1)
                if part in ("F1", "F2"):
                    for m in (range(4) if part == "F1" else range(4, 8)):
                        dve.wait_ge(f_act, done(F_ACT, n, f"relu{m}"))
                        V.tensor_tensor(R[:, m, :], R[:, m, :], R[:, m, :], ALU.mult).then_inc(f_dve, 1)
                if part == "F3b":
                    if not first(n):
                        dve.wait_ge(stored, n * 16)
                    for i in range(NT):
                        dve.wait_ge(f_pe, done(F_PE, n, f"cp{i}"))
                        V.scalar_tensor_tensor(x1[:, i, :], pf[(1 + i) % 4][:, 0:C], r2[:, i:i + 1], y2[:, i, :],
                                               ALU.mult, ALU.add).then_inc(f_dve, 1)
                    mine(F_DVE, n, "t3")
                    V.tensor_tensor(x1[:, :, :], x1[:, :, :], ga[b][:, :].unsqueeze(1).to_broadcast([P, NT, C]), ALU.mult).then_inc(f_dve, 1)
                    mine(F_DVE, n, "tg")
                    V.tensor_tensor(x1[:, :, :], x1[:, :, :], xin[b][:, :, :], ALU.add).then_inc(f_dve, 1)
                    mine(F_DVE, n, "x1")
                    for i in range(NT):
                        last = V.bn_stats(stat2[:, i, :], x1[:, i, :])
                    last.then_inc(f_dve, 1)
                    dve.wait_ge(f_dve, done(F_DVE, n, "stats"))
                    carry_wait(nc.vector)
                    for i in range(NT):
                        last = V.bn_aggr(mv2[:, i, :], stat2[:, i, :])
                    last.then_inc(f_dve, 1)
                    mine(F_DVE, n, "mv")
                    dve.wait_ge(f_pool, done(F_POOL, n, "rstd"))
                    for i in range(NT):
                        last = V.tensor_scalar(xn2[:, i, :], x1[:, i, :], mv2[:, i, 0:1], rstd2[:, i:i + 1],
                                               ALU.subtract, ALU.mult)
                    last.then_inc(f_dve, 1)
                if part == "F8":
                    dve.wait_ge(f_pe, done(F_PE, n, "r2"))
                    V.tensor_copy(L[:, :, :].rearrange("p i e -> p (i e)"), pf[0][:, 0:NT * NE]).then_inc(f_dve, 1)
                    mine(F_DVE, n, "L")
                    full = [P, NT, NE, NE]
                    le, lf = L[:, :, :].unsqueeze(3).to_broadcast(full), L[:, :, :].unsqueeze(2).to_broadcast(full)
                    tie = k("tie").rearrange("p (e f) -> p e f", e=NE).unsqueeze(1).to_broadcast(full)
                    V.tensor_tensor(cmp[:, 0], le, lf, ALU.is_lt).then_inc(f_dve, 1)
                    V.tensor_tensor(cmp[:, 1], le, lf, ALU.is_equal).then_inc(f_dve, 1)
                    mine(F_DVE, n, "eq")
                    V.tensor_tensor(cmp[:, 1], cmp[:, 1], tie, ALU.mult).then_inc(f_dve, 1)
                    mine(F_DVE, n, "eqm")
                    V.tensor_tensor(cmp[:, 0], cmp[:, 0], cmp[:, 1], ALU.add).then_inc(f_dve, 1)
                    mine(F_DVE, n, "rank4")
                    V.tensor_reduce(rank[:, :, :], cmp[:, 0], AX.X, ALU.add).then_inc(f_dve, 1)
                    mine(F_DVE, n, "rank")
                    for a in range(2):
                        V.tensor_scalar(top[:, a, :, :], rank[:, :, :], float(a), None, ALU.is_equal).then_inc(f_dve, 1)
                    V.tensor_reduce(sc[:, 0, :], L[:, :, :], AX.X, ALU.max).then_inc(f_dve, 1)
                    mine(F_DVE, n, "top2")
                    V.tensor_tensor(lm[:, :, :], L[:, :, :], top[:, 1, :, :], ALU.mult).then_inc(f_dve, 1)
                    mine(F_DVE, n, "l2m")
                    V.tensor_reduce(sc[:, 1, :], lm[:, :, :], AX.X, ALU.add).then_inc(f_dve, 1)
                    mine(F_DVE, n, "l2")
                    V.tensor_tensor(sc[:, 2, :], sc[:, 0, :], sc[:, 1, :], ALU.subtract).then_inc(f_dve, 1)
                    dve.wait_ge(f_act, done(F_ACT, n, "w1"))
                    V.tensor_scalar(sc[:, 4, :], sc[:, 3, :], -1.0, 1.0, ALU.mult, ALU.add).then_inc(f_dve, 1)
                    mine(F_DVE, n, "w2")
                    V.tensor_tensor(lm[:, :, :], top[:, 0, :, :], sc[:, 3, :].unsqueeze(2).to_broadcast([P, NT, NE]), ALU.mult).then_inc(f_dve, 1)
                    V.tensor_tensor(comb[:, :, :], top[:, 1, :, :], sc[:, 4, :].unsqueeze(2).to_broadcast([P, NT, NE]), ALU.mult).then_inc(f_dve, 1)
                    mine(F_DVE, n, "c2")
                    V.tensor_tensor(comb[:, :, :], comb[:, :, :], lm[:, :, :], ALU.add).then_inc(f_dve, 1)
                    mine(F_DVE, n, "comb")
                    V.tensor_copy(parts16[:, :, 0, :].bitcast(f32r), comb[:, :, :]).then_inc(f_dve, 1)
                    mine(F_DVE, n, "chi")
                    V.tensor_tensor(parts16[:, :, 1, :].bitcast(f32r), comb[:, :, :], parts16[:, :, 0, :], ALU.subtract).then_inc(f_dve, 1)
                if part[0] == "X" or part == "F10":
                    e = int(part[1:]) if part != "F10" else -1
                    for ee in [e + 1] if e < NE - 1 else []:
                        dve.wait_ge(f_pe, done(F_PE, n, f"sp{ee}"))
                        if ee >= 2:
                            dve.wait_ge(f_pe, done(F_PE, n, f"e1_{2 * (ee - 2) + 1}"))
                        V.tensor_tensor(ce[0:65, ee % 2, :], pf[0][0:65, :], cont[:, :], ALU.mult).then_inc(f_dve, 1)
                if part == "F21":
                    for i in range(NT):
                        dve.wait_ge(f_act, done(F_ACT, n, f"dec{i}"))
                        last = V.bn_stats(stat2[:, i, :], dec[:, i, :])
                    last.then_inc(f_dve, 1)
                    dve.wait_ge(f_dve, done(F_DVE, n, "stats3"))
                    carry_wait(nc.vector)
                    for i in range(NT):
                        last = V.bn_aggr(mv2[:, i, :], stat2[:, i, :])
                    last.then_inc(f_dve, 1)
                    mine(F_DVE, n, "mv3")
                    dve.wait_ge(f_pool, done(F_POOL, n, "rstd3"))
                    for i in range(NT):
                        last = V.tensor_scalar(dec[:, i, :], dec[:, i, :], mv2[:, i, 0:1], rstd2[:, i:i + 1],
                                               ALU.subtract, ALU.mult)
                    last.then_inc(f_dve, 1)
                    mine(F_DVE, n, "dn")
                    V.tensor_tensor(dec[:, :, :], dec[:, :, :], gscale[b][:, :].unsqueeze(1).to_broadcast([P, NT, C]), ALU.mult).then_inc(f_dve, 1)
                    mine(F_DVE, n, "g3")
                    V.tensor_tensor(res[:, :, :], dec[:, :, :], x1[:, :, :], ALU.add).then_inc(f_dve, 1)

            steps(dve, emit)

        @block.gpsimd
        def _(pool):
            G = nc.gpsimd
            G.memset(Vx[:, :, :].rearrange("p a b -> p (a b)"), 0.0).then_inc(zeroed, 1)
            pool.wait_ge(zeroed, 1)
            pool.wait_ge(const_loaded, 16)
            pool.wait_ge(setup_dve, SETUP_DVE)

            def before(n, sem_, table, name):
                if not first(n):
                    pool.wait_ge(sem_, done(table, n - 1, name))

            def rsqrt(mv_, out_, eps, table, sem_, n, a):
                G.tensor_scalar(out_[:, :], mv_[:, :, 1], eps, None, ALU.add).then_inc(sem_, 1)
                pool.wait_ge(sem_, done(table, n, a))
                G.tensor_tensor(out_[:, :], out_[:, :], k("neghalf"), ALU.pow).then_inc(sem_, 1)

            def spread_v(n, i):
                if i:
                    pool.wait_ge(g_pe, done(G_PE, n, f"Y{i - 1}"))
                else:
                    before(n, g_pe, G_PE, "Y3")
                carry_wait(nc.gpsimd)
                G.tensor_scalar(vx_diag, kv[:, i, C:2 * C].rearrange("p (a h d) -> p a h d", a=2, h=8), 1.0, 0.0,
                                ALU.mult, ALU.add).then_inc(g_pool, 1)

            def emit(part, n, b):
                if part == "G0":
                    pool.wait_ge(g_dve, done(G_DVE, n, "mv"))
                    carry_wait(nc.gpsimd)
                    rsqrt(mv, rstd, LN_EPS, G_POOL, g_pool, n, "var")
                if part == "G3":
                    pool.wait_ge(g_act, done(G_ACT, n, "q1"))
                    carry_wait(nc.gpsimd)
                    for h in range(2):
                        for a in range(2):
                            last = G.tensor_scalar(Qx[:, h, a, :], qs[:, h, :], k("pair")[:, a:a + 1], 0.0, ALU.mult, ALU.add)
                    last.then_inc(g_pool, 1)
                    full = [P, HEADS, CH]
                    eye = k("eye32").unsqueeze(1).to_broadcast(full)
                    pool.wait_ge(g_dve, done(G_DVE, n, "dt"))
                    before(n, g_act, G_ACT, "Ae3")
                    for i in range(NT):
                        G.tensor_tensor(BA[:, i, :, :], eye, dt[:, i, :].unsqueeze(2).to_broadcast(full), ALU.mult).then_inc(g_pool, 1)
                    for i in range(NT):
                        G.tensor_tensor(D[:, i, :, :], eye, gt[:, i, :].unsqueeze(2).to_broadcast(full), ALU.mult).then_inc(g_pool, 1)
                if part == "G6b":
                    before(n, f_dve, F_DVE, "t3")
                    for i in range(NT):
                        pool.wait_ge(g_dve, done(G_DVE, n, f"D{i}"))
                        full = [P, HEADS, HD]
                        G.tensor_tensor(Ks[:, i, :].rearrange("p (h d) -> p h d", h=HEADS),
                                        kv[:, i, 0:C].rearrange("p (h d) -> p h d", h=HEADS),
                                        D[:, i, :, CH - 1:CH].to_broadcast(full), ALU.mult).then_inc(g_pool, 1)
                def keep_blocks(i):
                    blk = k("headblk").unsqueeze(1)
                    lo = i * CT
                    if i == 0:
                        lo = 1
                        G.tensor_tensor(S[:, 0, :, :], carry[b][:, :, :], blk.to_broadcast([P, 2, P]), ALU.mult)
                    pool.wait_ge(g_dve, done(G_DVE, n, f"S{2 * CT * i + 2 * CT - 1}"))
                    hi = (i + 1) * CT
                    v = S[:, lo:hi, :, :].rearrange("p c h m -> p (c h) m")
                    G.tensor_tensor(v, v, blk.to_broadcast([P, 2 * (hi - lo), P]), ALU.mult).then_inc(g_pool, 1)

                if part == "G8":
                    spread_v(n, 0)
                if part == "G9":
                    keep_blocks(0)
                if part == "GY0":
                    spread_v(n, 1)
                    keep_blocks(1)
                if part == "GY1":
                    spread_v(n, 2)
                    keep_blocks(2)
                    keep_blocks(3)
                if part == "GY2":
                    spread_v(n, 3)
                if part == "F3b":
                    pool.wait_ge(f_dve, done(F_DVE, n, "mv"))
                    carry_wait(nc.gpsimd)
                    rsqrt(mv2, rstd2, LN_EPS, F_POOL, f_pool, n, "var")
                if part == "F5":
                    pool.wait_ge(f_dve, done(F_DVE, n, "xn"))
                    G.tensor_tensor(x1[:, :, :], x1[:, :, :], gshift[b][:, :].unsqueeze(1).to_broadcast([P, NT, C]),
                                    ALU.add).then_inc(f_pool, 1)
                if part == "F21":
                    pool.wait_ge(f_dve, done(F_DVE, n, "mv3"))
                    carry_wait(nc.gpsimd)
                    rsqrt(mv2, rstd2, LN_EPS, F_POOL, f_pool, n, "var3")

            steps(pool, emit)


def pack(table, offs, cols, arrays):
    out = np.zeros((P, cols), np.float32)
    for name, parts, n in table:
        out[0:parts, offs[name][0]:offs[name][0] + n] = arrays[name].reshape(parts, n)
    return out


def kernel(**inputs):
    import concourse.bacc as bacc
    from concourse.bass_utils import run_bass_kernel_spmd as run

    a = {n: np.asarray(v) for n, v in inputs.items()}
    at = {n[len("L0_attn_"):]: v for n, v in a.items() if n.startswith("L0_attn_")}
    ff = {n[len("L0_ffn_"):]: v for n, v in a.items() if n.startswith("L0_ffn_")}

    def rows(m, k=P):
        m = np.ascontiguousarray(m)
        return m.reshape(-1, k, m.shape[-1]).transpose(1, 0, 2)

    def under(m, bias):
        return np.concatenate([m, bias[..., None, :]], axis=-2)

    weights = {
        "wq": rows(at["Wq"].T), "wkv": rows(np.concatenate([at["Wk"].T, at["Wv"].T], axis=1)), "wm1": rows(at["Wm1"].T),
        "wm2": under(at["Wm2"].T, at["bm2"]), "wproj": rows(at["Wproj"].T), "wfc": rows(at["Wfc"].T),
        "wcp": rows(at["Wcp"].T), "enc": rows(ff["enc_w"]), "s2c": rows(ff["s2c_w"]), "rw1": ff["r_w1"],
        "rw2": under(ff["r_w2"], ff["r_b2"]), "ew1": under(ff["e_w1"], ff["e_b1"]).transpose(1, 0, 2),
        "ew2": ff["e_w2"].reshape(NE, 2, P, MOE).transpose(2, 1, 0, 3), "eb2": np.concatenate([ff["e_b2"], ff["e_b2"]]), "c2s": ff["c2s_w"],
        "dec": rows(ff["dec_w"]), "decb": ff["dec_b"], "bm1": at["bm1"], "bm2": at["bm2"],
        "encb": ff["enc_b"].reshape(4, P).T, "s2cb": ff["s2c_b"], "rb1": ff["r_b1"], "c2sb": ff["c2s_b"].reshape(4, P).T,
    }
    p, f = np.arange(P)[:, None], np.arange(P)[None, :]
    consts = {
        "ident": p == f, "headblk": p // HD == f // HD, "later": (p // CH == f // CH) & (p > f),
        "eye32": p % CH == np.arange(CH)[None, :], "pair": (p // HD) % 2 == np.arange(2)[None, :],
        "selP": np.arange(16)[:, None, None] == np.arange(2)[None, :, None] * 8 + (np.arange(P) // HD)[None, None, :],
        "tie": np.broadcast_to(np.arange(NE)[None, :] < np.arange(NE)[:, None], (P, NE, NE)),
        "inchunk": np.broadcast_to(np.arange(BLK) % CH != 0, (16, BLK)), "neghalf": np.full((P, NT), -0.5),
        "chunk": p // CH == np.arange(CT)[None, :], "ones": np.ones((1, P)),
        "expert": np.arange(16)[:, None] % NE == np.arange(NE)[None, :],
    }
    consts = {n: np.asarray(v, np.float32) for n, v in consts.items()}
    setup = {
        "wmod": rows(a["L0_wmod"]), "lng": np.broadcast_to(ff["ln_g"], (P, C)), "lnb": np.broadcast_to(ff["ln_b"], (P, C)),
        "cT": a["L0_c"].T.reshape(2, P, BATCH).transpose(1, 0, 2),
    }
    arrays = {"x": np.ascontiguousarray(at["x"]), "w": pack(WEIGHTS, WOFF, WCOLS, weights),
              "c": pack(CONSTS, COFF, CCOLS, consts), "s": pack(SETUP, SOFF, SCOLS, setup)}
    nc = bacc.Bacc("TRN2", target_bir_lowering=False, num_devices=1)
    args = [nc.dram_tensor(n, v.shape, mybir.dt.float32, kind="ExternalInput").ap() for n, v in arrays.items()]
    out = nc.dram_tensor("out", (BATCH, SEQ, C), mybir.dt.float32, kind="ExternalOutput").ap()
    build(nc, *args, out)
    r = run(nc, [arrays], core_ids=[0])
    return r.results[0]["out"]
```

```python
import numpy as np
import concourse.bass as bass
from concourse import mybir
from contextlib import ExitStack

BATCH, SEQ, C = 2, 2048, 256
HEADS, HD = 16, 16
HID = 64
FF = 1024
ENC = 512
MOE = 64
NE = 8
EH = 256
P = 128
BLK = 512
NBLK = BATCH * SEQ // BLK
NT = BLK // P
CH = 32
NC = BLK // CH
CT = P // CH
LN_EPS = 1e-5
RMS_EPS = float(np.finfo(np.float32).eps)

WEIGHTS = [
    ("wm2", 65, HEADS),
    ("wproj", 128, 2 * C), ("bm1", 64, 1), ("bm2", 16, 1), ("wfc", 128, 2 * FF),
    ("rw1", 64, 65), ("rw2", 65, NE), ("eb1", 128, 2 * NE),
   
    ("encb", 128, 4), ("s2cb", 64, 1), ("rb1", 65, 1), ("c2sb", 128, 4),
]
SPLIT = [("wcp", 128, 8 * C), ("dec", 128, 4 * C), ("ew2", 128, 2 * NE * MOE), ("s2c", 128, 4 * MOE),
         ("c2s", 65, ENC), ("eb2", 16, MOE), ("enc", 128, 2 * ENC)]
ATTN_SPLIT = [("wq", 128, 2 * C), ("wkv", 128, 2 * 2 * C), ("wm1", 128, 2 * HID)]
CONSTS = [
    ("ident", 128, 128), ("headblk", 128, 8), ("later", 128, 128), ("eye32", 128, CH), ("pair", 128, 2),
    ("selP", 16, 2 * 128), ("tie", 128, NE * NE), ("inchunk", 16, CH),
    ("neghalf", 128, NT), ("chunk", 128, CT), ("expert", 16, NE),
]
SETUP = [("wmod", 128, 2 * 6 * C), ("lng", 128, C), ("lnb", 128, C), ("cT", 128, 2 * BATCH)]


def offsets(table):
    out, at = {}, 0
    for name, parts, cols in table:
        out[name] = (at, parts, cols)
        at += cols
    return out, at


WOFF, WCOLS = offsets(WEIGHTS)
COFF, CCOLS = offsets(CONSTS)
SOFF, SCOLS = offsets(SETUP)
VOFF, VCOLS = offsets(SPLIT)
AOFF, ACOLS = offsets(ATTN_SPLIT)

G_PE = ["xT0", "xT1", "m1", "q0", "q1", "kv0", "kv1", "kv2", "kv3", "zf", "zt", "kT0", "kT1", "P0", "P1",
        "dk0", "dk1", "dk2", "dk3", "scores", "U0", "U1", "Y0", "Y1", "Y2", "Y3",
        "proj0", "proj1", "y2a", "y2b"]
G_ACT = ["hT0", "xh0", "hT1", "xh1", "m1s", "q0", "q1", "gf", "gt", "kT0", "kT1", "Vm0", "Vm1", "Ae0",
         "Vm2", "Vm3", "Ae1", "Ae2", "Ae3", "yT0", "yT1", "y2T0", "y2T1", "y2a", "y2b", "sq"]
G_DVE = ["stats", "mv", "xn", "xl0", "xl1", "kv0", "kv1", "kv2", "kv3", "df", "dt", "d0", "d1", "P", "pend", "qP",
         "D0", "D1", "D2", "D3", "A0", "A1", "A2", "A3"] \
    + [f"S{c}" for c in range(2 * NC)]
G_POOL = ["var", "rstd", "Qx", "B0", "B1", "B2", "B3", "G0", "G1", "G2", "G3", "Ks0", "Ks1", "Ks2", "Ks3",
          "Vx0", "Aq0", "Sm0", "Sm1", "Aq1", "Vx1", "Sm2", "Aq2", "Vx2", "Sm3", "Aq3", "Vx3"]
F_PE = ["fc0", "fc1"] + [s for m in range(6) for s in (f"fc{m + 2}", f"cp{m}")] + ["cp6", "cp7", "hT0", "hT1"] \
    + [f"enc{m}" for m in range(4)] + ["s2c", "r1", "r2", "cT"] \
    + [s for e in range(NE) for s in [f"e1_{2 * e}", f"e1_{2 * e + 1}", f"sp{e}"]
       + ([f"e2_{2 * e - 2}", f"e2_{2 * e - 1}"] if e else [])] \
    + ["e2_14", "e2_15", "moe"] + [f"c2s{m}" for m in range(4)] + [f"dec{i}" for i in range(4)]
F_ACT = [s for m in range(8) for s in (f"relu{m}", f"sqh{m}")] + ["hT0", "x1h0", "hT1", "x1h1"] \
    + [s for m in range(4) for s in (f"enc{m}", f"ench{m}")] + ["cont", "c1a", "c1b", "rh", "w1", "cT"] \
    + [s for e in range(NE) for s in (f"eh{2 * e}", f"eh{2 * e + 1}", f"ehh{2 * e}", f"ehh{2 * e + 1}")] \
    + ["mT"] + [s for m in range(4) for s in (f"ra{m}", f"rah{m}")] \
    + [f"dec{i}" for i in range(4)]
F_DVE = [s for m in range(8) for s in (f"sq{m}", f"sql{m}")] + ["ms", "r2"] + [f"t{i}" for i in range(4)] \
    + ["tg", "x1", "stats", "mv", "xn", "x1l0", "x1l1"] + [f"encl{m}" for m in range(4)] + ["c2"] \
    + ["L", "gt", "eq", "eqm", "rank4", "rank", "top1", "top2", "l1", "l2m", "l2", "diff",
       "w2", "cw1", "cw2", "comb", "chi", "clo"] \
    + [s for e in range(NE) for s in (f"ew{2 * e}", f"ew{2 * e + 1}", f"ehl{2 * e}", f"ehl{2 * e + 1}")] \
    + ["mTl"] + [f"ral{m}" for m in range(4)] + ["stats3", "mv3"]
F_POOL = ["var", "rstd", "x1b", "var3", "rstd3", "dn", "g3", "out"]


def done(steps, n, name):
    return n * len(steps) + steps.index(name) + 1


def build(nc, x, w_d, c_d, s_d, v_d, a_d, e_d, out):
    f32, f32r = mybir.dt.float32, mybir.dt.float32r
    ALU, ACT, AX = mybir.AluOpType, mybir.ActivationFunctionType, mybir.AxisListType
    ctx = ExitStack()
    with ctx:
        def sb(name, shape):
            return ctx.enter_context(nc.sbuf_tensor(name, shape, f32))

        def sem(name):
            return ctx.enter_context(nc.semaphore(name))

        W = sb("W", [P, WCOLS])
        K = sb("K", [P, CCOLS])

        def w(name):
            at, parts, cols = WOFF[name]
            return W[0:parts, at:at + cols]

        def k(name):
            at, parts, cols = COFF[name]
            return K[0:parts, at:at + cols]

        wproj = w("wproj").rearrange("p (k m) -> p k m", k=2)
        wfc = w("wfc").rearrange("p (k m) -> p k m", k=2)
        ident = k("ident")
        selP = [k("selP")[:, a * P:(a + 1) * P] for a in range(2)]

        def rounded(ap):
            return ap.bitcast(f32r)

        W_hi, W_lo = sb("W_hi", [P, VCOLS]), sb("W_lo", [P, VCOLS])

        E1 = sb("E1", [P, NE * EH])
        we1 = rounded(E1[:, :]).rearrange("p (e m) -> p e m", e=NE)
        A_hi, A_lo = sb("A_hi", [P, ACOLS]), sb("A_lo", [P, ACOLS])

        def both(name, pattern, **sizes):
            attn = name in AOFF
            at, parts, cols = (AOFF if attn else VOFF)[name]
            return [rounded(t_[0:parts, at:at + cols]).rearrange(pattern, **sizes)
                    for t_ in ((A_hi, A_lo) if attn else (W_hi, W_lo))]

        wq, wkv, wm1 = (both(name, "p (k m) -> p k m", k=2) for name in ("wq", "wkv", "wm1"))

        wcp = both("wcp", "p (k m) -> p k m", k=8)
        wdec = both("dec", "p (k m) -> p k m", k=4)
        we2 = both("ew2", "p (k e m) -> p k e m", k=2, e=NE)
        ws2c = both("s2c", "p (k m) -> p k m", k=4)
        wc2s = both("c2s", "p (k m) -> p k m", k=4)
        wenc = both("enc", "p (k m) -> p k m", k=2)
        web2 = both("eb2", "p (k m) -> p k m", k=1)
        decb = [a[64:65, 0:2, :].rearrange("p k m -> p (k m)") for a in wc2s]
        ones = wc2s[0][64:65, 2, :]

        modT = sb("modT", [P, 12, BATCH])
        ga = [sb(f"ga{b}", [P, C]) for b in range(BATCH)]
        gscale = [sb(f"gscale{b}", [P, C]) for b in range(BATCH)]
        gshift = [sb(f"gshift{b}", [P, C]) for b in range(BATCH)]

        xin = [sb(f"xin{i}", [P, NT, C]) for i in range(2)]
        stat = sb("stat", [P, NT, 6])
        mv = sb("mv", [P, NT, 2])
        rstd = sb("rstd", [P, NT])
        qs = sb("qs", [P, 2, BLK])
        S = sb("S", [P, NC, 2, P])
        Qx = S[:, 0:8, :, :].rearrange("p (h a t) c m -> p h a (t c m)", h=2, a=2)
        kv = sb("kv", [P, NT, 2 * C])
        kT = sb("kT", [P, 2, BLK])
        xn = Qx[:, 0, :, :].rearrange("p a (b c) -> p (a b) c", c=C)
        xfull = kv[:, 0:2, :]
        hT = kT
        gt = sb("gt", [P, NT, HEADS])
        dt = sb("dt", [P, NT, HEADS])
        pend = sb("pend", [P, 2, NC])
        BA = sb("BA", [P, NT, HEADS, CH])
        D = sb("D", [P, NT, HEADS, CH])
        carry = [sb(f"carry{b}", [P, 2, P]) for b in range(BATCH)]
        Vx = sb("Vx", [P, 2, 8 * (P + HD)])
        vx_diag = Vx[:, :, :].rearrange("p a (h m) -> p a h m", h=8)[:, :, :, 0:HD]
        Aexp = D[:, :, :, :].rearrange("p i h t -> p (i h t)").rearrange("p (h m) -> p h m", h=HEADS)
        Vm = [sb(f"Vm{i}", [P, CT, C]) for i in range(2)]
        gf = Vm[0][0:HEADS, 0:2, :].rearrange("p a b -> p (a b)")
        df = gf
        pm = Vm[1][0:HEADS, :, :].rearrange("p (a b) c -> p a (b c)", a=2)
        Pf = pm[:, 1, :]
        y2T = sb("y2T", [P, 2, BLK])
        y2 = sb("y2", [P, NT, C])
        Ks = y2
        sumsq = sb("sumsq", [P, NT])

        ms = sb("ms", [P, NT])
        r2 = sb("r2", [P, NT])
        R = sb("R", [P, 8, BLK])

        def Rr(slot):
            return rounded(R[:, slot, :])

        x1h, x1l = [Rr(2), Rr(3)], [Rr(6), Rr(7)]
        xh, xl = [Rr(0), Rr(1)], [Rr(4), Rr(5)]

        x1 = sb("x1", [P, NT, C])
        stat2 = sb("stat2", [P, NT, 6])
        mv2 = sb("mv2", [P, NT, 2])
        rstd2 = sb("rstd2", [P, NT])
        xn2 = sb("xn2", [P, NT, C])
        h2T = sb("h2T", [P, 2, BLK])
        cont = sb("cont", [65, BLK])
        m1s = cont
        rh = h2T[0:65, 0, :]
        L = sb("L", [P, NT, NE])
        cmp = xn2[:, 2:4, :].rearrange("p a (i e f) -> p a i e f", i=NT, e=NE)
        idle = sb("idle", [P, 16])
        rank = sb("rank", [P, NT, NE])
        top = sb("top", [P, 2, NT, NE])
        sc = sb("sc", [P, 6, NT])
        lm = sb("lm", [P, NT, NE])
        comb = sb("comb", [P, NT, NE])
        parts16 = sb("parts16", [P, NT, 2, NE])
        sel16 = sb("sel16", [16, NE])
        cT = R[0:16, 6, :]
        c1, c2 = Rr(5), rounded(R[0:MOE, 7, :])
        eh = h2T
        mT = [rounded(R[0:MOE, 3, :]), rounded(R[0:MOE, 7, :])]
        dec = xn2
        res = x1
        whole = xn2[:, :, :].rearrange("p (a b) c -> p a (b c)", a=2)
        relu, square = h2T, hT

        pg_all = ctx.enter_context(nc.psum_tensor("pg", [P, 4, BLK], f32))
        pg = [pg_all[:, i, :] for i in range(4)]
        pf = [ctx.enter_context(nc.psum_tensor(f"pf{i}", [P, BLK], f32)) for i in range(4)]

        const_loaded, gla_loaded, ffn_loaded = sem("const_loaded"), sem("gla_loaded"), sem("ffn_loaded")
        mod_loaded, norm_loaded = sem("mod_loaded"), sem("norm_loaded")
        x_loaded = [sem(f"x_loaded{i}") for i in range(2)]
        stored, end_dve = sem("stored"), sem("end_dve")
        zeroed = sem("zeroed")
        piece_loaded = [sem(f"piece_loaded{i}") for i in range(8)]
        split_done = sem("split_done")
        attn_loaded, attn_split = sem("attn_loaded"), sem("attn_split")
        attn_raw = BA[:, :, :, :].rearrange("p i h t -> p (i h t)")[:, 0:ACOLS]
        flat = "p a b -> p (a b)"
        PIECES = [(v_d[:, 0:1024], h2T[:, :, :].rearrange(flat), W_hi[:, 0:1024], W_lo[:, 0:1024], None),
                  (v_d[:, 1024:2048], y2T[:, :, :].rearrange(flat), W_hi[:, 1024:2048], W_lo[:, 1024:2048], None),
                  (v_d[:, 2048:3072], x1[:, :, :].rearrange(flat), W_hi[:, 2048:3072], W_lo[:, 2048:3072], None),
                  (v_d[:, 3072:4096], h2T[:, :, :].rearrange(flat), W_hi[:, 3072:4096], W_lo[:, 3072:4096], 0),
                  (v_d[:, 4096:5120], y2T[:, :, :].rearrange(flat), W_hi[:, 4096:5120], W_lo[:, 4096:5120], 1),
                  (e_d[:, 0:1024], x1[:, :, :].rearrange(flat), E1[:, 0:1024], None, 2),
                  (e_d[:, 1024:2048], h2T[:, :, :].rearrange(flat), E1[:, 1024:2048], None, 3),
                  (v_d[:, 5120:VCOLS], y2T[:, :, :].rearrange(flat), W_hi[:, 5120:VCOLS], W_lo[:, 5120:VCOLS], 4)]
        SPLIT_DONE = 2 * len(PIECES)
        setup_act, setup_dve, setup_pe = sem("setup_act"), sem("setup_dve"), sem("setup_pe")
        g_pe, g_act, g_dve, g_pool = sem("g_pe"), sem("g_act"), sem("g_dve"), sem("g_pool")
        f_pe, f_act, f_dve, f_pool = sem("f_pe"), sem("f_act"), sem("f_dve"), sem("f_pool")
        MOD = (0, 1, 2, 3, 6, 7, 8, 9)
        SETUP_MOD, SETUP_DVE = 8, 32

        s_all = lm[:, :, :].rearrange("p i e -> p (i e)")[:, 0:8]
        wm_v = S[:, 0:12, :, :].rearrange("p a b c -> p (a b c)")
        wmod = wm_v[:, 0:8 * C].rearrange("p (k m) -> p k m", k=2)
        wgate = wm_v[:, 8 * C:12 * C].rearrange("p (k m) -> p k m", k=2)
        lng, lnb = xn2[:, 0, :], xn2[:, 1, :]
        cTs = s_all[:, 0:4]
        silu = s_all[:, 4:8]
        silu_bc = S[:, 12:14, :, :].rearrange("p a c m -> p (a c m)").rearrange("p (k b m) -> p k b m", k=2, b=2)

        ORDER = ["F1", "G0a", "G0b", "F2", "G1", "F3a", "F3b", "G2", "F4", "G3", "F5", "F6", "G5", "G6a", "F7",
                 "G6b", "F8", "G7a", "G7b", "F9", "X0", "Y0", "G7c", "G7d", "X1", "Z0", "Y1", "G8", "G8b", "G8c",
                 "X2", "Z1", "G9", "Y2", "X3", "Z2", "Y3", "G9b", "X4", "Z3", "Y4", "G9c", "X5", "Z4", "Y5", "GY0",
                 "X6", "Z5", "Y6", "GY1", "X7", "Z6", "Y7", "GY2", "Z7", "X8", "GY3", "F20", "G13", "F21", "G14"]

        def steps(eng, emit):
            def step(ng, nf, bg, bf):
                for part in ORDER:
                    if part[0] == "G" and ng is not None:
                        emit(part, ng, bg)
                    if part[0] != "G" and nf is not None:
                        emit(part, nf, bf)
            step(0, None, 0, None)
            step(1, 0, 1, 0)
            with eng.Fori(0, NBLK // 2 - 1) as j:
                step(j * 2 + 2, j * 2 + 1, 0, 1)
                step(j * 2 + 3, j * 2 + 2, 1, 0)
            step(None, NBLK - 1, None, 1)

        carried = [0]

        def carry_wait(eng):
            if eng is nc.tensor:
                nc.tensor.ldweights(K[:, 0:64].bitcast(mybir.dt.bfloat16), tile_position=(0, 0))
            elif eng is nc.vector:
                nc.vector.memset(idle[:, 0:1], 0.0)
            else:
                carried[0] = carried[0] % 15 + 1
                nc.gpsimd.tensor_tensor(idle[:, carried[0]:carried[0] + 1], K[:, 0:1], K[:, 0:1], ALU.add)

        def first(n):
            return isinstance(n, int) and n == 0

        def last_block(n):
            return isinstance(n, int) and n == NBLK - 1

        def x_count(n, b):
            return (n // 2 + 1) * 16 if isinstance(n, int) else (n - b) * 8 + 16

        block = ctx.enter_context(nc.Block())

        @block.sync
        def _(sp):
            xv = x.rearrange("b (t i p) c -> b t p i c", p=P, i=NT)
            ov = out.rearrange("b (t i p) c -> b t p i c", p=P, i=NT)

            def load_x(t, b):
                sp.dma_start(xin[b][:, :, :], xv[b, t, :, :, :]).then_inc(x_loaded[b], 16)

            def store(n, t, b):
                sp.wait_ge(f_pool, done(F_POOL, n, "out"))
                sp.dma_start(ov[b, t, :, :, :], res[:, :, :]).then_inc(stored, 16)

            sp.dma_start(s_all[:, 0:4], s_d[:, SOFF["cT"][0]:SOFF["cT"][0] + 4]).then_inc(mod_loaded, 16)
            load_x(0, 0)
            sp.dma_start(K[:, :], c_d).then_inc(const_loaded, 16)
            sp.dma_start(wm_v, s_d[:, 0:12 * C]).then_inc(mod_loaded, 16)
            sp.dma_start(attn_raw, a_d).then_inc(attn_loaded, 16)
            cut = WOFF["wfc"][0]
            sp.dma_start(W[:, 0:cut], w_d[:, 0:cut]).then_inc(gla_loaded, 16)
            sp.dma_start(W[:, cut:WCOLS], w_d[:, cut:WCOLS]).then_inc(ffn_loaded, 16)
            sp.dma_start(xn2[:, 0:2, :].rearrange("p a c -> p (a c)"), s_d[:, 12 * C:14 * C]).then_inc(norm_loaded, 16)
            for i, (src, buf, _, _, after) in enumerate(PIECES):
                if i == 3:
                    load_x(0, 1)
                if after is not None:
                    sp.wait_ge(split_done, 2 * after + 2)
                sp.dma_start(buf[:, 0:src.shape[1]], src).then_inc(piece_loaded[i], 16)
            with sp.Fori(0, SEQ // BLK - 1) as t:
                for b in range(BATCH):
                    sp.wait_ge(f_dve, done(F_DVE, t * 2 + b, "x1"))
                    load_x(t + 1, b)
                    store(t * 2 + b, t, b)
            store(NBLK - 2, SEQ // BLK - 1, 0)
            for a in range(2):
                sp.wait_ge(end_dve, 2 * a + 3)
                sp.dma_start(ov[1, SEQ // BLK - 1, :, 2 * a:2 * a + 2, :], res[:, 2 * a:2 * a + 2, :]).then_inc(stored, 16)
            sp.wait_ge(stored, 16 * (NBLK + 1))

        @block.tensor
        def _(pe):
            mm = nc.tensor.matmul

            def tr(out_, in_):
                return nc.tensor.transpose(out_, in_, ident[0:in_.shape[0], 0:in_.shape[0]])

            pe.wait_ge(mod_loaded, 32)
            pe.wait_ge(setup_dve, 2)
            for m in MOD:
                for kk in range(2):
                    last = mm(pg[0][:, 2 * m:2 * m + 2], wmod[:, kk, MOD.index(m) * P:(MOD.index(m) + 1) * P], silu[:, 2 * kk:2 * kk + 2],
                              start=(kk == 0), stop=(kk == 1))
            last.then_inc(setup_pe, 1)
            pe.wait_ge(const_loaded, 16)
            pe.wait_ge(setup_dve, SETUP_MOD)

            def before(n, sem_, table, name):
                if not first(n):
                    pe.wait_ge(sem_, done(table, n - 1, name))

            def thrice(out_, a, a_lo, b, b_lo, start, stop):
                mm(out_, a, b, start=start, stop=False, skip_group_check=True)
                mm(out_, a, b_lo, start=False, stop=False, skip_group_check=True)
                return mm(out_, a_lo, b, start=False, stop=stop, skip_group_check=True)

            def project(n, m):
                if m == 0:
                    before(n, f_act, F_ACT, "dec3")
                pe.wait_ge(f_dve, done(F_DVE, n, f"sql{m}"))
                for i in range(NT):
                    t_ = slice(i * P, (i + 1) * P)
                    last = thrice(pf[(3, 0)[i // 2]][:, (i % 2) * C:(i % 2 + 1) * C], Rr(m % 4)[:, t_], Rr(4 + m % 4)[:, t_],
                                  wcp[0][:, m, :], wcp[1][:, m, :], m == 0 and i % 2 == 0, m == 7 and i % 2 == 1)
                last.then_inc(f_pe, 1)

            def emit(part, n, b):
                if part == "G1":
                    pe.wait_ge(g_dve, done(G_DVE, n, "xn"))
                    before(n, g_act, G_ACT, "y2b")
                    for h in range(2):
                        for i in range(NT):
                            last = tr(pg[h][:, i * P:(i + 1) * P], xn[:, i, h * P:(h + 1) * P])
                        last.then_inc(g_pe, 1)
                if part == "G2":
                    if first(n):
                        pe.wait_ge(gla_loaded, 16)
                        pe.wait_ge(attn_split, 2)
                    pe.wait_ge(g_dve, done(G_DVE, n, "xl1"))
                    for kk in range(2):
                        last = thrice(pg[2][0:HID, :], wm1[0][:, kk, :], wm1[1][:, kk, :], xh[kk], xl[kk], kk == 0, kk == 1)
                    last.then_inc(g_pe, 1)
                    for h, bank in ((0, 3), (1, 0)):
                        for kk in range(2):
                            m = slice(h * P, (h + 1) * P)
                            last = thrice(pg[bank][:, :], wq[0][:, kk, m], wq[1][:, kk, m], xh[kk], xl[kk], kk == 0, kk == 1)
                        last.then_inc(g_pe, 1)
                    for i, bank, freed in ((0, 1, None), (1, 2, "m1s"), (2, 3, "q0"), (3, 0, "q1")):
                        if freed:
                            pe.wait_ge(g_act, done(G_ACT, n, freed))
                        for kk in range(2):
                            t_ = slice(i * P, (i + 1) * P)
                            last = thrice(pg[bank][:, :], xh[kk][:, t_], xl[kk][:, t_], wkv[0][:, kk, :], wkv[1][:, kk, :],
                                          kk == 0, kk == 1)
                        last.then_inc(g_pe, 1)
                if part == "G3":
                    pe.wait_ge(g_dve, done(G_DVE, n, "kv1"))
                    carry_wait(nc.tensor)
                    mm(pg[1][0:HEADS, :], w("wm2")[0:HID, :], m1s[0:HID, :], start=True, stop=True).then_inc(g_pe, 1)
                    for i in range(NT):
                        last = mm(pg[2][:, i * HEADS:(i + 1) * HEADS], m1s[:, i * P:(i + 1) * P], w("wm2"),
                                  start=True, stop=True)
                    last.then_inc(g_pe, 1)
                    pe.wait_ge(g_dve, done(G_DVE, n, "kv3"))
                    for h, bank in ((0, 3), (1, 0)):
                        for i in range(NT):
                            last = tr(pg[bank][:, i * P:(i + 1) * P], kv[:, i, h * P:(h + 1) * P])
                        last.then_inc(g_pe, 1)
                if part == "G5":
                    pe.wait_ge(g_dve, done(G_DVE, n, "P"))
                    pe.wait_ge(g_act, done(G_ACT, n, "gt"))
                    for h in range(2):
                        mm(pg[1 + h][:, :], selP[h], Pf[:, :], start=True, stop=True).then_inc(g_pe, 1)
                if part in ("G6a", "G6b"):
                    pe.wait_ge(g_act, done(G_ACT, n, "kT1"))
                    for i, bank in ((0, 3), (1, 0)) if part == "G6a" else ((2, 1), (3, 2)):
                        pe.wait_ge(g_pool, done(G_POOL, n, f"B{i}"))
                        if i == 2:
                            pe.wait_ge(g_dve, done(G_DVE, n, "qP"))
                        mm(pg[bank][:, :], k("later"), BA[:, i, :, :].rearrange("p h t -> p (h t)"),
                           start=True, stop=True).then_inc(g_pe, 1)
                    if part == "G6b" and first(n):
                        for b in range(BATCH):
                            for a in range(2):
                                for kk in range(2):
                                    last = mm(pf[b][:, a * C:(a + 1) * C], silu_bc[:, kk, b, :],
                                              wgate[:, kk, a * C:(a + 1) * C], start=(kk == 0), stop=(kk == 1))
                        last.then_inc(setup_pe, 1)
                if part in ("G7a", "G7b", "G7c", "G7d"):
                    if part == "G7a":
                        pe.wait_ge(g_pool, done(G_POOL, n, "Qx"))
                        pe.wait_ge(g_dve, done(G_DVE, n, "D3"))
                        carry_wait(nc.tensor)
                    for ih in {"G7a": (0,), "G7b": (1, 2, 3, 4, 5), "G7c": (6,), "G7d": (7,)}[part]:
                        i, h = ih // 2, ih % 2
                        for c in range(CT):
                            t0 = i * P + c * CH
                            for r in range(4):
                                last = mm(pg[r][c * CH:(c + 1) * CH, i * P + h * 64:i * P + h * 64 + 64],
                                          kT[32 * r:32 * r + 32, h, t0:t0 + CH],
                                          Qx[32 * r:32 * r + 32, h, :, t0:t0 + CH], start=True, stop=True)
                    if part == "G7d":
                        last.then_inc(g_pe, 1)
                if part in ("G8", "G9"):
                    u = int(part == "G9")
                    pe.wait_ge(g_pool, done(G_POOL, n, f"Ks{2 * u + 1}"))
                    pe.wait_ge(g_dve, done(G_DVE, n, f"S{NC - 1}" if u else "A3"))
                    for ii in range(2):
                        i = 2 * u + ii
                        pe.wait_ge(g_act, done(G_ACT, n, f"Vm{i}"))
                        for h in range(2):
                            last = mm(pg[2 * ii + h][:, :], Ks[:, i, h * P:(h + 1) * P], Vm[ii][:, :, h * P:(h + 1) * P],
                                      start=True, stop=True)
                    last.then_inc(g_pe, 1)
                if part[0:2] == "GY":
                    i = int(part[2])
                    if i == 0:
                        pe.wait_ge(g_dve, done(G_DVE, n, f"S{2 * NC - 1}"))
                    pe.wait_ge(g_pool, done(G_POOL, n, ("Sm0", "Vx1", "Vx2", "Vx3")[i]))
                    pe.wait_ge(g_act, done(G_ACT, n, f"Ae{i}"))
                    for h in range(2):
                        for c in range(CT):
                            t0 = i * P + c * CH
                            mm(pg[h][:, t0:t0 + CH], S[:, i * CT + c, h, :], qs[:, h, t0:t0 + CH],
                               start=(c == 0), stop=False, skip_group_check=True)
                        for a in range(8 * h, 8 * h + 8):
                            last = mm(pg[h][:, i * P:(i + 1) * P], Vx[:, h, (a % 8) * P:(a % 8 + 1) * P], Aexp[:, a, :],
                                      start=False, stop=(a == 8 * h + 7), skip_group_check=True)
                    last.then_inc(g_pe, 1)
                if part == "G13":
                    pe.wait_ge(g_act, done(G_ACT, n, "yT1"))
                    for h in range(2):
                        for kk in range(2):
                            last = mm(pg[2 + h][:, :], wproj[:, kk, h * P:(h + 1) * P], hT[:, kk, :],
                                      start=(kk == 0), stop=(kk == 1))
                        last.then_inc(g_pe, 1)
                if part == "G14":
                    pe.wait_ge(g_act, done(G_ACT, n, "y2T1"))
                    for i in range(NT):
                        for h in range(2):
                            last = tr(pg[i // 2][:, (i % 2) * C + h * P:(i % 2) * C + (h + 1) * P],
                                      y2T[:, h, i * P:(i + 1) * P])
                        if i % 2:
                            last.then_inc(g_pe, 1)
                if part in ("F1", "F2"):
                    if part == "F1":
                        if first(n):
                            pe.wait_ge(ffn_loaded, 16)
                            pe.wait_ge(setup_dve, SETUP_DVE)
                            pe.wait_ge(split_done, SPLIT_DONE)
                        pe.wait_ge(g_act, done(G_ACT, n, "y2T1"))
                    for m in (range(4) if part == "F1" else range(4, 8)):
                        if m >= 2:
                            pe.wait_ge(f_act, done(F_ACT, n, f"relu{m - 2}"))
                        else:
                            before(n, f_act, F_ACT, f"dec{m}")
                        for kk in range(2):
                            last = mm(pf[1 + m % 2][:, :], wfc[:, kk, m * P:(m + 1) * P], y2T[:, kk, :],
                                      start=(kk == 0), stop=(kk == 1))
                        last.then_inc(f_pe, 1)
                        if m >= 2:
                            project(n, m - 2)
                if part == "F3a":
                    project(n, 6)
                    project(n, 7)
                if part == "F4":
                    pe.wait_ge(f_dve, done(F_DVE, n, "xn"))
                    for h in range(2):
                        for i in range(NT):
                            last = tr(pf[h][:, i * P:(i + 1) * P], xn2[:, i, h * P:(h + 1) * P])
                        last.then_inc(f_pe, 1)
                if part == "F5":
                    pe.wait_ge(f_dve, done(F_DVE, n, "x1l1"))
                    for m in range(4):
                        for kk in range(2):
                            cols = slice(m * P, (m + 1) * P)
                            last = thrice(pf[(2 + m) % 4][:, :], wenc[0][:, kk, cols], wenc[1][:, kk, cols], x1h[kk], x1l[kk],
                                          kk == 0, kk == 1)
                        last.then_inc(f_pe, 1)
                if part == "F6":
                    for kk in range(4):
                        pe.wait_ge(f_dve, done(F_DVE, n, f"encl{kk}"))
                        last = thrice(pf[2][0:MOE, :], ws2c[0][:, kk, :], ws2c[1][:, kk, :], Rr(kk), Rr(4 + kk),
                                      kk == 0, kk == 3)
                    last.then_inc(f_pe, 1)
                if part == "F7":
                    pe.wait_ge(f_act, done(F_ACT, n, "cont"))
                    carry_wait(nc.tensor)
                    mm(pf[3][0:65, :], w("rw1"), cont[0:64, :], start=True, stop=True).then_inc(f_pe, 1)
                if part == "F8":
                    pe.wait_ge(f_act, done(F_ACT, n, "rh"))
                    for i in range(NT):
                        last = mm(pf[0][:, i * NE:(i + 1) * NE], rh[:, i * P:(i + 1) * P], w("rw2"),
                                  start=True, stop=True)
                    last.then_inc(f_pe, 1)
                if part == "F9":
                    pe.wait_ge(f_dve, done(F_DVE, n, "clo"))
                    for i in range(NT):
                        last = tr(pf[0][0:2 * NE, i * P:(i + 1) * P], parts16[:, i, :, :].rearrange("p a e -> p (a e)"))
                    last.then_inc(f_pe, 1)

                def spread(e):
                    if e:
                        pe.wait_ge(f_dve, done(F_DVE, n, f"ew{2 * e - 1}"))
                    else:
                        pe.wait_ge(f_act, done(F_ACT, n, "cT"))
                    mm(pf[0][:, :], sel16[:, e:e + 1].to_broadcast([16, P]).bitcast(f32r), rounded(cT),
                       start=True, stop=True).then_inc(f_pe, 1)

                def second(e):
                    for m in range(2):
                        q = 2 * e + m
                        pe.wait_ge(f_dve, done(F_DVE, n, f"ehl{q}"))
                        thrice(pf[3][0:MOE, :], we2[0][:, m, e, :], we2[1][:, m, e, :], Rr(q % 3), Rr(3 + q % 2),
                               q == 0, False).then_inc(f_pe, 1)

                if part[0] == "X":
                    e = int(part[1:])
                    if e < NE:
                        if e == 0:
                            pe.wait_ge(f_act, done(F_ACT, n, "c1b"))
                            pe.wait_ge(f_dve, done(F_DVE, n, "c2"))
                        for m in range(2):
                            if e:
                                pe.wait_ge(f_act, done(F_ACT, n, f"eh{2 * e - 2 + m}"))
                            cols = slice(m * P, (m + 1) * P)
                            mm(pf[1 + m][:, :], we1[:, e, cols], c1, start=True, stop=False, skip_group_check=True)
                            mm(pf[1 + m][:, :], we1[0:MOE, e, cols], c2, start=False, stop=True,
                               skip_group_check=True).then_inc(f_pe, 1)
                        spread(e)
                    if e == NE:
                        mm(pf[3][0:MOE, :], web2[0][:, 0, :], rounded(cT), start=False, stop=False, skip_group_check=True)
                        mm(pf[3][0:MOE, :], web2[1][:, 0, :], rounded(cT), start=False, stop=True,
                           skip_group_check=True).then_inc(f_pe, 1)
                if part[0] == "Z":
                    second(int(part[1:]))
                if part == "F20":
                    pe.wait_ge(f_dve, done(F_DVE, n, "mTl"))
                    for m in range(4):
                        thrice(pf[(1 + m) % 4][:, :], wc2s[0][0:MOE, m, :], wc2s[1][0:MOE, m, :], mT[0], mT[1],
                               True, True).then_inc(f_pe, 1)
                if part == "F21":
                    for i in range(NT):
                        for kk in range(4):
                            if i == 0:
                                pe.wait_ge(f_dve, done(F_DVE, n, f"ral{kk}"))
                            t_ = slice(i * P, (i + 1) * P)
                            thrice(pf[(1 + i) % 4][:, 0:C], Rr(kk)[:, t_], Rr(4 + kk)[:, t_], wdec[0][:, kk, :],
                                   wdec[1][:, kk, :], kk == 0, False)
                        mm(pf[(1 + i) % 4][:, 0:C], ones, decb[0], start=False, stop=False, skip_group_check=True)
                        mm(pf[(1 + i) % 4][:, 0:C], ones, decb[1], start=False, stop=True,
                           skip_group_check=True).then_inc(f_pe, 1)

            steps(pe, emit)

        @block.scalar
        def _(act):
            A = nc.scalar.activation
            act.wait_ge(mod_loaded, 32)
            A(silu, cTs, ACT.Sigmoid).then_inc(setup_act, 1)
            act.wait_ge(const_loaded, 16)
            act.wait_ge(setup_dve, SETUP_MOD)

            def before(n, sem_, table, name):
                if not first(n):
                    act.wait_ge(sem_, done(table, n - 1, name))

            def mask_v(n, i):
                for c in range(CT):
                    last = A(Vm[i % 2][:, c, :], kv[:, i, C:2 * C], ACT.Copy, scale=k("chunk")[:, c:c + 1])
                last.then_inc(g_act, 1)

            def expand(n, i):
                act.wait_ge(g_dve, done(G_DVE, n, f"A{i}"))
                for c in range(CT // 2):
                    last = A(Aexp[:, :, c * CH:(c + 1) * CH], BA[:, i, :, :], ACT.Copy, scale=k("chunk")[:, c:c + 1])
                last.then_inc(g_act, 1)

            def emit(part, n, b):
                if part == "G1":
                    before(n, g_act, G_ACT, "Vm3")
                    before(n, g_pool, G_POOL, "Vx3")
                    if not first(n):
                        act.wait_ge(f_pe, done(F_PE, n - 1, "cp5"))
                    for h in range(2):
                        act.wait_ge(g_pe, done(G_PE, n, f"xT{h}"))
                        A(xfull[:, h, :], pg[h][:, :], ACT.Identity, scale=modT[:, 2 + h, b:b + 1],
                          bias=modT[:, h, b:b + 1]).then_inc(g_act, 1)
                        act.wait_ge(g_act, done(G_ACT, n, f"hT{h}"))
                        A(xh[h], xfull[:, h, :], ACT.Copy).then_inc(g_act, 1)
                if part == "G2":
                    if first(n):
                        act.wait_ge(gla_loaded, 16)
                    act.wait_ge(g_pe, done(G_PE, n, "m1"))
                    A(m1s[0:HID, :], pg[2][0:HID, :], ACT.Relu, bias=w("bm1")).then_inc(g_act, 1)
                    for h, bank in ((0, 3), (1, 0)):
                        act.wait_ge(g_pe, done(G_PE, n, f"q{h}"))
                        A(qs[:, h, :], pg[bank][:, :], ACT.Copy).then_inc(g_act, 1)
                if part == "G3":
                    act.wait_ge(g_pe, done(G_PE, n, "zf"))
                    A(gf[:, :], pg[1][0:HEADS, :], ACT.Sigmoid, bias=w("bm2")).then_inc(g_act, 1)
                    act.wait_ge(g_pe, done(G_PE, n, "zt"))
                    A(gt[:, :, :].rearrange("p i h -> p (i h)"), pg[2][:, 0:NT * HEADS], ACT.Sigmoid).then_inc(g_act, 1)
                    for h, bank in ((0, 3), (1, 0)):
                        act.wait_ge(g_pe, done(G_PE, n, f"kT{h}"))
                        A(kT[:, h, :], pg[bank][:, :], ACT.Copy).then_inc(g_act, 1)
                if part == "G5":
                    act.wait_ge(g_dve, done(G_DVE, n, "kv3"))
                    act.wait_ge(g_pe, done(G_PE, n, "P1"))
                    mask_v(n, 0)
                    mask_v(n, 1)
                if part == "G8":
                    act.wait_ge(g_dve, done(G_DVE, n, "A3"))
                    act.wait_ge(g_pool, done(G_POOL, n, "Ks3"))
                    expand(n, 0)
                    act.wait_ge(g_pe, done(G_PE, n, "U0"))
                    mask_v(n, 2)
                    mask_v(n, 3)
                if part in ("GY0", "GY1", "GY2"):
                    act.wait_ge(g_pe, done(G_PE, n, f"Y{part[2]}"))
                    expand(n, int(part[2]) + 1)
                if part == "GY3":
                    act.wait_ge(g_pe, done(G_PE, n, "Y3"))
                    for h in range(2):
                        A(hT[:, h, :], pg[h][:, :], ACT.Copy).then_inc(g_act, 1)
                if part == "G13":
                    before(n, f_pe, F_PE, "fc7")
                    if first(n):
                        act.wait_ge(split_done, SPLIT_DONE)
                    for h in range(2):
                        act.wait_ge(g_pe, done(G_PE, n, f"proj{h}"))
                        A(y2T[:, h, :], pg[2 + h][:, :], ACT.Copy).then_inc(g_act, 1)
                if part == "G14":
                    before(n, f_dve, F_DVE, "t3")
                    for a in range(2):
                        act.wait_ge(g_pe, done(G_PE, n, f"y2{'ab'[a]}"))
                        A(y2[:, 2 * a:2 * a + 2, :].rearrange("p i c -> p (i c)"), pg[a][:, :], ACT.Copy).then_inc(g_act, 1)
                    act.wait_ge(g_act, done(G_ACT, n, "y2b"))
                    before(n, f_dve, F_DVE, "ms")
                    act.wait_ge(g_pe, done(G_PE, n, "proj1"))
                    for i in range(NT):
                        last = A(hT[:, i // 2, (i % 2) * C:(i % 2 + 1) * C], y2[:, i, :], ACT.Square,
                                 accum_out=sumsq[:, i:i + 1])
                    last.then_inc(g_act, 1)
                if part in ("F1", "F2"):
                    if part == "F1":
                        if first(n):
                            act.wait_ge(ffn_loaded, 16)
                        before(n, f_pe, F_PE, "dec3")
                    for m in (range(4) if part == "F1" else range(4, 8)):
                        act.wait_ge(f_pe, done(F_PE, n, f"fc{m}"))
                        if m >= 2:
                            act.wait_ge(f_dve, done(F_DVE, n, f"sq{m - 2}"))
                        A(relu[:, m % 2, :], pf[1 + m % 2][:, :], ACT.Relu).then_inc(f_act, 1)
                        act.wait_ge(f_act, done(F_ACT, n, f"relu{m}"))
                        if m >= 4:
                            act.wait_ge(f_pe, done(F_PE, n, f"cp{m - 4}"))
                        A(Rr(m % 4), relu[:, m % 2, :], ACT.Square).then_inc(f_act, 1)
                if part == "F4":
                    for h in range(2):
                        act.wait_ge(f_pe, done(F_PE, n, f"hT{h}"))
                        A(h2T[:, h, :], pf[h][:, :], ACT.Identity, scale=modT[:, 8 + h, b:b + 1],
                          bias=modT[:, 6 + h, b:b + 1]).then_inc(f_act, 1)
                        act.wait_ge(f_act, done(F_ACT, n, f"hT{h}"))
                        A(x1h[h], h2T[:, h, :], ACT.Copy).then_inc(f_act, 1)
                if part == "F5":
                    for m in range(4):
                        act.wait_ge(f_pe, done(F_PE, n, f"enc{m}"))
                        if m >= 2:
                            act.wait_ge(f_dve, done(F_DVE, n, f"encl{m - 2}"))
                        else:
                            act.wait_ge(f_pe, done(F_PE, n, "hT1"))
                        A(whole[:, m % 2, :], pf[(2 + m) % 4][:, :], ACT.Sigmoid, bias=w("encb")[:, m:m + 1]).then_inc(f_act, 1)
                        act.wait_ge(f_act, done(F_ACT, n, f"enc{m}"))
                        if m == 2:
                            act.wait_ge(f_pe, done(F_PE, n, "enc3"))
                        A(Rr(m), whole[:, m % 2, :], ACT.Copy).then_inc(f_act, 1)
                if part == "F6":
                    act.wait_ge(f_pe, done(F_PE, n, "s2c"))
                    A(cont[0:MOE, :], pf[2][0:MOE, :], ACT.Identity, bias=w("s2cb")).then_inc(f_act, 1)
                    act.wait_ge(f_act, done(F_ACT, n, "cont"))
                    for h in range(2):
                        A(c1[h * MOE:(h + 1) * MOE, :], cont[0:MOE, :], ACT.Copy).then_inc(f_act, 1)
                if part == "F7":
                    act.wait_ge(f_pe, done(F_PE, n, "r1"))
                    A(rh, pf[3][0:65, :], ACT.Relu, bias=w("rb1")).then_inc(f_act, 1)
                if part == "F8":
                    act.wait_ge(f_dve, done(F_DVE, n, "diff"))
                    A(sc[:, 3, :], sc[:, 2, :], ACT.Sigmoid).then_inc(f_act, 1)
                if part == "F9":
                    act.wait_ge(f_pe, done(F_PE, n, "cT"))
                    A(rounded(cT), pf[0][0:2 * NE, :], ACT.Copy).then_inc(f_act, 1)
                if part[0] == "X" and int(part[1:]) < NE:
                    e = int(part[1:])
                    for q in (2 * e, 2 * e + 1):
                        act.wait_ge(f_pe, done(F_PE, n, f"e1_{q}"))
                        if q >= 2:
                            act.wait_ge(f_dve, done(F_DVE, n, f"ew{q - 2}"))
                        A(eh[:, q % 2, :], pf[1 + q % 2][:, :], ACT.Relu, bias=w("eb1")[:, q:q + 1]).then_inc(f_act, 1)
                if part[0] == "Y":
                    e = int(part[1:])
                    for q in (2 * e, 2 * e + 1):
                        act.wait_ge(f_dve, done(F_DVE, n, f"ew{q}"))
                        if q >= 3:
                            act.wait_ge(f_pe, done(F_PE, n, f"e2_{q - 3}"))
                        A(Rr(q % 3), whole[:, q % 2, :], ACT.Copy).then_inc(f_act, 1)
                if part == "X8":
                    act.wait_ge(f_pe, done(F_PE, n, "moe"))
                    A(mT[0], pf[3][0:MOE, :], ACT.Copy).then_inc(f_act, 1)
                if part == "F20":
                    for m in range(4):
                        act.wait_ge(f_pe, done(F_PE, n, f"c2s{m}"))
                        if m >= 2:
                            act.wait_ge(f_dve, done(F_DVE, n, f"ral{m - 2}"))
                        A(whole[:, m % 2, :], pf[(1 + m) % 4][:, :], ACT.Sigmoid, bias=w("c2sb")[:, m:m + 1]).then_inc(f_act, 1)
                        act.wait_ge(f_act, done(F_ACT, n, f"ra{m}"))
                        A(Rr(m), whole[:, m % 2, :], ACT.Copy).then_inc(f_act, 1)
                if part == "F21":
                    for i in range(NT):
                        act.wait_ge(f_pe, done(F_PE, n, f"dec{i}"))
                        A(dec[:, i, :], pf[(1 + i) % 4][:, 0:C], ACT.Sigmoid).then_inc(f_act, 1)

            steps(act, emit)

        @block.vector
        def _(dve):
            V = nc.vector
            made = [0]

            def setup(ins):
                made[0] += 1
                ins.then_inc(setup_dve, 1)
                dve.wait_ge(setup_dve, made[0])

            dve.wait_ge(setup_act, 1)
            setup(V.tensor_tensor(silu, cTs, silu, ALU.mult))
            setup(V.tensor_copy(silu_bc, silu.rearrange("p (k b) -> p k b", k=2).unsqueeze(3).to_broadcast([P, 2, 2, P])))
            V.memset(cont[64:65, :], 1.0)
            V.memset(carry[0][:, :, :].rearrange("p a b -> p (a b)"), 0.0)
            setup(V.memset(carry[1][:, :, :].rearrange("p a b -> p (a b)"), 0.0))
            setup(V.tensor_copy(sel16[:, :].bitcast(f32r), k("expert")))

            def before(n, sem_, table, name):
                if not first(n):
                    dve.wait_ge(sem_, done(table, n - 1, name))

            def modulation():
                dve.wait_ge(setup_pe, 1)
                for m in (0, 6):
                    setup(V.tensor_copy(modT[:, m:m + 4, :].rearrange("p m b -> p (m b)"), pg[0][:, 2 * m:2 * m + 8]))
                for m in (2, 8):
                    setup(V.tensor_scalar(modT[:, m:m + 2, :], modT[:, m:m + 2, :], 1.0, None, ALU.add))
                dve.wait_ge(const_loaded, 16)
                assert made[0] == SETUP_MOD

            def gates():
                dve.wait_ge(norm_loaded, 16)
                dve.wait_ge(setup_pe, 2)
                for b in range(BATCH):
                    raw, sgn, mag = (x1[:, a, :] for a in range(3))
                    for a in range(2):
                        setup(V.tensor_copy(raw, pf[b][:, a * C:(a + 1) * C]))
                        setup(V.tensor_scalar(sgn, raw, 0.0, 2.0, ALU.is_ge, ALU.mult))
                        setup(V.scalar_tensor_tensor(mag, sgn, -1.0, raw, ALU.add, ALU.mult))
                        setup(V.tensor_scalar(mag, mag, 0.25, None, ALU.max))
                        dst = ga[b] if a == 0 else gshift[b]
                        setup(V.scalar_tensor_tensor(dst[:, :], sgn, -1.0, mag, ALU.add, ALU.mult))
                    setup(V.tensor_tensor(gscale[b][:, :], gshift[b][:, :], lng, ALU.mult))
                    setup(V.tensor_tensor(gshift[b][:, :], gshift[b][:, :], lnb, ALU.mult))
                assert made[0] == SETUP_DVE

            def mine(table, n, name):
                dve.wait_ge(g_dve if table is G_DVE else f_dve, done(table, n, name))

            def emit(part, n, b):
                if part == "G0a":
                    dve.wait_ge(x_loaded[b], x_count(n, b))
                    for i in range(NT):
                        last = V.bn_stats(stat[:, i, :], xin[b][:, i, :])
                    last.then_inc(g_dve, 1)
                    dve.wait_ge(g_dve, done(G_DVE, n, "stats"))
                    carry_wait(nc.vector)
                    for i in range(NT):
                        last = V.bn_aggr(mv[:, i, :], stat[:, i, :])
                    last.then_inc(g_dve, 1)
                if part == "G0b" and first(n):
                    dve.wait_ge(attn_loaded, 16)
                    V.tensor_copy(rounded(A_hi[:, :]), attn_raw).then_inc(attn_split, 1)
                    dve.wait_ge(attn_split, 1)
                    V.tensor_tensor(rounded(A_lo[:, :]), attn_raw, A_hi[:, :], ALU.subtract).then_inc(attn_split, 1)
                    modulation()
                if part == "G0b":
                    mine(G_DVE, n, "mv")
                    dve.wait_ge(g_pool, done(G_POOL, n, "rstd"))
                    before(n, g_pe, G_PE, "Y1")
                    for i in range(NT):
                        last = V.tensor_scalar(xn[:, i, :], xin[b][:, i, :], mv[:, i, 0:1], rstd[:, i:i + 1],
                                               ALU.subtract, ALU.mult)
                    last.then_inc(g_dve, 1)
                if part == "G1":
                    if not first(n):
                        dve.wait_ge(f_pe, done(F_PE, n - 1, "cp5"))
                    for h in range(2):
                        dve.wait_ge(g_act, done(G_ACT, n, f"xh{h}"))
                        V.tensor_tensor(xl[h], xfull[:, h, :], R[:, h, :], ALU.subtract).then_inc(g_dve, 1)
                if part == "G2":
                    for i, bank in enumerate((1, 2, 3, 0)):
                        dve.wait_ge(g_pe, done(G_PE, n, f"kv{i}"))
                        V.tensor_copy(kv[:, i, :], pg[bank][:, :]).then_inc(g_dve, 1)
                if part == "G3":
                    dve.wait_ge(g_act, done(G_ACT, n, "gf"))
                    V.tensor_scalar(df[:, :], gf[:, :], -1.0, 1.0, ALU.mult, ALU.add).then_inc(g_dve, 1)
                    dve.wait_ge(g_act, done(G_ACT, n, "gt"))
                    V.tensor_scalar(dt[:, :, :].rearrange("p i h -> p (i h)"), gt[:, :, :].rearrange("p i h -> p (i h)"),
                                    -1.0, 1.0, ALU.mult, ALU.add).then_inc(g_dve, 1)
                    mine(G_DVE, n, "df")
                    V.tensor_tensor(pm[:, 0, :].rearrange("p (c t) -> p c t", t=CH), df[:, :].rearrange("p (c t) -> p c t", t=CH),
                                    k("inchunk").unsqueeze(1).to_broadcast([HEADS, NC, CH]), ALU.mult).then_inc(g_dve, 1)
                    mine(G_DVE, n, "d0")
                    V.tensor_tensor(pm[:, 1, :], df[:, :], pm[:, 0, :], ALU.subtract).then_inc(g_dve, 1)
                    mine(G_DVE, n, "d1")
                    V.tensor_tensor_scan(Pf[:, :], pm[:, 0, :], pm[:, 1, :], 0.0, ALU.mult, ALU.add).then_inc(g_dve, 1)
                if part == "G5":
                    dve.wait_ge(g_pe, done(G_PE, n, "P1"))
                    for h in range(2):
                        last = V.tensor_copy(pend[:, h, :], pg[1 + h][:, CH - 1:BLK:CH])
                    last.then_inc(g_dve, 1)
                    dve.wait_ge(g_pool, done(G_POOL, n, "Qx"))
                    for h in range(2):
                        last = V.tensor_tensor(qs[:, h, :], qs[:, h, :], pg[1 + h][:, :], ALU.mult)
                    last.then_inc(g_dve, 1)
                if part in ("G6a", "G6b"):
                    for i, bank in ((0, 3), (1, 0)) if part == "G6a" else ((2, 1), (3, 2)):
                        dve.wait_ge(g_pe, done(G_PE, n, f"dk{i}"))
                        dve.wait_ge(g_pool, done(G_POOL, n, f"G{i}"))
                        d = D[:, i, :, :].rearrange("p h t -> p (h t)")
                        V.tensor_tensor_scan(d, pg[bank][:, :], d, 0.0, ALU.mult, ALU.add).then_inc(g_dve, 1)
                if part == "G7d":
                    dve.wait_ge(g_pe, done(G_PE, n, "scores"))
                    mine(G_DVE, n, "D3")
                    for i in range(NT):
                        V.tensor_tensor(BA[:, i, :, :].rearrange("p (a r b) t -> p r a (b t)", a=2, r=4),
                                        pg_all[:, :, i * P:(i + 1) * P].rearrange("p r (a m) -> p r a m", a=2),
                                        D[:, i, :, :].rearrange("p (a r b) t -> p r a (b t)", a=2, r=4),
                                        ALU.mult).then_inc(g_dve, 1)
                if part in ("G8b", "G8c", "G9b", "G9c"):
                    u = ("G8b", "G8c", "G9b", "G9c").index(part)
                    dve.wait_ge(g_pe, done(G_PE, n, f"U{u // 2}"))
                    if u == 2:
                        dve.wait_ge(g_pool, done(G_POOL, n, "Sm0"))
                    for c in range(CT * u, CT * (u + 1)):
                        ii, cc = (c // CT) % 2, c % CT
                        for h in range(2):
                            if c:
                                mine(G_DVE, n, f"S{2 * (c - 1) + h}")
                            src = S[:, c, h, :] if c else carry[b][:, h, :]
                            dst = S[:, c + 1, h, :] if c < NC - 1 else carry[b][:, h, :]
                            V.scalar_tensor_tensor(dst, src, pend[:, h, c:c + 1], pg[2 * ii + h][:, cc * P:(cc + 1) * P],
                                                   ALU.mult, ALU.add).then_inc(g_dve, 1)
                if part == "GY0" and first(n):
                    for i, (src, buf, hi, lo, _) in enumerate(PIECES):
                        raw = buf[:, 0:src.shape[1]]
                        dve.wait_ge(piece_loaded[i], 16)
                        V.tensor_copy(rounded(hi), raw).then_inc(split_done, 1)
                        dve.wait_ge(split_done, 2 * i + 1)
                        if lo is None:
                            raw, hi = raw[MOE:P, :], hi[MOE:P, :]
                            lo = hi
                        V.tensor_tensor(rounded(lo), raw, hi, ALU.subtract).then_inc(split_done, 1)
                    dve.wait_ge(split_done, SPLIT_DONE)
                    gates()
                if part in ("F1", "F2"):
                    dve.wait_ge(g_act, done(G_ACT, n, "sq"))
                    for m in (range(4) if part == "F1" else range(4, 8)):
                        dve.wait_ge(f_act, done(F_ACT, n, f"relu{m}"))
                        V.tensor_tensor(square[:, m % 2, :], relu[:, m % 2, :], relu[:, m % 2, :], ALU.mult).then_inc(f_dve, 1)
                        mine(F_DVE, n, f"sq{m}")
                        dve.wait_ge(f_act, done(F_ACT, n, f"sqh{m}"))
                        if m >= 4:
                            dve.wait_ge(f_pe, done(F_PE, n, f"cp{m - 4}"))
                        V.tensor_tensor(Rr(4 + m % 4), square[:, m % 2, :], R[:, m % 4, :], ALU.subtract).then_inc(f_dve, 1)
                if part == "F3b":
                    V.tensor_scalar(ms[:, :], sumsq[:, :], 1.0 / C, RMS_EPS, ALU.mult, ALU.add).then_inc(f_dve, 1)
                    mine(F_DVE, n, "ms")
                    V.reciprocal(r2[:, :], ms[:, :]).then_inc(f_dve, 1)
                    mine(F_DVE, n, "r2")
                if part == "F3b":
                    if not first(n):
                        dve.wait_ge(stored, n * 16)
                    for i in range(NT):
                        dve.wait_ge(f_pe, done(F_PE, n, "cp7"))
                        V.scalar_tensor_tensor(x1[:, i, :], pf[(3, 0)[i // 2]][:, (i % 2) * C:(i % 2 + 1) * C], r2[:, i:i + 1], y2[:, i, :],
                                               ALU.mult, ALU.add).then_inc(f_dve, 1)
                    mine(F_DVE, n, "t3")
                    V.tensor_tensor(x1[:, :, :], x1[:, :, :], ga[b][:, :].unsqueeze(1).to_broadcast([P, NT, C]), ALU.mult).then_inc(f_dve, 1)
                    mine(F_DVE, n, "tg")
                    V.tensor_tensor(x1[:, :, :], x1[:, :, :], xin[b][:, :, :], ALU.add).then_inc(f_dve, 1)
                    mine(F_DVE, n, "x1")
                    for i in range(NT):
                        last = V.bn_stats(stat2[:, i, :], x1[:, i, :])
                    last.then_inc(f_dve, 1)
                    dve.wait_ge(f_dve, done(F_DVE, n, "stats"))
                    carry_wait(nc.vector)
                    for i in range(NT):
                        last = V.bn_aggr(mv2[:, i, :], stat2[:, i, :])
                    last.then_inc(f_dve, 1)
                    mine(F_DVE, n, "mv")
                    dve.wait_ge(f_pool, done(F_POOL, n, "rstd"))
                    for i in range(NT):
                        last = V.tensor_scalar(xn2[:, i, :], x1[:, i, :], mv2[:, i, 0:1], rstd2[:, i:i + 1],
                                               ALU.subtract, ALU.mult)
                    last.then_inc(f_dve, 1)
                if part == "F4":
                    for h in range(2):
                        dve.wait_ge(f_act, done(F_ACT, n, f"x1h{h}"))
                        V.tensor_tensor(x1l[h], h2T[:, h, :], R[:, 2 + h, :], ALU.subtract).then_inc(f_dve, 1)
                if part == "F5":
                    for m in range(4):
                        dve.wait_ge(f_act, done(F_ACT, n, f"ench{m}"))
                        V.tensor_tensor(Rr(4 + m), whole[:, m % 2, :], R[:, m, :], ALU.subtract).then_inc(f_dve, 1)
                if part == "F20":
                    for m in range(4):
                        dve.wait_ge(f_act, done(F_ACT, n, f"rah{m}"))
                        V.tensor_tensor(Rr(4 + m), whole[:, m % 2, :], R[:, m, :], ALU.subtract).then_inc(f_dve, 1)
                if part == "F8":
                    dve.wait_ge(f_pe, done(F_PE, n, "r2"))
                    V.tensor_copy(L[:, :, :].rearrange("p i e -> p (i e)"), pf[0][:, 0:NT * NE]).then_inc(f_dve, 1)
                    mine(F_DVE, n, "L")
                    full = [P, NT, NE, NE]
                    le, lf = L[:, :, :].unsqueeze(3).to_broadcast(full), L[:, :, :].unsqueeze(2).to_broadcast(full)
                    tie = k("tie").rearrange("p (e f) -> p e f", e=NE).unsqueeze(1).to_broadcast(full)
                    V.tensor_tensor(cmp[:, 0], le, lf, ALU.is_lt).then_inc(f_dve, 1)
                    V.tensor_tensor(cmp[:, 1], le, lf, ALU.is_equal).then_inc(f_dve, 1)
                    mine(F_DVE, n, "eq")
                    V.tensor_tensor(cmp[:, 1], cmp[:, 1], tie, ALU.mult).then_inc(f_dve, 1)
                    mine(F_DVE, n, "eqm")
                    V.tensor_tensor(cmp[:, 0], cmp[:, 0], cmp[:, 1], ALU.add).then_inc(f_dve, 1)
                    mine(F_DVE, n, "rank4")
                    V.tensor_reduce(rank[:, :, :], cmp[:, 0], AX.X, ALU.add).then_inc(f_dve, 1)
                    mine(F_DVE, n, "rank")
                    for a in range(2):
                        V.tensor_scalar(top[:, a, :, :], rank[:, :, :], float(a), None, ALU.is_equal).then_inc(f_dve, 1)
                    V.tensor_reduce(sc[:, 0, :], L[:, :, :], AX.X, ALU.max).then_inc(f_dve, 1)
                    mine(F_DVE, n, "top2")
                    V.tensor_tensor(lm[:, :, :], L[:, :, :], top[:, 1, :, :], ALU.mult).then_inc(f_dve, 1)
                    mine(F_DVE, n, "l2m")
                    V.tensor_reduce(sc[:, 1, :], lm[:, :, :], AX.X, ALU.add).then_inc(f_dve, 1)
                    mine(F_DVE, n, "l2")
                    V.tensor_tensor(sc[:, 2, :], sc[:, 0, :], sc[:, 1, :], ALU.subtract).then_inc(f_dve, 1)
                    dve.wait_ge(f_act, done(F_ACT, n, "w1"))
                    V.tensor_scalar(sc[:, 4, :], sc[:, 3, :], -1.0, 1.0, ALU.mult, ALU.add).then_inc(f_dve, 1)
                    mine(F_DVE, n, "w2")
                    V.tensor_tensor(lm[:, :, :], top[:, 0, :, :], sc[:, 3, :].unsqueeze(2).to_broadcast([P, NT, NE]), ALU.mult).then_inc(f_dve, 1)
                    V.tensor_tensor(comb[:, :, :], top[:, 1, :, :], sc[:, 4, :].unsqueeze(2).to_broadcast([P, NT, NE]), ALU.mult).then_inc(f_dve, 1)
                    mine(F_DVE, n, "cw2")
                    V.tensor_tensor(comb[:, :, :], comb[:, :, :], lm[:, :, :], ALU.add).then_inc(f_dve, 1)
                    mine(F_DVE, n, "comb")
                    V.tensor_copy(parts16[:, :, 0, :].bitcast(f32r), comb[:, :, :]).then_inc(f_dve, 1)
                    mine(F_DVE, n, "chi")
                    V.tensor_tensor(parts16[:, :, 1, :].bitcast(f32r), comb[:, :, :], parts16[:, :, 0, :], ALU.subtract).then_inc(f_dve, 1)
                if part == "F6":
                    dve.wait_ge(f_act, done(F_ACT, n, "c1a"))
                    V.tensor_tensor(c2, cont[0:MOE, :], R[0:MOE, 5, :], ALU.subtract).then_inc(f_dve, 1)
                if part[0] == "X":
                    e = int(part[1:])
                    if e == NE:
                        dve.wait_ge(f_act, done(F_ACT, n, "mT"))
                        V.tensor_tensor(mT[1], pf[3][0:MOE, :], R[0:MOE, 3, :], ALU.subtract).then_inc(f_dve, 1)
                    else:
                        dve.wait_ge(f_pe, done(F_PE, n, f"sp{e}"))
                        for q in (2 * e, 2 * e + 1):
                            dve.wait_ge(f_act, done(F_ACT, n, f"eh{q}"))
                            if q >= 2:
                                mine(F_DVE, n, f"ehl{q - 2}")
                            V.tensor_tensor(whole[:, q % 2, :], eh[:, q % 2, :], pf[0][:, :], ALU.mult).then_inc(f_dve, 1)
                if part[0] == "Y":
                    e = int(part[1:])
                    for q in (2 * e, 2 * e + 1):
                        dve.wait_ge(f_act, done(F_ACT, n, f"ehh{q}"))
                        if q >= 2:
                            dve.wait_ge(f_pe, done(F_PE, n, f"e2_{q - 2}"))
                        V.tensor_tensor(Rr(3 + q % 2), whole[:, q % 2, :], R[:, q % 3, :], ALU.subtract).then_inc(f_dve, 1)
                if part == "F21":
                    for i in range(NT):
                        dve.wait_ge(f_act, done(F_ACT, n, f"dec{i}"))
                        last = V.bn_stats(stat2[:, i, :], dec[:, i, :])
                    last.then_inc(f_dve, 1)
                    dve.wait_ge(f_dve, done(F_DVE, n, "stats3"))
                    carry_wait(nc.vector)
                    for i in range(NT):
                        last = V.bn_aggr(mv2[:, i, :], stat2[:, i, :])
                    last.then_inc(f_dve, 1)
                    if last_block(n):
                        dve.wait_ge(f_pool, done(F_POOL, n, "rstd3"))
                        for i in range(NT):
                            last = V.tensor_scalar(dec[:, i, :], dec[:, i, :], mv2[:, i, 0:1], rstd2[:, i:i + 1],
                                                   ALU.subtract, ALU.mult)
                        last.then_inc(end_dve, 1)
                        dve.wait_ge(end_dve, 1)
                        for a in range(2):
                            t_ = slice(2 * a, 2 * a + 2)
                            V.tensor_tensor(dec[:, t_, :], dec[:, t_, :], gscale[b][:, :].unsqueeze(1).to_broadcast([P, 2, C]),
                                            ALU.mult).then_inc(end_dve, 1)
                            dve.wait_ge(end_dve, 2 * a + 2)
                            V.tensor_tensor(res[:, t_, :], dec[:, t_, :], x1[:, t_, :], ALU.add).then_inc(end_dve, 1)

            steps(dve, emit)

        @block.gpsimd
        def _(pool):
            G = nc.gpsimd
            G.memset(Vx[:, :, :].rearrange("p a b -> p (a b)"), 0.0).then_inc(zeroed, 1)
            pool.wait_ge(zeroed, 1)
            pool.wait_ge(const_loaded, 16)

            def before(n, sem_, table, name):
                if not first(n):
                    pool.wait_ge(sem_, done(table, n - 1, name))

            def rsqrt(mv_, out_, eps, table, sem_, n, a):
                G.tensor_scalar(out_[:, :], mv_[:, :, 1], eps, None, ALU.add).then_inc(sem_, 1)
                pool.wait_ge(sem_, done(table, n, a))
                G.tensor_tensor(out_[:, :], out_[:, :], k("neghalf"), ALU.pow).then_inc(sem_, 1)

            def spread_v(n, i):
                if i:
                    pool.wait_ge(g_pe, done(G_PE, n, f"Y{i - 1}"))
                else:
                    before(n, g_pe, G_PE, "Y3")
                carry_wait(nc.gpsimd)
                G.tensor_scalar(vx_diag, kv[:, i, C:2 * C].rearrange("p (a h d) -> p a h d", a=2, h=8), 1.0, 0.0,
                                ALU.mult, ALU.add).then_inc(g_pool, 1)

            def emit(part, n, b):
                if part == "G0a":
                    pool.wait_ge(g_dve, done(G_DVE, n, "mv"))
                    carry_wait(nc.gpsimd)
                    rsqrt(mv, rstd, LN_EPS, G_POOL, g_pool, n, "var")
                if part == "G3":
                    pool.wait_ge(g_act, done(G_ACT, n, "q1"))
                    carry_wait(nc.gpsimd)
                    for h in range(2):
                        for a in range(2):
                            last = G.tensor_scalar(Qx[:, h, a, :], qs[:, h, :], k("pair")[:, a:a + 1], 0.0, ALU.mult, ALU.add)
                    last.then_inc(g_pool, 1)
                    full = [P, HEADS, CH]
                    eye = k("eye32").unsqueeze(1).to_broadcast(full)
                    pool.wait_ge(g_dve, done(G_DVE, n, "dt"))
                    before(n, g_act, G_ACT, "Ae3")
                    for i in range(NT):
                        G.tensor_tensor(BA[:, i, :, :], eye, dt[:, i, :].unsqueeze(2).to_broadcast(full), ALU.mult).then_inc(g_pool, 1)
                    before(n, g_pe, G_PE, "Y3")
                    for i in range(NT):
                        G.tensor_tensor(D[:, i, :, :], eye, gt[:, i, :].unsqueeze(2).to_broadcast(full), ALU.mult).then_inc(g_pool, 1)
                if part == "G6b":
                    before(n, f_dve, F_DVE, "t3")
                    for i in range(NT):
                        pool.wait_ge(g_dve, done(G_DVE, n, f"D{i}"))
                        full = [P, HEADS, HD]
                        G.tensor_tensor(Ks[:, i, :].rearrange("p (h d) -> p h d", h=HEADS),
                                        kv[:, i, 0:C].rearrange("p (h d) -> p h d", h=HEADS),
                                        D[:, i, :, CH - 1:CH].to_broadcast(full), ALU.mult).then_inc(g_pool, 1)
                def keep_blocks(i):
                    def keep(out_, v):
                        blk = k("headblk").unsqueeze(1).unsqueeze(3).to_broadcast([P, v.shape[1], 8, HD])
                        return G.tensor_tensor(out_.rearrange("p c (h d) -> p c h d", h=8), v.rearrange("p c (h d) -> p c h d", h=8),
                                               blk, ALU.mult)
                    lo = i * CT
                    if i == 0:
                        lo = 1
                        keep(S[:, 0, :, :], carry[b][:, :, :])
                    pool.wait_ge(g_dve, done(G_DVE, n, f"S{2 * CT * i + 2 * CT - 1}"))
                    v = S[:, lo:(i + 1) * CT, :, :].rearrange("p c h m -> p (c h) m")
                    keep(v, v).then_inc(g_pool, 1)

                def expand(i):
                    pool.wait_ge(g_dve, done(G_DVE, n, f"A{i}" if i else "A3"))
                    if i:
                        pool.wait_ge(g_pe, done(G_PE, n, f"Y{i - 1}"))
                    else:
                        pool.wait_ge(g_pool, done(G_POOL, n, "Ks3"))
                    carry_wait(nc.gpsimd)
                    for c in range(CT // 2, CT):
                        last = G.tensor_scalar(Aexp[:, :, c * CH:(c + 1) * CH], BA[:, i, :, :], k("chunk")[:, c:c + 1], 0.0,
                                               ALU.mult, ALU.add)
                    last.then_inc(g_pool, 1)

                if part == "G8":
                    spread_v(n, 0)
                    expand(0)
                if part == "G9":
                    keep_blocks(0)
                if part == "G9c":
                    keep_blocks(1)
                if part in ("GY0", "GY1", "GY2"):
                    i = int(part[2]) + 1
                    expand(i)
                    spread_v(n, i)
                    if i < 3:
                        keep_blocks(i + 1)
                if part == "F3b":
                    pool.wait_ge(f_dve, done(F_DVE, n, "mv"))
                    carry_wait(nc.gpsimd)
                    rsqrt(mv2, rstd2, LN_EPS, F_POOL, f_pool, n, "var")
                if part == "F5":
                    if first(n):
                        pool.wait_ge(setup_dve, SETUP_DVE)
                    pool.wait_ge(f_dve, done(F_DVE, n, "xn"))
                    G.tensor_tensor(x1[:, :, :], x1[:, :, :], gshift[b][:, :].unsqueeze(1).to_broadcast([P, NT, C]),
                                    ALU.add).then_inc(f_pool, 1)
                if part == "F21":
                    pool.wait_ge(f_dve, done(F_DVE, n, "mv3"))
                    carry_wait(nc.gpsimd)
                    rsqrt(mv2, rstd2, LN_EPS, F_POOL, f_pool, n, "var3")
                    if last_block(n):
                        return
                    pool.wait_ge(f_pool, done(F_POOL, n, "rstd3"))
                    carry_wait(nc.gpsimd)
                    for i in range(NT):
                        last = G.tensor_scalar(dec[:, i, :], dec[:, i, :], mv2[:, i, 0:1], rstd2[:, i:i + 1],
                                               ALU.subtract, ALU.mult)
                    last.then_inc(f_pool, 1)
                    pool.wait_ge(f_pool, done(F_POOL, n, "dn"))
                    G.tensor_tensor(dec[:, :, :], dec[:, :, :], gscale[b][:, :].unsqueeze(1).to_broadcast([P, NT, C]),
                                    ALU.mult).then_inc(f_pool, 1)
                    pool.wait_ge(f_pool, done(F_POOL, n, "g3"))
                    G.tensor_tensor(res[:, :, :], dec[:, :, :], x1[:, :, :], ALU.add).then_inc(f_pool, 1)

            steps(pool, emit)


def pack(table, offs, cols, arrays):
    out = np.zeros((P, cols), np.float32)
    for name, parts, n in table:
        out[0:parts, offs[name][0]:offs[name][0] + n] = arrays[name].reshape(parts, n)
    return out


def kernel(**inputs):
    import concourse.bacc as bacc
    from concourse.bass_utils import run_bass_kernel_spmd as run

    a = {n: np.asarray(v) for n, v in inputs.items()}
    at = {n[len("L0_attn_"):]: v for n, v in a.items() if n.startswith("L0_attn_")}
    ff = {n[len("L0_ffn_"):]: v for n, v in a.items() if n.startswith("L0_ffn_")}

    def rows(m, k=P):
        m = np.ascontiguousarray(m)
        return m.reshape(-1, k, m.shape[-1]).transpose(1, 0, 2)

    def under(m, bias):
        return np.concatenate([m, bias[..., None, :]], axis=-2)

    last_row = np.concatenate([ff["dec_b"], np.ones(P, np.float32), np.zeros(ENC - C - P, np.float32)])
    split = {"enc": rows(ff["enc_w"]), "wcp": rows(at["Wcp"].T), "dec": rows(ff["dec_w"]), "s2c": rows(ff["s2c_w"]),
             "c2s": np.concatenate([ff["c2s_w"], last_row[None, :]]), "eb2": np.concatenate([ff["e_b2"], ff["e_b2"]]),
             "ew2": ff["e_w2"].reshape(NE, 2, P, MOE).transpose(2, 1, 0, 3)}
    first_w = ff["e_w1"].transpose(1, 0, 2).reshape(MOE, NE * EH)
    attn = {"wq": rows(at["Wq"].T), "wkv": rows(np.concatenate([at["Wk"].T, at["Wv"].T], axis=1)), "wm1": rows(at["Wm1"].T)}
    weights = {
        "wm2": under(at["Wm2"].T, at["bm2"]), "wproj": rows(at["Wproj"].T), "wfc": rows(at["Wfc"].T),
        "rw1": np.pad(ff["r_w1"], ((0, 0), (0, 1))),
        "rw2": under(ff["r_w2"], ff["r_b2"]), "eb1": ff["e_b1"].reshape(NE, 2, P).transpose(2, 0, 1),
        
        "bm1": at["bm1"], "bm2": at["bm2"],
        "encb": ff["enc_b"].reshape(4, P).T, "s2cb": ff["s2c_b"], "rb1": np.append(ff["r_b1"], np.float32(1)), "c2sb": ff["c2s_b"].reshape(4, P).T,
    }
    p, f = np.arange(P)[:, None], np.arange(P)[None, :]
    consts = {
        "ident": p == f, "headblk": p // HD == np.arange(8)[None, :], "later": (p // CH == f // CH) & (p > f),
        "eye32": p % CH == np.arange(CH)[None, :], "pair": (p // HD) % 2 == np.arange(2)[None, :],
        "selP": np.arange(16)[:, None, None] == np.arange(2)[None, :, None] * 8 + (np.arange(P) // HD)[None, None, :],
        "tie": np.broadcast_to(np.arange(NE)[None, :] < np.arange(NE)[:, None], (P, NE, NE)),
        "inchunk": np.broadcast_to(np.arange(CH) != 0, (16, CH)), "neghalf": np.full((P, NT), -0.5),
        "chunk": p // CH == np.arange(CT)[None, :],
        "expert": np.arange(16)[:, None] % NE == np.arange(NE)[None, :],
    }
    consts = {n: np.asarray(v, np.float32) for n, v in consts.items()}
    setup = {
        "wmod": np.concatenate([rows(np.concatenate([a["L0_wmod"][:, i * C:(i + 1) * C] for i in part], axis=1)).reshape(P, -1)
                                for part in ((0, 1, 3, 4), (2, 5))], axis=1), "lng": np.broadcast_to(ff["ln_g"], (P, C)), "lnb": np.broadcast_to(ff["ln_b"], (P, C)),
        "cT": a["L0_c"].T.reshape(2, P, BATCH).transpose(1, 0, 2),
    }
    arrays = {"x": np.ascontiguousarray(at["x"]), "w": pack(WEIGHTS, WOFF, WCOLS, weights),
              "c": pack(CONSTS, COFF, CCOLS, consts), "s": pack(SETUP, SOFF, SCOLS, setup),
              "v": pack(SPLIT, VOFF, VCOLS, split), "a": pack(ATTN_SPLIT, AOFF, ACOLS, attn),
              "e": np.concatenate([first_w, first_w])}
    nc = bacc.Bacc("TRN2", target_bir_lowering=False, num_devices=1)
    args = [nc.dram_tensor(n, v.shape, mybir.dt.float32, kind="ExternalInput").ap() for n, v in arrays.items()]
    out = nc.dram_tensor("out", (BATCH, SEQ, C), mybir.dt.float32, kind="ExternalOutput").ap()
    build(nc, *args, out)
    r = run(nc, [arrays], core_ids=[0])
    return r.results[0]["out"]
```
